# Optimizing a Trainium2 kernel written in Bass

```python
import numpy as np
import jax
import jax.numpy as jnp

def _softmax(x, axis=-1):
    return jax.nn.softmax(x, axis=axis)

def _gelu(x):
    return jax.nn.gelu(x, approximate=True)

def _silu(x):
    return jax.nn.silu(x)

def _sigmoid(x):
    return jax.nn.sigmoid(x)

def _layernorm(x, axis=-1, eps=1e-05):
    m = jnp.mean(x, axis=axis, keepdims=True)
    v = jnp.var(x, axis=axis, keepdims=True)
    return (x - m) / jnp.sqrt(v + eps)

def _scatter_add(tgt, idx, src, axis=0):
    return tgt.at[idx].add(src)

def _segment_sum(src, seg, n):
    return jax.ops.segment_sum(src, seg, n)
kernel_name = 'mk_xattn_ffn_d4_seqx_r8_b44866'

def setup_inputs(seed: int=0):
    np.random.seed(seed)
    _w = jnp.asarray

    def _rec_inputs():
        import jax
        import jax.numpy as jnp
        _rk = jax.random.key(seed)
        x = -0.0002928 + 1 * jax.random.normal(jax.random.fold_in(_rk, 1), (4, 512, 128), jnp.float32)
        _lenS = 512 - jax.random.randint(jax.random.fold_in(_rk, 7), (4,), 0, max(1, 512 // 4) + 1, jnp.int32)
        _lenS2 = 77 - jax.random.randint(jax.random.fold_in(_rk, 8), (4,), 0, max(1, 77 // 4) + 1, jnp.int32)
        _ctx_1024P = jax.random.normal(jax.random.fold_in(_rk, 11), (4, 16, 128), jnp.float32)
        _ctx_1024c = jax.random.dirichlet(jax.random.fold_in(_rk, 511), 0.3 * jnp.ones((16,), jnp.float32), (4, 77))
        _ctx_1024t = jnp.einsum('bsk,bkd->bsd', _ctx_1024c, _ctx_1024P)
        _ctx_1024t = _ctx_1024t * jax.lax.rsqrt(jnp.mean(jnp.square(_ctx_1024t)) + 1e-12) * 0.953939
        ctx_1024 = 0.000227908 + 0.99994 * (_ctx_1024t + 0.3 * jax.random.normal(jax.random.fold_in(_rk, 611), (4, 77, 128), jnp.float32))
        _validS = jnp.arange(512)[None, :] < _lenS[:, None]
        _validS2 = jnp.arange(77)[None, :] < _lenS2[:, None]
        _causal = jnp.tril(jnp.ones((512, 512), dtype=bool))
        mask_SxS_bc0 = jnp.logical_not(jnp.broadcast_to(_causal[:, :], (512, 512)))
        mask_BxS2_if0 = jnp.where(jnp.ones((4, 77), dtype=bool), 0, 1).astype(jnp.int32)
        return (x, ctx_1024, mask_SxS_bc0, mask_BxS2_if0)
    x, ctx_1024, mask_SxS_bc0, mask_BxS2_if0 = _rec_inputs()

    def _L0_xattn_setup():
        import jax, jax.numpy as jnp
        import numpy as np
        from jax import lax
        H = 16
        K1, K2 = (3, 3)
        LN_EPS = 1e-05

        def _ln(x, g, b):
            m = jnp.mean(x, axis=-1, keepdims=True)
            v = jnp.mean(jnp.square(x - m), axis=-1, keepdims=True)
            return (x - m) * lax.rsqrt(v + LN_EPS) * g + b

        def _gelu(x):
            return jax.nn.gelu(x, approximate=False)
        key = jax.random.key(seed)
        B, T, D, Th = (4, 128, 128, 32)
        C = 2 * D
        ks = jax.random.split(key, 16)

        def w(k, shape):
            fan_in = shape[0]
            return (jax.random.normal(k, shape, jnp.float32) / np.sqrt(fan_in)).astype(jnp.float32)
        inp = {'x': jax.random.normal(ks[0], (B, T, D), jnp.float32), 'historical_data': jax.random.normal(ks[1], (B, Th, D), jnp.float32), 'Wq': w(ks[2], (D, D)), 'Wk': w(ks[3], (D, D)), 'Wv': w(ks[4], (D, D)), 'hist_W': w(ks[5], (D, C)), 'hist_b': jnp.zeros((C,), jnp.float32), 'hist_ln_g': jnp.ones((C,), jnp.float32), 'hist_ln_b': jnp.zeros((C,), jnp.float32), 'ctx_W1': w(ks[6], (C, C // 4)), 'ctx_b1': jnp.zeros((C // 4,), jnp.float32), 'ctx_W2': w(ks[7], (C // 4, 1)), 'ctx_b2': jnp.zeros((1,), jnp.float32), 'kg_W1': w(ks[8], (C, D)), 'kg_b1': jnp.zeros((D,), jnp.float32), 'kg_ln_g': jnp.ones((D,), jnp.float32), 'kg_ln_b': jnp.zeros((D,), jnp.float32), 'kg_W2': w(ks[9], (D, H * K1 * K2)), 'kg_b2': jnp.zeros((H * K1 * K2,), jnp.float32), 'proj_W': w(ks[10], (D, D)), 'proj_b': jnp.zeros((D,), jnp.float32), 'causal_mask': jnp.triu(jnp.ones((T, T), bool), k=1)}
        return inp
    _L0_xattn_all = _L0_xattn_setup()
    _L0_xattn_in = {k: v for k, v in _L0_xattn_all.items() if k in ('Wq', 'Wk', 'Wv', 'hist_W', 'hist_b', 'hist_ln_g', 'hist_ln_b', 'ctx_W1', 'ctx_b1', 'ctx_W2', 'ctx_b2', 'kg_W1', 'kg_b1', 'kg_ln_g', 'kg_ln_b', 'kg_W2', 'kg_b2', 'proj_W', 'proj_b')}
    del _L0_xattn_all

    def _L0_ffn_setup():
        import jax, jax.numpy as jnp
        import numpy as np
        import math
        N_EMBD = 128
        HIDDEN = 4 * N_EMBD
        N_EXPERTS = 8
        TOP_K = 2
        B, T = (4, 256)

        def new_gelu(x):
            c = math.sqrt(2.0 / math.pi)
            return 0.5 * x * (1.0 + jnp.tanh(c * (x + 0.044715 * x * x * x)))

        def _moe_forward(x, Wfc_s, bfc_s, Wproj_s, bproj_s, Wr, Wfc, bfc, Wproj, bproj):
            Bb, Tt, C = x.shape
            xf = x.reshape(Bb * Tt, C)
            N = Bb * Tt
            shared = new_gelu(xf @ Wfc_s + bfc_s) @ Wproj_s + bproj_s
            logits = xf @ Wr
            probs = jax.nn.softmax(logits, axis=-1)
            topk_p, topk_i = jax.lax.top_k(probs, TOP_K)
            topk_p = topk_p / jnp.sum(topk_p, axis=-1, keepdims=True)
            gate = jnp.zeros((N, N_EXPERTS), dtype=xf.dtype)
            gate = gate.at[jnp.arange(N)[:, None], topk_i].add(topk_p)
            routed = jnp.zeros_like(xf)
            for e in range(N_EXPERTS):
                h = new_gelu(xf @ Wfc[e] + bfc[e]) @ Wproj[e] + bproj[e]
                routed = routed + h * gate[:, e:e + 1]
            return (shared + routed).reshape(Bb, Tt, C)
        key = jax.random.key(seed)
        ks = jax.random.split(key, 10)
        s = 0.02
        return {'x': jax.random.normal(ks[0], (B, T, N_EMBD), dtype=jnp.float32), 'Wfc_s': jax.random.normal(ks[1], (N_EMBD, HIDDEN), dtype=jnp.float32) * s, 'bfc_s': jnp.zeros((HIDDEN,), dtype=jnp.float32), 'Wproj_s': jax.random.normal(ks[2], (HIDDEN, N_EMBD), dtype=jnp.float32) * s, 'bproj_s': jnp.zeros((N_EMBD,), dtype=jnp.float32), 'Wr': jax.random.normal(ks[3], (N_EMBD, N_EXPERTS), dtype=jnp.float32) * s, 'Wfc': jax.random.normal(ks[4], (N_EXPERTS, N_EMBD, HIDDEN), dtype=jnp.float32) * s, 'bfc': jnp.zeros((N_EXPERTS, HIDDEN), dtype=jnp.float32), 'Wproj': jax.random.normal(ks[5], (N_EXPERTS, HIDDEN, N_EMBD), dtype=jnp.float32) * s, 'bproj': jnp.zeros((N_EXPERTS, N_EMBD), dtype=jnp.float32)}
    _L0_ffn_all = _L0_ffn_setup()
    _L0_ffn_in = {k: v for k, v in _L0_ffn_all.items() if k in ('Wfc_s', 'bfc_s', 'Wproj_s', 'bproj_s', 'Wr', 'Wfc', 'bfc', 'Wproj', 'bproj')}
    del _L0_ffn_all

    def _L1_xattn_setup():
        import jax, jax.numpy as jnp
        import numpy as np
        import math
        B, M, D, H, NK = (4, 256, 128, 16, 5)
        HD = D // H

        def _gather_pad0(x, idx):
            Bx, Hx, W, hd = x.shape
            valid = (idx >= 0) & (idx < W)
            idxc = jnp.clip(idx, 0, W - 1).reshape(Bx, Hx, -1)
            g = jnp.take_along_axis(x, idxc[..., None], axis=2)
            g = g.reshape(idx.shape + (hd,))
            return g * valid[..., None].astype(x.dtype)
        key = jax.random.key(seed)
        ks = jax.random.split(key, 9)
        w = lambda k, shape: jax.random.normal(k, shape, jnp.float32) * 0.02
        return {'k': jax.random.normal(ks[0], (B, M, D), jnp.float32), 'v': jax.random.normal(ks[1], (B, M, D), jnp.float32), 'q': jax.random.normal(ks[2], (B, M, D), jnp.float32), 'mask': jnp.zeros((B, M), jnp.int32), 'Wk': w(ks[3], (D, D)), 'bk': jnp.zeros((D,), jnp.float32), 'Wv': w(ks[4], (D, D)), 'bv': jnp.zeros((D,), jnp.float32), 'Wq': w(ks[5], (D, D)), 'bq': jnp.zeros((D,), jnp.float32), 'Woff': w(ks[6], (H * NK, D)), 'boff': jnp.zeros((H * NK,), jnp.float32), 'Wo': w(ks[7], (D, D)), 'bo': jnp.zeros((D,), jnp.float32)}
    _L1_xattn_all = _L1_xattn_setup()
    _L1_xattn_in = {k: v for k, v in _L1_xattn_all.items() if k in ('Wk', 'bk', 'Wv', 'bv', 'Wq', 'bq', 'Woff', 'boff', 'Wo', 'bo')}
    del _L1_xattn_all

    def _L1_ffn_setup():
        import jax, jax.numpy as jnp
        import numpy as np
        TOP_K = 2
        NUM_EXPERTS = 8
        DIM = 128
        HIDDEN = 352
        BS, SLEN = (2, 128)

        def _grouped_ffn(x, w1, w2, w3, counts):
            num_experts = w1.shape[0]
            ends = jnp.cumsum(counts)
            starts = ends - counts
            t = jnp.arange(x.shape[0])
            out = jnp.zeros((x.shape[0], w2.shape[-1]), x.dtype)
            for e in range(num_experts):
                m = ((t >= starts[e]) & (t < ends[e])).astype(x.dtype)[:, None]
                xe = x * m
                h = jax.nn.silu(xe @ w1[e]) * (xe @ w3[e])
                out = out + h @ w2[e] * m
            return out
        key = jax.random.key(seed)
        k = jax.random.split(key, 5)
        std = 0.02
        return {'x': jax.random.normal(k[0], (BS, SLEN, DIM), jnp.float32), 'gate_w': jax.random.normal(k[1], (NUM_EXPERTS, DIM), jnp.float32) * std, 'expert_bias': jnp.zeros((NUM_EXPERTS,), jnp.float32), 'w1': jax.random.normal(k[2], (NUM_EXPERTS, DIM, HIDDEN), jnp.float32) * std, 'w2': jax.random.normal(k[3], (NUM_EXPERTS, HIDDEN, DIM), jnp.float32) * std, 'w3': jax.random.normal(k[4], (NUM_EXPERTS, DIM, HIDDEN), jnp.float32) * std}
    _L1_ffn_all = _L1_ffn_setup()
    _L1_ffn_in = {k: v for k, v in _L1_ffn_all.items() if k in ('gate_w', 'expert_bias', 'w1', 'w2', 'w3')}
    del _L1_ffn_all

    def _L2_xattn_setup():
        import jax, jax.numpy as jnp
        import numpy as np
        NUM_HEADS = 16
        key = jax.random.key(seed)
        ks = jax.random.split(key, 6)
        B, N, M, D = (4, 256, 256, 128)
        s = 1.0 / np.sqrt(D)
        return {'inputs': jax.random.normal(ks[0], (B, N, D), dtype=jnp.float32), 'encoderOutputs': jax.random.normal(ks[1], (B, M, D), dtype=jnp.float32), 'wq': jax.random.normal(ks[2], (D, D), dtype=jnp.float32) * s, 'wk': jax.random.normal(ks[3], (D, D), dtype=jnp.float32) * s, 'wv': jax.random.normal(ks[4], (D, D), dtype=jnp.float32) * s, 'wo': jax.random.normal(ks[5], (D, D), dtype=jnp.float32) * s}
    _L2_xattn_all = _L2_xattn_setup()
    _L2_xattn_in = {k: v for k, v in _L2_xattn_all.items() if k in ('wq', 'wk', 'wv', 'wo')}
    del _L2_xattn_all

    def _L2_ffn_setup():
        import jax, jax.numpy as jnp
        import numpy as np
        B, S, D = (4, 256, 128)
        EXP = 4
        H = EXP * D
        E = 8
        TOP_K = 2
        key = jax.random.key(seed)
        ks = jax.random.split(key, 8)
        scale1 = 1.0 / np.sqrt(D)
        scale2 = 1.0 / np.sqrt(H)
        x = jax.random.normal(ks[0], (B, S, D), dtype=jnp.float32)
        W1 = jax.random.uniform(ks[1], (E, D, H), jnp.float32, -scale1, scale1)
        b1 = jax.random.uniform(ks[2], (E, H), jnp.float32, -scale1, scale1)
        W2 = jax.random.uniform(ks[3], (E, H, D), jnp.float32, -scale2, scale2)
        b2 = jax.random.uniform(ks[4], (E, D), jnp.float32, -scale2, scale2)
        Wr = jax.random.uniform(ks[5], (D, E), jnp.float32, -scale1, scale1)
        br = jax.random.uniform(ks[6], (E,), jnp.float32, -scale1, scale1)
        return {'input_emb': x, 'W1': W1, 'b1': b1, 'W2': W2, 'b2': b2, 'Wr': Wr, 'br': br}
    _L2_ffn_all = _L2_ffn_setup()
    _L2_ffn_in = {k: v for k, v in _L2_ffn_all.items() if k in ('W1', 'b1', 'W2', 'b2', 'Wr', 'br')}
    del _L2_ffn_all

    def _L3_xattn_setup():
        import jax, jax.numpy as jnp
        import numpy as np
        DIM = 128
        NUM_HEADS = 16
        HEAD_DIM = DIM // NUM_HEADS
        SCALE = HEAD_DIM ** (-0.5)
        key = jax.random.key(seed)
        k1, k2, k3, k4 = jax.random.split(key, 4)
        B, N_q, N_kv = (4, 128, 512)
        q = jax.random.normal(k1, (B, N_q, DIM), dtype=jnp.float32)
        kv = jax.random.normal(k2, (B, N_kv, DIM), dtype=jnp.float32)
        W_qkv = jax.random.normal(k3, (DIM, 3 * DIM), dtype=jnp.float32) * DIM ** (-0.5)
        W_proj = jax.random.normal(k4, (DIM, DIM), dtype=jnp.float32) * DIM ** (-0.5)
        b_proj = jnp.zeros((DIM,), dtype=jnp.float32)
        return {'q': q, 'kv': kv, 'W_qkv': W_qkv, 'W_proj': W_proj, 'b_proj': b_proj}
    _L3_xattn_all = _L3_xattn_setup()
    _L3_xattn_in = {k: v for k, v in _L3_xattn_all.items() if k in ('W_qkv', 'W_proj', 'b_proj')}
    del _L3_xattn_all

    def _L3_ffn_setup():
        import jax, jax.numpy as jnp
        import numpy as np
        DIM = 128
        HEADS = 8
        NUM_EXPERTS = 8192
        NUM_KEYS = 32
        DIM_KEY = 64
        PK_TOPK = 16
        FINAL_TOPK = 1
        BATCH, SEQ = (4, 256)
        key = jax.random.key(seed)
        k1, k2, k3, k4, k5 = jax.random.split(key, 5)
        x = jax.random.normal(k1, (BATCH, SEQ, DIM), jnp.float32)
        w_q = jax.random.normal(k2, (DIM, 2 * HEADS * DIM_KEY), jnp.float32) * 0.02
        keys = jax.random.normal(k3, (HEADS, NUM_KEYS, 2, DIM_KEY), jnp.float32) * 0.02
        w_down = jax.random.normal(k4, (NUM_EXPERTS, DIM), jnp.float32) * 0.02
        w_up = jax.random.normal(k5, (NUM_EXPERTS, DIM), jnp.float32) * 0.02
        return {'x': x, 'w_q': w_q, 'keys': keys, 'w_down': w_down, 'w_up': w_up}
    _L3_ffn_all = _L3_ffn_setup()
    _L3_ffn_in = {k: v for k, v in _L3_ffn_all.items() if k in ('w_q', 'keys', 'w_down', 'w_up')}
    del _L3_ffn_all
    return {'x': x, 'ctx_1024': ctx_1024, 'mask_SxS_bc0': mask_SxS_bc0, 'mask_BxS2_if0': mask_BxS2_if0, 'L0_xattn_Wq': _L0_xattn_in['Wq'], 'L0_xattn_Wk': _L0_xattn_in['Wk'], 'L0_xattn_Wv': _L0_xattn_in['Wv'], 'L0_xattn_hist_W': _L0_xattn_in['hist_W'], 'L0_xattn_hist_b': _L0_xattn_in['hist_b'], 'L0_xattn_hist_ln_g': _L0_xattn_in['hist_ln_g'], 'L0_xattn_hist_ln_b': _L0_xattn_in['hist_ln_b'], 'L0_xattn_ctx_W1': _L0_xattn_in['ctx_W1'], 'L0_xattn_ctx_b1': _L0_xattn_in['ctx_b1'], 'L0_xattn_ctx_W2': _L0_xattn_in['ctx_W2'], 'L0_xattn_ctx_b2': _L0_xattn_in['ctx_b2'], 'L0_xattn_kg_W1': _L0_xattn_in['kg_W1'], 'L0_xattn_kg_b1': _L0_xattn_in['kg_b1'], 'L0_xattn_kg_ln_g': _L0_xattn_in['kg_ln_g'], 'L0_xattn_kg_ln_b': _L0_xattn_in['kg_ln_b'], 'L0_xattn_kg_W2': _L0_xattn_in['kg_W2'], 'L0_xattn_kg_b2': _L0_xattn_in['kg_b2'], 'L0_xattn_proj_W': _L0_xattn_in['proj_W'], 'L0_xattn_proj_b': _L0_xattn_in['proj_b'], 'L0_ffn_Wfc_s': _L0_ffn_in['Wfc_s'], 'L0_ffn_bfc_s': _L0_ffn_in['bfc_s'], 'L0_ffn_Wproj_s': _L0_ffn_in['Wproj_s'], 'L0_ffn_bproj_s': _L0_ffn_in['bproj_s'], 'L0_ffn_Wr': _L0_ffn_in['Wr'], 'L0_ffn_Wfc': _L0_ffn_in['Wfc'], 'L0_ffn_bfc': _L0_ffn_in['bfc'], 'L0_ffn_Wproj': _L0_ffn_in['Wproj'], 'L0_ffn_bproj': _L0_ffn_in['bproj'], 'L1_xattn_Wk': _L1_xattn_in['Wk'], 'L1_xattn_bk': _L1_xattn_in['bk'], 'L1_xattn_Wv': _L1_xattn_in['Wv'], 'L1_xattn_bv': _L1_xattn_in['bv'], 'L1_xattn_Wq': _L1_xattn_in['Wq'], 'L1_xattn_bq': _L1_xattn_in['bq'], 'L1_xattn_Woff': _L1_xattn_in['Woff'], 'L1_xattn_boff': _L1_xattn_in['boff'], 'L1_xattn_Wo': _L1_xattn_in['Wo'], 'L1_xattn_bo': _L1_xattn_in['bo'], 'L1_ffn_gate_w': _L1_ffn_in['gate_w'], 'L1_ffn_expert_bias': _L1_ffn_in['expert_bias'], 'L1_ffn_w1': _L1_ffn_in['w1'], 'L1_ffn_w2': _L1_ffn_in['w2'], 'L1_ffn_w3': _L1_ffn_in['w3'], 'L2_xattn_wq': _L2_xattn_in['wq'], 'L2_xattn_wk': _L2_xattn_in['wk'], 'L2_xattn_wv': _L2_xattn_in['wv'], 'L2_xattn_wo': _L2_xattn_in['wo'], 'L2_ffn_W1': _L2_ffn_in['W1'], 'L2_ffn_b1': _L2_ffn_in['b1'], 'L2_ffn_W2': _L2_ffn_in['W2'], 'L2_ffn_b2': _L2_ffn_in['b2'], 'L2_ffn_Wr': _L2_ffn_in['Wr'], 'L2_ffn_br': _L2_ffn_in['br'], 'L3_xattn_W_qkv': _L3_xattn_in['W_qkv'], 'L3_xattn_W_proj': _L3_xattn_in['W_proj'], 'L3_xattn_b_proj': _L3_xattn_in['b_proj'], 'L3_ffn_w_q': _L3_ffn_in['w_q'], 'L3_ffn_keys': _L3_ffn_in['keys'], 'L3_ffn_w_down': _L3_ffn_in['w_down'], 'L3_ffn_w_up': _L3_ffn_in['w_up']}

def reference(x, ctx_1024, mask_SxS_bc0, mask_BxS2_if0, L0_xattn_Wq, L0_xattn_Wk, L0_xattn_Wv, L0_xattn_hist_W, L0_xattn_hist_b, L0_xattn_hist_ln_g, L0_xattn_hist_ln_b, L0_xattn_ctx_W1, L0_xattn_ctx_b1, L0_xattn_ctx_W2, L0_xattn_ctx_b2, L0_xattn_kg_W1, L0_xattn_kg_b1, L0_xattn_kg_ln_g, L0_xattn_kg_ln_b, L0_xattn_kg_W2, L0_xattn_kg_b2, L0_xattn_proj_W, L0_xattn_proj_b, L0_ffn_Wfc_s, L0_ffn_bfc_s, L0_ffn_Wproj_s, L0_ffn_bproj_s, L0_ffn_Wr, L0_ffn_Wfc, L0_ffn_bfc, L0_ffn_Wproj, L0_ffn_bproj, L1_xattn_Wk, L1_xattn_bk, L1_xattn_Wv, L1_xattn_bv, L1_xattn_Wq, L1_xattn_bq, L1_xattn_Woff, L1_xattn_boff, L1_xattn_Wo, L1_xattn_bo, L1_ffn_gate_w, L1_ffn_expert_bias, L1_ffn_w1, L1_ffn_w2, L1_ffn_w3, L2_xattn_wq, L2_xattn_wk, L2_xattn_wv, L2_xattn_wo, L2_ffn_W1, L2_ffn_b1, L2_ffn_W2, L2_ffn_b2, L2_ffn_Wr, L2_ffn_br, L3_xattn_W_qkv, L3_xattn_W_proj, L3_xattn_b_proj, L3_ffn_w_q, L3_ffn_keys, L3_ffn_w_down, L3_ffn_w_up):
    import jax
    import jax.numpy as jnp

    def _L0_xattn_ref(x, historical_data, Wq, Wk, Wv, hist_W, hist_b, hist_ln_g, hist_ln_b, ctx_W1, ctx_b1, ctx_W2, ctx_b2, kg_W1, kg_b1, kg_ln_g, kg_ln_b, kg_W2, kg_b2, proj_W, proj_b, causal_mask):
        import jax, jax.numpy as jnp
        import numpy as np
        from jax import lax
        H = 16
        K1, K2 = (3, 3)
        LN_EPS = 1e-05

        def _ln(x, g, b):
            m = jnp.mean(x, axis=-1, keepdims=True)
            v = jnp.mean(jnp.square(x - m), axis=-1, keepdims=True)
            return (x - m) * lax.rsqrt(v + LN_EPS) * g + b

        def _gelu(x):
            return jax.nn.gelu(x, approximate=False)
        B, T, D = x.shape
        hd = D // H
        scale = hd ** (-0.5)
        q = (x @ Wq).reshape(B, T, H, hd).transpose(0, 2, 1, 3)
        k = (x @ Wk).reshape(B, T, H, hd).transpose(0, 2, 1, 3)
        v = (x @ Wv).reshape(B, T, H, hd).transpose(0, 2, 1, 3)
        attn = jnp.einsum('bhqd,bhkd->bhqk', q, k) * scale
        eh = _gelu(_ln(historical_data @ hist_W + hist_b, hist_ln_g, hist_ln_b))
        aw = _gelu(eh @ ctx_W1 + ctx_b1) @ ctx_W2 + ctx_b2
        aw = jax.nn.softmax(aw, axis=1)
        cc = jnp.sum(eh * aw, axis=1)
        kp = _gelu(_ln(cc @ kg_W1 + kg_b1, kg_ln_g, kg_ln_b)) @ kg_W2 + kg_b2
        kernels = jax.nn.softmax(kp.reshape(B, H, K1 * K2), axis=-1)
        kernels = kernels.reshape(B * H, 1, K1, K2)
        mask = causal_mask[None, None]
        attn0 = jnp.where(mask, 0.0, attn).reshape(1, B * H, T, T)
        attn = lax.conv_general_dilated(attn0, kernels, window_strides=(1, 1), padding=((K1 // 2, K1 // 2), (K2 // 2, K2 // 2)), feature_group_count=B * H, dimension_numbers=('NCHW', 'OIHW', 'NCHW')).reshape(B, H, T, T)
        attn = jnp.where(mask, -jnp.inf, attn)
        p = jax.nn.softmax(attn, axis=-1)
        out = jnp.einsum('bhqk,bhkd->bhqd', p, v)
        out = out.transpose(0, 2, 1, 3).reshape(B, T, D)
        return out @ proj_W + proj_b

    def _L0_ffn_ref(x, Wfc_s, bfc_s, Wproj_s, bproj_s, Wr, Wfc, bfc, Wproj, bproj):
        import jax, jax.numpy as jnp
        import numpy as np
        import math
        N_EMBD = 128
        HIDDEN = 4 * N_EMBD
        N_EXPERTS = 8
        TOP_K = 2
        B, T = (4, 256)

        def new_gelu(x):
            c = math.sqrt(2.0 / math.pi)
            return 0.5 * x * (1.0 + jnp.tanh(c * (x + 0.044715 * x * x * x)))

        def _moe_forward(x, Wfc_s, bfc_s, Wproj_s, bproj_s, Wr, Wfc, bfc, Wproj, bproj):
            Bb, Tt, C = x.shape
            xf = x.reshape(Bb * Tt, C)
            N = Bb * Tt
            shared = new_gelu(xf @ Wfc_s + bfc_s) @ Wproj_s + bproj_s
            logits = xf @ Wr
            probs = jax.nn.softmax(logits, axis=-1)
            topk_p, topk_i = jax.lax.top_k(probs, TOP_K)
            topk_p = topk_p / jnp.sum(topk_p, axis=-1, keepdims=True)
            gate = jnp.zeros((N, N_EXPERTS), dtype=xf.dtype)
            gate = gate.at[jnp.arange(N)[:, None], topk_i].add(topk_p)
            routed = jnp.zeros_like(xf)
            for e in range(N_EXPERTS):
                h = new_gelu(xf @ Wfc[e] + bfc[e]) @ Wproj[e] + bproj[e]
                routed = routed + h * gate[:, e:e + 1]
            return (shared + routed).reshape(Bb, Tt, C)
        return _moe_forward(x, Wfc_s, bfc_s, Wproj_s, bproj_s, Wr, Wfc, bfc, Wproj, bproj)

    def _L1_xattn_ref(k, v, q, mask, Wk, bk, Wv, bv, Wq, bq, Woff, boff, Wo, bo):
        import jax, jax.numpy as jnp
        import numpy as np
        import math
        B, M, D, H, NK = (4, 256, 128, 16, 5)
        HD = D // H

        def _gather_pad0(x, idx):
            Bx, Hx, W, hd = x.shape
            valid = (idx >= 0) & (idx < W)
            idxc = jnp.clip(idx, 0, W - 1).reshape(Bx, Hx, -1)
            g = jnp.take_along_axis(x, idxc[..., None], axis=2)
            g = g.reshape(idx.shape + (hd,))
            return g * valid[..., None].astype(x.dtype)
        Bq, Q, _ = q.shape
        key_len = k.shape[1]
        K = jnp.einsum('bmd,ed->bme', k, Wk) + bk
        V = jnp.einsum('bmd,ed->bme', v, Wv) + bv
        Qp = jnp.einsum('bqd,ed->bqe', q, Wq) + bq
        off = jnp.einsum('bqd,ed->bqe', Qp, Woff) + boff
        off = off.reshape(Bq, Q, H, NK).transpose(0, 2, 1, 3)
        Kh = K.reshape(Bq, key_len, H, HD).transpose(0, 2, 1, 3)
        Vh = V.reshape(Bq, key_len, H, HD).transpose(0, 2, 1, 3)
        Qh = Qp.reshape(Bq, Q, H, HD).transpose(0, 2, 1, 3)
        loc = jnp.arange(Q, dtype=jnp.float32)[:, None]
        left = -NK // 2
        ref = jnp.arange(left, NK + left, dtype=jnp.float32)
        sign_lens = (1 - mask).sum(-1).astype(jnp.float32) - 1.0
        loc_x = jnp.mod(ref + off + loc, sign_lens[:, None, None, None])
        xg = loc_x / (key_len - 1) * 2.0 - 1.0
        ix = ((xg + 1.0) * key_len - 1.0) / 2.0
        x0 = jnp.floor(ix)
        dx = ix - x0
        i0 = x0.astype(jnp.int32)
        i1 = i0 + 1
        w0 = (1.0 - dx)[..., None]
        w1 = dx[..., None]
        sk = 0.5 * (w0 * _gather_pad0(Kh, i0) + w1 * _gather_pad0(Kh, i1))
        sv = 0.5 * (w0 * _gather_pad0(Vh, i0) + w1 * _gather_pad0(Vh, i1))
        scores = jnp.einsum('bhqd,bhqkd->bhqk', Qh / math.sqrt(HD), sk)
        attn = jax.nn.softmax(scores, axis=-1)
        ctx = jnp.einsum('bhqk,bhqkd->bhqd', attn, sv)
        ctx = ctx.transpose(0, 2, 1, 3).reshape(Bq, Q, H * HD)
        return jnp.einsum('bqd,ed->bqe', ctx, Wo) + bo

    def _L1_ffn_ref(x, gate_w, expert_bias, w1, w2, w3):
        import jax, jax.numpy as jnp
        import numpy as np
        TOP_K = 2
        NUM_EXPERTS = 8
        DIM = 128
        HIDDEN = 352
        BS, SLEN = (2, 128)

        def _grouped_ffn(x, w1, w2, w3, counts):
            num_experts = w1.shape[0]
            ends = jnp.cumsum(counts)
            starts = ends - counts
            t = jnp.arange(x.shape[0])
            out = jnp.zeros((x.shape[0], w2.shape[-1]), x.dtype)
            for e in range(num_experts):
                m = ((t >= starts[e]) & (t < ends[e])).astype(x.dtype)[:, None]
                xe = x * m
                h = jax.nn.silu(xe @ w1[e]) * (xe @ w3[e])
                out = out + h @ w2[e] * m
            return out
        bs, slen, dim = x.shape
        num_experts = gate_w.shape[0]
        xf = x.reshape(bs * slen, dim)
        scores = jax.nn.softmax((xf @ gate_w.T).astype(jnp.float32), axis=-1)
        _, sel = jax.lax.top_k(scores + expert_bias, TOP_K)
        top_scores = jnp.take_along_axis(scores, sel, axis=1).reshape(-1)
        sel_flat = sel.reshape(-1)
        counts = jnp.zeros((num_experts,), jnp.int32).at[sel_flat].add(1)
        order = jnp.argsort(sel_flat, stable=True)
        top_scores_sorted = top_scores[order]
        token_idx = order // TOP_K
        routed = xf[token_idx] * top_scores_sorted[:, None].astype(xf.dtype)
        routed_out = _grouped_ffn(routed, w1, w2, w3, counts)
        out = jnp.zeros_like(xf).at[token_idx].add(routed_out)
        return out.reshape(bs, slen, dim)

    def _L2_xattn_ref(inputs, encoderOutputs, wq, wk, wv, wo):
        import jax, jax.numpy as jnp
        import numpy as np
        NUM_HEADS = 16
        B, N, D = inputs.shape
        M = encoderOutputs.shape[1]
        H = NUM_HEADS
        hd = D // H
        q = (inputs @ wq.T).reshape(B, N, H, hd).transpose(0, 2, 1, 3)
        k = (encoderOutputs @ wk.T).reshape(B, M, H, hd).transpose(0, 2, 1, 3)
        v = (encoderOutputs @ wv.T).reshape(B, M, H, hd).transpose(0, 2, 1, 3)
        scores = jnp.einsum('bhnd,bhmd->bhnm', q, k) / jnp.sqrt(jnp.float32(hd))
        attn = jax.nn.softmax(scores, axis=-1)
        ctx = jnp.einsum('bhnm,bhmd->bhnd', attn, v)
        ctx = ctx.transpose(0, 2, 1, 3).reshape(B, N, D)
        return ctx @ wo.T

    def _L2_ffn_ref(input_emb, W1, b1, W2, b2, Wr, br):
        import jax, jax.numpy as jnp
        import numpy as np
        B, S, D = (4, 256, 128)
        EXP = 4
        H = EXP * D
        E = 8
        TOP_K = 2
        logits = jnp.einsum('bsd,de->bse', input_emb, Wr) + br
        route_w = jax.nn.softmax(logits, axis=-1)
        _, topk_idx = jax.lax.top_k(route_w, TOP_K)
        mask = jax.nn.one_hot(topk_idx, E, dtype=route_w.dtype).sum(-2)
        routed = route_w * mask
        routed = routed / routed.sum(axis=-1, keepdims=True)
        h = jax.nn.relu(jnp.einsum('bsd,edh->ebsh', input_emb, W1) + b1[:, None, None, :])
        expert_out = jnp.einsum('ebsh,ehd->ebsd', h, W2) + b2[:, None, None, :]
        return jnp.einsum('bse,ebsd->bsd', routed, expert_out)

    def _L3_xattn_ref(q, kv, W_qkv, W_proj, b_proj):
        import jax, jax.numpy as jnp
        import numpy as np
        DIM = 128
        NUM_HEADS = 16
        HEAD_DIM = DIM // NUM_HEADS
        SCALE = HEAD_DIM ** (-0.5)
        B, N_q, C = q.shape
        N_kv = kv.shape[1]
        H, hd = (NUM_HEADS, HEAD_DIM)
        kv_qkv = (kv @ W_qkv).reshape(B, N_kv, 3, H, hd)
        k = jnp.transpose(kv_qkv[:, :, 1], (0, 2, 1, 3))
        v = jnp.transpose(kv_qkv[:, :, 2], (0, 2, 1, 3))
        q_qkv = (q @ W_qkv).reshape(B, N_q, 3, H, hd)
        qh = jnp.transpose(q_qkv[:, :, 0], (0, 2, 1, 3))
        attn = jnp.einsum('bhqd,bhkd->bhqk', qh, k) * SCALE
        attn = jax.nn.softmax(attn, axis=-1)
        x = jnp.einsum('bhqk,bhkd->bhqd', attn, v)
        x = jnp.transpose(x, (0, 2, 1, 3)).reshape(B, N_q, C)
        return x @ W_proj + b_proj

    def _L3_ffn_ref(x, w_q, keys, w_down, w_up):
        import jax, jax.numpy as jnp
        import numpy as np
        DIM = 128
        HEADS = 8
        NUM_EXPERTS = 8192
        NUM_KEYS = 32
        DIM_KEY = 64
        PK_TOPK = 16
        FINAL_TOPK = 1
        BATCH, SEQ = (4, 256)
        b, n, d = x.shape
        q = (x @ w_q).reshape(b, n, 2, HEADS, DIM_KEY).transpose(2, 0, 1, 3, 4)
        sim = jnp.einsum('pbnhd,hkpd->pbnhk', q, keys)
        vals, idx = jax.lax.top_k(sim, PK_TOPK)
        sx, sy = (vals[0], vals[1])
        ix, iy = (idx[0], idx[1])
        all_scores = (sx[..., :, None] + sy[..., None, :]).reshape(b, n, HEADS, PK_TOPK * PK_TOPK)
        all_indices = (ix[..., :, None] * NUM_KEYS + iy[..., None, :]).reshape(b, n, HEADS, PK_TOPK * PK_TOPK)
        scores, pk_indices = jax.lax.top_k(all_scores, FINAL_TOPK)
        indices = jnp.take_along_axis(all_indices, pk_indices, axis=-1)
        weights_down = w_down[indices]
        weights_up = w_up[indices]
        h = jnp.einsum('bnd,bnhkd->bnhk', x, weights_down)
        h = jax.nn.gelu(h, approximate=False)
        h = h * jax.nn.relu(scores)
        return jnp.einsum('bnhk,bnhkd->bnd', h, weights_up)
    x = x + _L0_xattn_ref(_layernorm(x, axis=-1), ctx_1024, L0_xattn_Wq, L0_xattn_Wk, L0_xattn_Wv, L0_xattn_hist_W, L0_xattn_hist_b, L0_xattn_hist_ln_g, L0_xattn_hist_ln_b, L0_xattn_ctx_W1, L0_xattn_ctx_b1, L0_xattn_ctx_W2, L0_xattn_ctx_b2, L0_xattn_kg_W1, L0_xattn_kg_b1, L0_xattn_kg_ln_g, L0_xattn_kg_ln_b, L0_xattn_kg_W2, L0_xattn_kg_b2, L0_xattn_proj_W, L0_xattn_proj_b, mask_SxS_bc0)
    x = x + _L0_ffn_ref(_layernorm(x, axis=-1), L0_ffn_Wfc_s, L0_ffn_bfc_s, L0_ffn_Wproj_s, L0_ffn_bproj_s, L0_ffn_Wr, L0_ffn_Wfc, L0_ffn_bfc, L0_ffn_Wproj, L0_ffn_bproj)
    x = x + _L1_xattn_ref(ctx_1024, ctx_1024, _layernorm(x, axis=-1), mask_BxS2_if0, L1_xattn_Wk, L1_xattn_bk, L1_xattn_Wv, L1_xattn_bv, L1_xattn_Wq, L1_xattn_bq, L1_xattn_Woff, L1_xattn_boff, L1_xattn_Wo, L1_xattn_bo)
    x = x + _L1_ffn_ref(_layernorm(x, axis=-1), L1_ffn_gate_w, L1_ffn_expert_bias, L1_ffn_w1, L1_ffn_w2, L1_ffn_w3)
    x = x + _L2_xattn_ref(_layernorm(x, axis=-1), ctx_1024, L2_xattn_wq, L2_xattn_wk, L2_xattn_wv, L2_xattn_wo)
    x = x + _L2_ffn_ref(_layernorm(x, axis=-1), L2_ffn_W1, L2_ffn_b1, L2_ffn_W2, L2_ffn_b2, L2_ffn_Wr, L2_ffn_br)
    x = x + _L3_xattn_ref(_layernorm(x, axis=-1), ctx_1024, L3_xattn_W_qkv, L3_xattn_W_proj, L3_xattn_b_proj)
    x = x + _L3_ffn_ref(_layernorm(x, axis=-1), L3_ffn_w_q, L3_ffn_keys, L3_ffn_w_down, L3_ffn_w_up)
    return x

_drawn_inputs = setup_inputs


def setup_inputs(seed=0):
    import zlib

    import numpy as np

    out = dict(_drawn_inputs(seed))
    spreads = {'L0_xattn_hist_b': (0.0, 0.8),
     'L0_xattn_hist_ln_g': (1.0, 0.6),
     'L0_xattn_hist_ln_b': (0.0, 0.8),
     'L0_xattn_ctx_b1': (0.0, 0.8),
     'L0_xattn_kg_b1': (0.0, 0.752),
     'L0_xattn_kg_ln_g': (1.0, 0.6),
     'L0_xattn_kg_ln_b': (0.0, 0.8),
     'L0_xattn_kg_b2': (0.0, 0.8),
     'L0_xattn_proj_b': (0.0, 0.1),
     'L0_ffn_bfc_s': (0.0, 0.32),
     'L0_ffn_bproj_s': (0.0, 0.1),
     'L0_ffn_bfc': (0.0, 0.409),
     'L0_ffn_bproj': (0.0, 0.1),
     'L1_xattn_bk': (0.0, 0.8),
     'L1_xattn_bv': (0.0, 0.548),
     'L1_xattn_bq': (0.0, 0.8),
     'L1_xattn_boff': (0.0, 0.8),
     'L1_xattn_bo': (0.0, 0.1),
     'L1_ffn_expert_bias': (0.0, 0.8),
     'L3_xattn_b_proj': (0.0, 0.1)}
    factors = {'L0_xattn_hist_W': 2.94,
     'L0_xattn_ctx_W1': 8.0,
     'L0_xattn_ctx_W2': 8.0,
     'L1_xattn_Wk': 8.0,
     'L1_xattn_Wv': 3.345,
     'L1_xattn_Wq': 8.0,
     'L1_xattn_Woff': 8.0,
     'L1_xattn_Wo': 2.772,
     'L1_ffn_gate_w': 8.0,
     'L1_ffn_w1': 8.0,
     'L1_ffn_w2': 8.0,
     'L1_ffn_w3': 8.0,
     'L2_ffn_b1': 4.889,
     'L2_ffn_b2': 4.046,
     'L3_ffn_w_q': 8.0,
     'L3_ffn_keys': 8.0,
     'L3_ffn_w_down': 8.0,
     'L3_ffn_w_up': 8.0}
    for name, (base, spread) in spreads.items():
        noise = np.random.default_rng([zlib.crc32(name.encode()), seed]).standard_normal(out[name].shape)
        drawn = base * np.exp(spread * noise) if base else spread * noise
        out[name] = jnp.asarray(drawn.astype(out[name].dtype))
    for name, factor in factors.items():
        out[name] = (out[name] * factor).astype(out[name].dtype)
    return out
```

```python
from contextlib import ExitStack

import numpy as np

import concourse.bass as bass
from concourse import mybir

ALU = mybir.AluOpType
ACT = mybir.ActivationFunctionType
F32 = mybir.dt.float32
U32 = mybir.dt.uint32
I32 = mybir.dt.int32
U8 = mybir.dt.uint8
AX_X = mybir.AxisListType.X

P = 128
B, T, D = 4, 512, 128
NT = T // P
S2 = 77
H, HD = 16, 8
EPS = 1e-5
SCALE = HD ** -0.5
NK = 5
E = 8
HID = 512
HID1 = 352
CH1 = [(0, 128), (128, 128), (256, 96)]
R = 103
RT = -(-T // R)
RI = R + 2
NEG = -1e30
STOP = 99
PKH, PKN, PKD = 8, 32, 64


class Chain:

    def __init__(self, eng, sem):
        self.eng, self.sem, self.n = eng, sem, 0

    def link(self, ins):
        self.n += 1
        ins.then_inc(self.sem, 1)
        self.eng.wait_ge(self.sem, self.n)


def build(nc, A, out, stop_after=99):
    with ExitStack() as ctx:
        used = [0]

        def sb(name, shape, dt=F32):
            used[0] += int(np.prod(shape[1:])) * (1 if dt == U8 else 4)
            return ctx.enter_context(nc.sbuf_tensor(name, shape, dt))

        def sem(name):
            return ctx.enter_context(nc.semaphore(name))

        ps = ctx.enter_context(nc.psum_tensor("ps", [P, 8, 512], F32))

        ident = sb("ident", [P, P])
        shift = sb("shift", [P, 3, P])
        headmask = sb("headmask", [P, H])
        iota_j = sb("iota_j", [P, S2])
        iota_e = sb("iota_e", [P, E])
        iota_k = sb("iota_k", [P, PKN])
        neghalf = sb("neghalf", [P, 8])
        ref_k = sb("ref_k", [P, H, NK])
        loc = sb("loc", [P, NT])
        sel4 = sb("sel4", [B, B, P])
        scratch_i = sb("scratch_i", [P, P], I32)

        wq0 = sb("wq0", [P, D]); wk0 = sb("wk0", [P, D]); wv0 = sb("wv0", [P, D]); wp0 = sb("wp0", [P, D])
        pb0 = sb("pb0", [P, D])
        wa = [{n: sb(f"w{n}{i}", [P, D]) for n in "qkvo"} for i in (1, 2, 3)]
        woff = sb("woff", [P, H * NK]); boff = sb("boff", [P, H * NK])
        bq1 = sb("bq1", [P, 1]); bk1 = sb("bk1", [P, 1]); bv1 = sb("bv1", [P, D])
        bo1 = sb("bo1", [P, D]); bo3 = sb("bo3", [P, D])
        m77 = sb("m77", [P, B, S2], I32)
        len1 = sb("len1", [P, B]); rlen1 = sb("rlen1", [P, B])
        gw = sb("gw", [P, 3, E])
        gb = sb("gb", [P, 2, E])
        w1_0 = sb("w1_0", [P, E + 1, HID]); w2_0 = sb("w2_0", [P, E + 1, 4, D])
        b1_0 = sb("b1_0", [P, E + 1, 4]); bs0 = sb("bs0", [P, 1]); b2_0 = sb("b2_0", [E, D])
        w1_1 = sb("w1_1", [P, E, HID1]); w3_1 = sb("w3_1", [P, E, HID1]); w2_1 = sb("w2_1", [P, E, 3, D])
        w1_2 = sb("w1_2", [P, E, HID]); w2_2 = sb("w2_2", [P, E, 4, D])
        b1_2 = sb("b1_2", [P, E, 4]); b2_2 = sb("b2_2", [E, D])
        wcomb = sb("wcomb", [P, 2 * PKH * PKN])
        ctxT = sb("ctxT", [P, B, S2])
        kern = sb("kern", [P, B, H * 9])
        keep = sb("keep", [RI, RT, T], U8)
        maskq = sb("maskq", [R, RT, T], U8)
        zero8 = sb("zero8", [E, T])

        x = sb("x", [P, NT, D]); xn = sb("xn", [P, NT, D]); xnT = sb("xnT", [P, T])
        stats = sb("stats", [P, NT, 6]); mv = sb("mv", [P, NT, 2]); rstd = sb("rstd", [P, NT])
        ctxTb = sb("ctxTb", [P, S2]); kernb = sb("kernb", [P, H * 9])
        lenb = sb("lenb", [P, 2])
        gate = sb("gate", [P, NT, E]); glog = sb("glog", [P, NT, E]); gsel = sb("gsel", [P, NT, E])
        gtop = sb("gtop", [P, NT, 8]); gidx = sb("gidx", [P, NT, 8], U32); gidf = sb("gidf", [P, NT, 2])
        gm = sb("gm", [P, 2, NT, E]); gs = sb("gs", [P, NT]); gr = sb("gr", [P, NT])
        gT = sb("gT", [E, T])
        arena = sb("arena", [P, 13200])


        at = [0]

        def carve(*shape, rows=P, dt=F32):
            n = int(np.prod(shape))
            v = arena[0:rows, at[0]:at[0] + n]
            at[0] += n
            assert at[0] <= 13200, at[0]
            if dt is not F32:
                v = v.bitcast(dt)
            names = "abcd"[:len(shape)]
            if len(shape) > 1:
                v = v.rearrange(f"p ({' '.join(names)}) -> p {' '.join(names)}",
                                **{n_: s for n_, s in zip(names, shape)})
            return v

        done = sem("done")
        ln_stats = sem("ln_stats"); ln_mean = sem("ln_mean"); ln_rstd = sem("ln_rstd")
        ln_xn = sem("ln_xn"); ln_turned = sem("ln_turned"); ln_xnT = sem("ln_xnT")
        x_new = sem("x_new")
        dve_chain = sem("dve_chain"); act_chain = sem("act_chain"); pool_chain = sem("pool_chain")
        x_in = sem("x_in"); x_out = sem("x_out"); batch_in = sem("batch_in")
        loop_sems = [ln_stats, ln_mean, ln_rstd, ln_xn, ln_turned, ln_xnT, x_new, dve_chain,
                     act_chain, pool_chain, x_in, x_out, batch_in]

        def lsem(name):
            s = sem(name)
            loop_sems.append(s)
            return s

        W = {k: sem("w_" + k) for k in ("attn0", "misc", "ffn0", "ffn1", "ffn2", "last", "kgen", "keep", "p3")}
        wcount = {k: 0 for k in W}

        def clear_sems(sems):
            for s in sems:
                nc.gpsimd.sem_clear(s)
            nc.all_engine_barrier()

        at[0] = 0
        ctx_sb = carve(B, D, rows=S2)
        histw = carve(2 * D)
        histb = carve(2 * D, rows=S2); histg = carve(2 * D, rows=S2); histlb = carve(2 * D, rows=S2)
        cw1 = carve(2, 64); cb1 = carve(64, rows=S2); cw2 = carve(64, rows=S2); cb2 = carve(1, rows=S2)
        kw1 = carve(2, D); kb1 = carve(D, rows=B); kg = carve(D, rows=B); kb = carve(D, rows=B)
        kw2 = carve(H * 9); kb2 = carve(H * 9, rows=B)
        eh = carve(B, 2 * D, rows=S2); ehT = carve(B, 2, S2)
        hst = carve(B, 6, rows=S2); hmv = carve(B, 2, rows=S2); hrs = carve(B, rows=S2)
        aw1 = carve(B, 64, rows=S2); aws = carve(B, rows=S2); awt = carve(S2, rows=B); awn = carve(S2, rows=B)
        sm = carve(4, rows=B); awc = carve(B, rows=S2); ccT = carve(2, B)
        kh = carve(D, rows=B); khT = carve(B); kst = carve(6, rows=B); kmv = carve(2, rows=B)
        krs = carve(1, rows=B); kp = carve(H, 9, rows=B); kmx = carve(H, rows=B)
        wqt = carve(8, D); keyd = carve(8, 2 * PKN)

        p_const = sem("p_const"); p_pe = sem("p_pe"); p_dve = sem("p_dve"); p_act = sem("p_act")
        p_dvec = sem("p_dvec"); p_pool = sem("p_pool"); p_poolc = sem("p_poolc")
        with nc.Block() as block:
            @block.sync
            def _(sp):
                def ld(group, dst, src):
                    wcount[group] += 16
                    sp.dma_start(dst, src).then_inc(W[group], 16)

                row = lambda v, n: v.rearrange("(a n) -> a n", a=1).to_broadcast([n, v.shape[0]])
                ld("kgen", ctx_sb, A["ctx_1024"].rearrange("b s d -> s b d"))
                ld("kgen", histw, A["hist_W"])
                ld("kgen", histb, row(A["hist_b"], S2))
                ld("kgen", histg, row(A["hist_ln_g"], S2))
                ld("kgen", histlb, row(A["hist_ln_b"], S2))
                ld("kgen", cw1, A["ctx_W1"].rearrange("(c p) n -> p c n", p=P))
                ld("kgen", cb1, row(A["ctx_b1"], S2))
                ld("kgen", cw2, row(A["ctx_W2"], S2))
                ld("kgen", cb2, row(A["ctx_b2"], S2))
                ld("kgen", kw1, A["kg_W1"].rearrange("(c p) n -> p c n", p=P))
                ld("kgen", kb1, row(A["kg_b1"], B))
                ld("kgen", kg, row(A["kg_ln_g"], B))
                ld("kgen", kb, row(A["kg_ln_b"], B))
                ld("kgen", kw2, A["kg_W2"])
                ld("kgen", kb2, row(A["kg_b2"], B))
                ld("p3", wqt, A["w_qT"].rearrange("(c p) d -> p c d", p=P))
                ld("attn0", wq0[:, :], A["Wq0"]); ld("attn0", wk0[:, :], A["Wk0"])
                ld("attn0", wv0[:, :], A["Wv0"]); ld("attn0", wp0[:, :], A["Wp0"])
                ld("attn0", pb0[:, :], row(A["bp0"], P))
                sp.wait_ge(p_const, 1)
                for t in range(RT):
                    lo, hi = max(0, R * t - 1), min(T, R * t + R + 1)
                    o = lo - (R * t - 1)
                    ld("keep", keep[o:o + hi - lo, t, :], A["mask"][lo:hi, :])
                for t in range(RT):
                    n = min(R, T - R * t)
                    ld("keep", maskq[0:n, t, :], A["mask"][R * t:R * t + n, :])
                ld("misc", m77[:, :, :], A["mask2"].rearrange("(a b) s -> a b s", a=1).to_broadcast([P, B, S2]))
                for i, d in enumerate(wa):
                    for n in "qkvo":
                        ld("misc", d[n][:, :], A[f"w{n}{i + 1}"])
                ld("misc", woff[:, :], A["Woff"]); ld("misc", boff[:, :], row(A["boff"], P))
                ld("misc", bq1[:, :], A["bq1"].rearrange("(n a) -> n a", a=1))
                ld("misc", bk1[:, :], A["bk1"].rearrange("(n a) -> n a", a=1))
                ld("misc", bv1[:, :], row(A["bv1"], P)); ld("misc", bo1[:, :], row(A["bo1"], P))
                ld("misc", bo3[:, :], row(A["bo3"], P))
                for i, n in enumerate(("Wr0", "Wr1", "Wr2")):
                    ld("misc", gw[:, i, :], A[n])
                ld("misc", gb[:, 0, :], row(A["eb1"], P)); ld("misc", gb[:, 1, :], row(A["br2"], P))
                ld("ffn0", w1_0[:, 0, :], A["Wfc_s"])
                ld("ffn0", w1_0[:, 1:, :], A["Wfc"].rearrange("e d h -> d e h"))
                ld("ffn0", w2_0[:, 0, :, :], A["Wproj_s"].rearrange("(c p) d -> p c d", p=P))
                ld("ffn0", b1_0[:, :, :], A["bfc"])
                for e in range(E):
                    ld("ffn0", w2_0[:, 1 + e, :, :], A["Wproj"][e].rearrange("(c p) d -> p c d", p=P))
                ld("ffn0", bs0[:, :], A["bproj_s"].rearrange("(n a) -> n a", a=1))
                ld("ffn0", b2_0[:, :], A["bproj"])
                ld("ffn1", w1_1[:, :, :], A["w1"].rearrange("e d h -> d e h"))
                ld("ffn1", w3_1[:, :, :], A["w3"].rearrange("e d h -> d e h"))
                for e in range(E):
                    ld("ffn1", w2_1[:, e, 0:2, :], A["w2"][e, 0:256].rearrange("(c p) d -> p c d", p=P))
                    ld("ffn1", w2_1[0:96, e, 2, :], A["w2"][e, 256:HID1])
                ld("ffn2", w1_2[:, :, :], A["W1"].rearrange("e d h -> d e h"))
                for e in range(E):
                    ld("ffn2", w2_2[:, e, :, :], A["W2"][e].rearrange("(c p) d -> p c d", p=P))
                ld("ffn2", b2_2[:, :], A["b2"])
                ld("ffn2", b1_2[:, :, :], A["b1"])
                for s, n in wcount.items():
                    if n:
                        sp.wait_ge(W[s], n)

            @block.gpsimd
            def _(pool):
                ch = Chain(pool, p_poolc)
                nc.gpsimd.memset(maskq[:, :, :], 0)
                nc.gpsimd.memset(zero8[:, :], 0.0)
                ch.link(nc.gpsimd.memset(keep[:, :, :], 1))
                nc.gpsimd.memset(neghalf[:, :], -0.5).then_inc(p_const, 1)
                ch.link(nc.gpsimd.memset(keyd, 0.0))
                for c in range(8):
                    p_, hp = c // 4, c % 4
                    for u in range(2):
                        pool.dma_start(keyd[64 * u:64 * u + 64, c, PKN * u:PKN * u + PKN],
                                       A["keysT"][2 * hp + u, p_]).then_inc(W["last"], 16)
                ch.link(nc.gpsimd.memset(ident[:, :], 0.0))
                ch.link(nc.gpsimd.affine_select(out=ident[:, :], in_=ident[:, :], compare_op=ALU.not_equal,
                                                fill=1.0, base=0, pattern=[[-1, P]], channel_multiplier=1))
                ch.link(nc.gpsimd.memset(shift[:, :, :], 0.0))
                ch.link(nc.gpsimd.affine_select(out=shift[:, :, :], in_=shift[:, :, :], compare_op=ALU.not_equal,
                                                fill=1.0, base=0, pattern=[[-1, 3], [-1, P]], channel_multiplier=1))
                ch.link(nc.gpsimd.memset(headmask[:, :], 1.0))
                ch.link(nc.gpsimd.affine_select(out=headmask[:, :], in_=headmask[:, :], compare_op=ALU.is_ge,
                                                fill=0.0, base=0, pattern=[[-HD, H]], channel_multiplier=1))
                ch.link(nc.gpsimd.affine_select(out=headmask[:, :], in_=headmask[:, :], compare_op=ALU.is_ge,
                                                fill=0.0, base=HD - 1, pattern=[[HD, H]], channel_multiplier=-1))
                ch.link(nc.gpsimd.memset(sel4[:, :, :], 0.0))
                ch.link(nc.gpsimd.affine_select(out=sel4[:, :, :], in_=sel4[:, :, :], compare_op=ALU.not_equal,
                                                fill=1.0, base=0, pattern=[[-1, B], [0, P]], channel_multiplier=1))
                fl = dict(allow_small_or_imprecise_dtypes=True)
                ch.link(nc.gpsimd.iota(iota_j[:, :], [[1, S2]], base=0, channel_multiplier=0, **fl))
                ch.link(nc.gpsimd.iota(iota_e[:, :], [[1, E]], base=0, channel_multiplier=0, **fl))
                ch.link(nc.gpsimd.iota(iota_k[:, :], [[1, PKN]], base=-PKN, channel_multiplier=0, **fl))
                ch.link(nc.gpsimd.iota(ref_k[:, :, :], [[0, H], [1, NK]], base=-3, channel_multiplier=0, **fl))
                nc.gpsimd.iota(loc[:, :], [[P, NT]], base=0, channel_multiplier=1, **fl).then_inc(p_const, 1)
                pool.wait_ge(p_dve, 2)
                ch.link(nc.gpsimd.tensor_scalar(hrs, hmv[:, :, 1], EPS, None, ALU.add))
                nc.gpsimd.tensor_tensor(hrs, hrs, neghalf[0:S2, 0:B], ALU.pow).then_inc(p_pool, 1)
                pool.wait_ge(p_dve, 9)
                ch.link(nc.gpsimd.tensor_scalar(krs, kmv[:, 1:2], EPS, None, ALU.add))
                nc.gpsimd.tensor_tensor(krs, krs, neghalf[0:B, 0:1], ALU.pow).then_inc(p_pool, 1)

            @block.tensor
            def _(pe):
                pe.wait_ge(p_const, 2)
                pe.wait_ge(W["kgen"], wcount["kgen"])
                for b in range(B):
                    mm = nc.tensor.transpose(ps[:, 0, b * P:b * P + S2], ctx_sb[:, b, :], ident[0:S2, 0:S2])
                mm.then_inc(p_pe, 1)
                pe.wait_ge(p_dve, 1)
                for b in range(B):
                    mm = nc.tensor.matmul(ps[0:S2, 1 + b // 2, (b % 2) * 256:(b % 2) * 256 + 256], ctxT[:, b, :], histw,
                                          start=True, stop=True)
                mm.then_inc(p_pe, 1)
                pe.wait_ge(p_act, 1)
                for b in range(B):
                    for c in range(2):
                        o = (b * 2 + c) % 4 * P
                        mm = nc.tensor.transpose(ps[:, 3 + b // 2, o:o + S2], eh[:, b, c * P:c * P + P],
                                                 ident[0:S2, 0:S2])
                mm.then_inc(p_pe, 1)
                pe.wait_ge(p_dve, 3)
                for b in range(B):
                    for c in range(2):
                        mm = nc.tensor.matmul(ps[0:S2, 5, b * 64:b * 64 + 64], ehT[:, b, c, :], cw1[:, c, :],
                                              start=c == 0, stop=c == 1)
                mm.then_inc(p_pe, 1)
                pe.wait_ge(p_dve, 5)
                nc.tensor.transpose(ps[0:B, 6, 0:S2], aws, ident[0:S2, 0:S2]).then_inc(p_pe, 1)
                pe.wait_ge(p_dve, 7)
                nc.tensor.transpose(ps[0:S2, 6, 128:128 + B], awn, ident[0:B, 0:B]).then_inc(p_pe, 1)
                pe.wait_ge(p_act, 4)
                for b in range(B):
                    for c in range(2):
                        mm = nc.tensor.matmul(ps[:, 7, c * B + b:c * B + b + 1], eh[:, b, c * P:c * P + P],
                                              awc[:, b:b + 1], start=True, stop=True)
                mm.then_inc(p_pe, 1)
                pe.wait_ge(p_act, 5)
                for c in range(2):
                    mm = nc.tensor.matmul(ps[0:B, 0, 0:D], ccT[:, c, :], kw1[:, c, :], start=c == 0, stop=c == 1)
                mm.then_inc(p_pe, 1)
                pe.wait_ge(p_act, 6)
                nc.tensor.transpose(ps[:, 1, 0:B], kh, ident[0:B, 0:B]).then_inc(p_pe, 1)
                pe.wait_ge(p_act, 7)
                nc.tensor.matmul(ps[0:B, 2, 0:H * 9], khT, kw2, start=True, stop=True).then_inc(p_pe, 1)
                pe.wait_ge(p_dve, 12)
                for b in range(B):
                    mm = nc.tensor.matmul(ps[:, 3 + b // 2, (b % 2) * 256:(b % 2) * 256 + H * 9], sel4[:, b, :],
                                          kp.rearrange("p h n -> p (h n)"), start=True, stop=True)
                mm.then_inc(p_pe, 1)
                pe.wait_ge(W["p3"], wcount["p3"])
                pe.wait_ge(W["last"], 16 * 16)
                for c in range(8):
                    mm = nc.tensor.matmul(ps[:, 5, c * 64:c * 64 + 64], wqt[:, c, :], keyd[:, c, :],
                                          start=True, stop=True)
                mm.then_inc(p_pe, 1)

            @block.vector
            def _(dve):
                ch = Chain(dve, p_dvec)
                dve.wait_ge(p_pe, 1)
                nc.vector.tensor_copy(ctxT[:, :, :], ps[:, 0, :].rearrange("p (b s) -> p b s", b=B)[:, :, 0:S2])\
                    .then_inc(p_dve, 1)
                dve.wait_ge(p_pe, 2)
                for b in range(B):
                    src = ps[0:S2, 1 + b // 2, (b % 2) * 256:(b % 2) * 256 + 256]
                    ch.link(nc.vector.tensor_tensor(eh[:, b, :], src, histb, ALU.add))
                    ch.link(nc.vector.bn_stats(hst[:, b, :], eh[:, b, :]))
                    ch.link(nc.vector.bn_aggr(hmv[:, b, :], hst[:, b, :]))
                nc.vector.memset(sm[:, :], 0.0).then_inc(p_dve, 1)
                dve.wait_ge(p_pool, 1)
                for b in range(B):
                    ch.link(nc.vector.tensor_scalar(eh[:, b, :], eh[:, b, :], hmv[:, b, 0:1], hrs[:, b:b + 1],
                                                    ALU.subtract, ALU.mult))
                    ch.link(nc.vector.tensor_tensor(eh[:, b, :], eh[:, b, :], histg, ALU.mult))
                    ch.link(nc.vector.tensor_tensor(eh[:, b, :], eh[:, b, :], histlb, ALU.add))
                dve.wait_ge(p_pe, 3)
                for b in range(B):
                    src = ps[:, 3 + b // 2, (b % 2) * 256:(b % 2) * 256 + 256]
                    last = nc.vector.tensor_copy(ehT[:, b, :, :], src.rearrange("p (c s) -> p c s", c=2)[:, :, 0:S2])
                last.then_inc(p_dve, 1)
                dve.wait_ge(p_pe, 4)
                nc.vector.tensor_tensor(aw1, ps[0:S2, 5, 0:B * 64].rearrange("p (b n) -> p b n", b=B),
                                        cb1.unsqueeze(1).to_broadcast([S2, B, 64]), ALU.add).then_inc(p_dve, 1)
                dve.wait_ge(p_act, 2)
                ch.link(nc.vector.tensor_tensor(aw1, aw1, cw2.unsqueeze(1).to_broadcast([S2, B, 64]), ALU.mult))
                ch.link(nc.vector.tensor_reduce(aws, aw1, AX_X, ALU.add))
                nc.vector.tensor_scalar(aws, aws, cb2, None, ALU.add).then_inc(p_dve, 1)
                dve.wait_ge(p_pe, 5)
                ch.link(nc.vector.tensor_reduce(sm[:, 0:1], ps[0:B, 6, 0:S2], AX_X, ALU.max))
                nc.vector.tensor_scalar(awt, ps[0:B, 6, 0:S2], sm[:, 0:1], None, ALU.subtract).then_inc(p_dve, 1)
                dve.wait_ge(p_act, 3)
                ch.link(nc.vector.tensor_reduce(sm[:, 1:2], awt, AX_X, ALU.add))
                ch.link(nc.vector.reciprocal(sm[:, 2:3], sm[:, 1:2]))
                nc.vector.tensor_scalar(awn, awt, sm[:, 2:3], None, ALU.mult).then_inc(p_dve, 1)
                dve.wait_ge(p_pe, 8)
                ch.link(nc.vector.tensor_tensor(kh, ps[0:B, 0, 0:D], kb1, ALU.add))
                ch.link(nc.vector.bn_stats(kst, kh))
                nc.vector.bn_aggr(kmv, kst).then_inc(p_dve, 2)
                dve.wait_ge(p_pool, 2)
                ch.link(nc.vector.tensor_scalar(kh, kh, kmv[:, 0:1], krs, ALU.subtract, ALU.mult))
                ch.link(nc.vector.tensor_tensor(kh, kh, kg, ALU.mult))
                nc.vector.tensor_tensor(kh, kh, kb, ALU.add).then_inc(p_dve, 1)
                dve.wait_ge(p_pe, 10)
                kp2 = kp.rearrange("p h n -> p (h n)")
                ch.link(nc.vector.tensor_tensor(kp2, ps[0:B, 2, 0:H * 9], kb2, ALU.add))
                ch.link(nc.vector.tensor_reduce(kmx, kp, AX_X, ALU.max))
                nc.vector.tensor_tensor(kp, kp, kmx.unsqueeze(2).to_broadcast([B, H, 9]), ALU.subtract)\
                    .then_inc(p_dve, 1)
                dve.wait_ge(p_act, 8)
                ch.link(nc.vector.tensor_reduce(kmx, kp, AX_X, ALU.add))
                ch.link(nc.vector.reciprocal(kmx, kmx))
                nc.vector.tensor_tensor(kp, kp, kmx.unsqueeze(2).to_broadcast([B, H, 9]), ALU.mult)\
                    .then_inc(p_dve, 1)
                dve.wait_ge(p_pe, 11)
                for b in range(B):
                    nc.vector.tensor_copy(kern[:, b, :], ps[:, 3 + b // 2, (b % 2) * 256:(b % 2) * 256 + H * 9])
                dve.wait_ge(p_pe, 12)
                nc.vector.tensor_copy(wcomb[:, :], ps[:, 5, :])
                dve.wait_ge(W["misc"], wcount["misc"])
                mf = arena[:, 12000:12000 + B * S2].rearrange("p (b s) -> p b s", b=B)
                ch.link(nc.vector.tensor_scalar(mf, m77[:, :, :], -1.0, 1.0, ALU.mult, ALU.add))
                ch.link(nc.vector.tensor_reduce(len1[:, :], mf, AX_X, ALU.add))
                ch.link(nc.vector.tensor_scalar(len1[:, :], len1[:, :], -1.0, None, ALU.add))
                ch.link(nc.vector.reciprocal(rlen1[:, :], len1[:, :]))
                dve.wait_ge(W["keep"], wcount["keep"])
                nc.vector.tensor_scalar(keep[:, :, :], keep[:, :, :], -1.0, 1.0, ALU.mult, ALU.add)

            @block.scalar
            def _(act):
                act.wait_ge(p_dvec, 6 * B)
                nc.scalar.activation(eh, eh, ACT.Gelu).then_inc(p_act, 1)
                act.wait_ge(p_dve, 4)
                nc.scalar.activation(aw1, aw1, ACT.Gelu).then_inc(p_act, 1)
                act.wait_ge(p_dve, 6)
                nc.scalar.activation(awt, awt, ACT.Exp).then_inc(p_act, 1)
                act.wait_ge(p_pe, 6)
                nc.scalar.copy(awc, ps[0:S2, 6, 128:128 + B]).then_inc(p_act, 1)
                act.wait_ge(p_pe, 7)
                nc.scalar.copy(ccT, ps[:, 7, 0:2 * B].rearrange("p (c b) -> p c b", c=2)).then_inc(p_act, 1)
                act.wait_ge(p_dve, 10)
                nc.scalar.activation(kh, kh, ACT.Gelu).then_inc(p_act, 1)
                act.wait_ge(p_pe, 9)
                nc.scalar.copy(khT, ps[:, 1, 0:B]).then_inc(p_act, 1)
                act.wait_ge(p_dve, 11)
                nc.scalar.activation(kp, kp, ACT.Exp).then_inc(p_act, 1)

        at[0] = 0
        qT = carve(RT * R + 2)
        kT0 = carve(T); v0 = carve(NT, D)
        qm = carve(RT * R + 2); band = carve(3, R)
        sc = carve(2, T + 2); pr = carve(2, T); pT = carve(2, 4, R)
        at_out = carve(RT, D); mx = carve(8); rs = carve(RT); rr = carve(RT)
        oT = carve(T)
        at[0] = 0
        qTx = carve(T); kTx = carve(S2); vx = carve(D, rows=S2); kbd = carve(H, S2)
        sx = carve(H, S2); aT = carve(H, P, rows=S2); ox = carve(D); oTx = carve(P)
        smx = carve(H); ssm = carve(H); srs = carve(H)
        offs = carve(NT, H * NK); ofq = carve(NT, H * NK); off_i = carve(NT, H * NK, dt=I32)
        HG = 4
        hat = carve(HG, NK, S2); hpr = carve(HG, NK, S2)
        psc = carve(H, NK); pmx = carve(H)
        ax = carve(H, S2)
        at[0] = 0
        hb = carve(4, T); xs = carve(2, T); yT = carve(T)
        at[0] = 0
        sims = carve(16, PKN); eqk = carve(16, PKN); kmax = carve(16); kidx = carve(16)
        eid = carve(8); eidi = carve(8, dt=I32); esc = carve(8); dots = carve(8); hv = carve(8)
        rows_g = carve(PKH, 2 * D); junk = carve(D); accu = carve(D)

        rows_in = sem("rows_in")
        b_ready = lsem("b_ready")
        q0_mm = lsem("q0_mm"); q0_sb = lsem("q0_sb")
        g = {n: lsem("g_" + n) for n in ("log", "max", "exp", "done", "turn", "gT")}
        f = {n: lsem("f_" + n) for n in ("up", "act", "hg", "gb", "xs", "down", "y", "ysb", "yt")}
        a = {n: lsem("a_" + n) for n in ("proj", "q", "kv", "s", "sub", "exp", "p", "turn", "aT", "o", "osb",
                                         "ot", "otsb", "y", "off", "offsb", "hat", "abs", "hatok", "softk", "softe", "aT_even")}
        k = {n: lsem("k_" + n) for n in ("sim", "idx", "dot", "act")}
        i0 = {n: lsem("i0_" + n) for n in ("qm", "s", "a", "c", "m", "p", "t", "pt", "o", "n", "mb", "turn", "oT", "y")}

        bnk = lambda i: ps[:, i, :]
        HS = [(0, 6), (6, 12), (12, 16)]
        U0 = 4 * (E + 1)
        NX = (1, 2, 6, 7, 11, 12, 16, 20)[min(stop_after, 7)]

        with nc.Fori(0, B) as b:
            with nc.Block() as block:
                @block.sync
                def _(sp):
                    sp.dma_start(x[:, :, :], A["x"][bass.ds(b, 1)].rearrange("a (t p) d -> p (a t) d", p=P))\
                        .then_inc(x_in, 16)

                @block.gpsimd
                def _(pool):
                    ch = Chain(pool, pool_chain)
                    norm_pool(nc, pool, ch, 0, ln_mean, ln_rstd, mv, rstd, neghalf)

                @block.vector
                def _(dve):
                    nc.vector.tensor_copy(kernb[:, :], kern[:, bass.ds(b, 1), :].rearrange("p a n -> p (a n)"))
                    nc.vector.tensor_copy(ctxTb[:, :], ctxT[:, bass.ds(b, 1), :].rearrange("p a n -> p (a n)"))
                    nc.vector.tensor_copy(lenb[:, 0:1], len1[:, bass.ds(b, 1)])
                    nc.vector.tensor_copy(lenb[:, 1:2], rlen1[:, bass.ds(b, 1)])
                    nc.vector.memset(qT[:, 0:1], 0.0)
                    nc.vector.memset(qT[:, 1 + T:RT * R + 2], 0.0)
                    nc.vector.memset(sc[:, :, 0:1], 0.0)
                    nc.vector.memset(sc[:, :, T + 1:T + 2], 0.0)
                    dve.wait_ge(x_in, 16)
                    norm_vector(nc, dve, 0, x, xn, stats, mv, rstd, ln_stats, ln_mean, ln_rstd, ln_xn)
                    dve.wait_ge(q0_mm, 2)
                    nc.vector.tensor_copy(kT0, bnk(2)).then_inc(q0_sb, 1)
                    dve.wait_ge(q0_mm, 3)
                    nc.vector.tensor_copy(v0, bnk(3).rearrange("p (t d) -> p t d", t=NT)).then_inc(q0_sb, 1)

                @block.tensor
                def _(pe):
                    norm_tensor(nc, pe, 0, xn, ident, bnk(0), ln_xn, ln_turned)
                    pe.wait_ge(ln_xnT, 1)
                    nc.tensor.matmul(bnk(1), wq0[:, :], xnT[:, :], start=True, stop=True).then_inc(q0_mm, 1)
                    nc.tensor.matmul(bnk(2), wk0[:, :], xnT[:, :], start=True, stop=True).then_inc(q0_mm, 1)
                    for t in range(NT):
                        mm = nc.tensor.matmul(ps[:, 3, t * P:t * P + P], xnT[:, t * P:t * P + P], wv0[:, :],
                                              start=True, stop=True)
                    mm.then_inc(q0_mm, 1)

                @block.scalar
                def _(act):
                    norm_scalar(nc, act, 0, xnT, bnk(0), ln_turned, ln_xnT)
                    act.wait_ge(q0_mm, 1)
                    nc.scalar.copy(qT[:, 1:1 + T], bnk(1))
            clear_sems(loop_sems)

            with nc.Fori(0, H) as h:
                with nc.Block() as block:
                    @block.vector
                    def _(dve):
                        ch = Chain(dve, dve_chain)
                        nc.vector.tensor_scalar(qm, qT, headmask[:, bass.ds(h, 1)], None, ALU.mult)\
                            .then_inc(i0["qm"], 1)
                        for dx in range(3):
                            for dy in range(3):
                                w = kernb[0:RI, bass.ds(h * 9 + (dy * 3 + dx), 1)]
                                if dy == 0:
                                    ch.link(nc.vector.tensor_scalar(band[0:RI, dx, :], shift[0:RI, 0, 0:R], w, None,
                                                                    ALU.mult))
                                else:
                                    ins = nc.vector.scalar_tensor_tensor(band[0:RI, dx, :], shift[0:RI, dy, 0:R], w,
                                                                         band[0:RI, dx, :], ALU.mult, ALU.add)
                                    if dy == 2:
                                        ins.then_inc(i0["qm"], 1)
                                    else:
                                        ch.link(ins)

                        def finish(t):
                            dve.wait_ge(i0["t"], t + 1)
                            nc.vector.tensor_copy(pT[:, t % 2, :, :], ps[:, 4 + t % 2, 0:4 * R]
                                                  .rearrange("p (c r) -> p c r", c=4)).then_inc(i0["pt"], 1)
                            dve.wait_ge(i0["p"], t + 1)
                            ch.link(nc.vector.reciprocal(rr[0:R, t:t + 1], rs[0:R, t:t + 1]))
                            dve.wait_ge(i0["o"], t + 1)
                            nc.vector.tensor_scalar(at_out[0:R, t, bass.ds(h * HD, HD)],
                                                    ps[0:R, 6, t * HD:t * HD + HD], rr[0:R, t:t + 1], None, ALU.mult)

                        for t in range(RT):
                            dve.wait_ge(i0["s"], t + 1)
                            if t >= 2:
                                dve.wait_ge(i0["c"], t - 1)
                            nc.vector.tensor_tensor(sc[0:RI, t % 2, 1:T + 1], ps[0:RI, t % 2, :], keep[:, t, :], ALU.mult)\
                                .then_inc(i0["a"], 1)
                            dve.wait_ge(i0["c"], t + 1)
                            if t >= 2:
                                dve.wait_ge(i0["t"], t - 1)
                            ch.link(nc.vector.scalar_tensor_tensor(pr[0:R, t % 2, :], maskq[0:R, t, :], NEG,
                                                                   ps[0:R, 2 + t % 2, :], ALU.mult, ALU.add))
                            ch.link(nc.vector.tensor_reduce(mx[0:R, t:t + 1], pr[0:R, t % 2, :], AX_X, ALU.max))
                            nc.vector.tensor_scalar(mx[0:R, t:t + 1], mx[0:R, t:t + 1], -SCALE, None, ALU.mult)\
                                .then_inc(i0["m"], 1)
                            if t >= 1:
                                finish(t - 1)
                        finish(RT - 1)

                    @block.tensor
                    def _(pe):
                        pe.wait_ge(i0["qm"], 1)

                        def scores(t):
                            if t >= 2:
                                pe.wait_ge(i0["a"], t - 1)
                            nc.tensor.matmul(ps[0:RI, t % 2, :], qm[:, R * t:R * t + RI], kT0, start=True, stop=True)\
                                .then_inc(i0["s"], 1)

                        def pv(t):
                            pe.wait_ge(i0["p"], t + 1)
                            if t >= 2:
                                pe.wait_ge(i0["pt"], t - 1)
                            for c in range(4):
                                mm = nc.tensor.transpose(ps[:, 4 + t % 2, c * R:c * R + R],
                                                         pr[0:R, t % 2, c * P:c * P + P], ident[0:R, 0:R])
                            mm.then_inc(i0["t"], 1)
                            pe.wait_ge(i0["pt"], t + 1)
                            for c in range(4):
                                mm = nc.tensor.matmul(ps[0:R, 6, t * HD:t * HD + HD], pT[:, t % 2, c, :],
                                                      v0[:, c, bass.ds(h * HD, HD)], start=c == 0, stop=c == 3)
                            mm.then_inc(i0["o"], 1)

                        scores(0)
                        for t in range(RT):
                            if t + 1 < RT:
                                scores(t + 1)
                            pe.wait_ge(i0["a"], t + 1)
                            pe.wait_ge(i0["qm"], 4)
                            if t >= 2:
                                pe.wait_ge(i0["m"], t - 1)
                            for dx in range(3):
                                mm = nc.tensor.matmul(ps[0:R, 2 + t % 2, :], band[0:RI, dx, :],
                                                      sc[0:RI, t % 2, dx:dx + T], start=dx == 0, stop=dx == 2)
                            mm.then_inc(i0["c"], 1)
                            if t >= 1:
                                pv(t - 1)
                        pv(RT - 1)

                    @block.scalar
                    def _(act):
                        for t in range(RT):
                            act.wait_ge(i0["m"], t + 1)
                            nc.scalar.activation(pr[0:R, t % 2, :], pr[0:R, t % 2, :], ACT.Exp, bias=mx[0:R, t:t + 1],
                                                 scale=SCALE, accum_out=rs[0:R, t:t + 1]).then_inc(i0["p"], 1)
                clear_sems(loop_sems)

            with nc.Block() as block:
                LN = dict(x=x, xn=xn, stats=stats, mv=mv, rstd=rstd, ln_stats=ln_stats, ln_mean=ln_mean,
                          ln_rstd=ln_rstd, ln_xn=ln_xn)

                @block.sync
                def _(sp):
                    sp.wait_ge(x_new, NX)
                    sp.dma_start(out[bass.ds(b, 1)].rearrange("a (t p) d -> p (a t) d", p=P), x[:, :, :])\
                        .then_inc(x_out, 16)
                    sp.wait_ge(x_out, 16)

                @block.gpsimd
                def _(pool):
                    ch = Chain(pool, pool_chain)
                    norm = lambda n: norm_pool(nc, pool, ch, n, ln_mean, ln_rstd, mv, rstd, neghalf)
                    for n in range(min(7, stop_after)):
                        norm(n)
                    for t in range(NT if stop_after >= 7 else 0):
                        pool.wait_ge(k["idx"], t + 1)
                        for h in range(PKH):
                            pool.indirect_dma_start(out=rows_g[:, h, :], out_offset=None, in_=A["w_ud"],
                                                    in_offset=bass.IndirectOffsetOnAxis(ap=eidi[:, h:h + 1], axis=0))\
                                .then_inc(rows_in, 16)

                @block.vector
                def _(dve):
                    ch = Chain(dve, dve_chain)
                    nx = [0]

                    def norm(n):
                        if nx[0]:
                            dve.wait_ge(x_new, nx[0])
                        norm_vector(nc, dve, n, **LN)

                    def add_x(ins):
                        nx[0] += 1
                        ins.then_inc(x_new, 1)

                    def gates(n):
                        dve.wait_ge(g["log"], n + 1)
                        lg = ps[:, 7, 0:NT * E].rearrange("p (t e) -> p t e", t=NT)
                        if n == 2:
                            ch.link(nc.vector.tensor_tensor(glog[:, :, :], lg, gb[:, 1:2, :].to_broadcast([P, NT, E]), ALU.add))
                        else:
                            ch.link(nc.vector.tensor_copy(glog[:, :, :], lg))
                        ch.link(nc.vector.tensor_reduce(gs[:, :], glog[:, :, :], AX_X, ALU.max))
                        nc.vector.tensor_tensor(glog[:, :, :], glog[:, :, :], gs[:, :].unsqueeze(2).to_broadcast([P, NT, E]),
                                                ALU.subtract).then_inc(g["max"], 1)
                        dve.wait_ge(g["exp"], n + 1)
                        ch.link(nc.vector.tensor_reduce(gs[:, :], glog[:, :, :], AX_X, ALU.add))
                        ch.link(nc.vector.reciprocal(gr[:, :], gs[:, :]))
                        ch.link(nc.vector.tensor_tensor(glog[:, :, :], glog[:, :, :], gr[:, :].unsqueeze(2).to_broadcast([P, NT, E]),
                                                        ALU.mult))
                        pick = glog
                        if n == 1:
                            pick = gsel
                            ch.link(nc.vector.tensor_tensor(gsel[:, :, :], glog[:, :, :], gb[:, 0:1, :].to_broadcast([P, NT, E]),
                                                            ALU.add))
                        for t in range(NT):
                            ins = nc.vector.max(gtop[:, t, :], pick[:, t, :])
                            ins.then_inc(dve_chain, 1)
                            ch.n += 1
                        dve.wait_ge(dve_chain, ch.n)
                        for t in range(NT):
                            ins = nc.vector.max_index(gidx[:, t, :], gtop[:, t, :], pick[:, t, :])
                            ins.then_inc(dve_chain, 1)
                            ch.n += 1
                        dve.wait_ge(dve_chain, ch.n)
                        ch.link(nc.vector.tensor_copy(gidf[:, :, :], gidx[:, :, 0:2]))
                        for j in range(2):
                            ins = nc.vector.tensor_tensor(gm[:, j, :, :], iota_e[:, :].unsqueeze(1).to_broadcast([P, NT, E]),
                                                          gidf[:, :, j:j + 1].to_broadcast([P, NT, E]), ALU.is_equal)
                            ins.then_inc(dve_chain, 1)
                            ch.n += 1
                        dve.wait_ge(dve_chain, ch.n)
                        ch.link(nc.vector.tensor_tensor(gm[:, 0, :, :], gm[:, 0, :, :], gm[:, 1, :, :], ALU.add))
                        mul = nc.vector.tensor_tensor(gate[:, :, :], glog[:, :, :], gm[:, 0, :, :], ALU.mult)
                        if n != 1:
                            ch.link(mul)
                            ch.link(nc.vector.tensor_reduce(gs[:, :], gate[:, :, :], AX_X, ALU.add))
                            ch.link(nc.vector.reciprocal(gr[:, :], gs[:, :]))
                            mul = nc.vector.tensor_tensor(gate[:, :, :], gate[:, :, :],
                                                          gr[:, :].unsqueeze(2).to_broadcast([P, NT, E]), ALU.mult)
                        mul.then_inc(g["done"], 1)
                        dve.wait_ge(g["turn"], n + 1)
                        nc.vector.tensor_copy(gT[:, :], ps[0:E, 6, :]).then_inc(g["gT"], 1)

                    def add_ffn(n):
                        dve.wait_ge(f["yt"], n + 1)
                        add_x(nc.vector.tensor_tensor(x[:, :, :], x[:, :, :], bnk(4).rearrange("p (t d) -> p t d", t=NT), ALU.add))

                    def project_rows(i, bias):
                        dve.wait_ge(a["y"], i + NT)
                        for t in range(NT):
                            y = ps[:, 7, t * P:t * P + P]
                            if bias is not None:
                                ch.link(nc.vector.tensor_tensor(x[:, t, :], x[:, t, :], bias[:, :], ALU.add))
                            add_x(nc.vector.tensor_tensor(x[:, t, :], x[:, t, :], y, ALU.add))

                    def keys_values(i):
                        w = wa[i]
                        dve.wait_ge(a["proj"], 2 * i + 2)
                        if i == 0:
                            dve.wait_ge(W["misc"], wcount["misc"])
                            ch.link(nc.vector.tensor_scalar(kTx, ps[:, 1, 0:S2], bk1[:, :], None, ALU.add))
                            nc.vector.tensor_tensor(vx, ps[0:S2, 1, P:2 * P], bv1[0:S2, :], ALU.add).then_inc(a["kv"], 1)
                        else:
                            ch.link(nc.vector.tensor_copy(kTx, ps[:, 1, 0:S2]))
                            nc.vector.tensor_copy(vx, ps[0:S2, 1, P:2 * P]).then_inc(a["kv"], 1)
                        nc.vector.tensor_tensor(kbd, kTx.unsqueeze(1).to_broadcast([P, H, S2]),
                                                headmask[:, :].unsqueeze(2).to_broadcast([P, H, S2]), ALU.mult)\
                            .then_inc(a["kv"], 1)

                    def offsets():
                        o3 = ofq
                        dve.wait_ge(a["off"], 1)
                        pso = ps[:, 6, 0:NT * H * NK].rearrange("p (t n) -> p t n", t=NT)
                        bc = lambda v: v.unsqueeze(1).to_broadcast([P, NT, H * NK])
                        ch.link(nc.vector.tensor_tensor(o3, pso, bc(boff[:, :]), ALU.add))
                        ch.link(nc.vector.tensor_tensor(o3, o3, bc(ref_k[:, :, :].rearrange("p h k -> p (h k)")), ALU.add))
                        ch.link(nc.vector.tensor_tensor(o3, o3, loc[:, :].unsqueeze(2).to_broadcast([P, NT, H * NK]), ALU.add))
                        m, rm = lenb[:, 0:1], lenb[:, 1:2]
                        ch.link(nc.vector.tensor_scalar(offs, o3, rm, None, ALU.mult))
                        ch.link(nc.vector.tensor_copy(off_i, offs))
                        tmp = hat.rearrange("p a b c -> p (a b c)")[:, 0:NT * H * NK].rearrange("p (t n) -> p t n", t=NT)
                        ch.link(nc.vector.tensor_copy(tmp, off_i))
                        ch.link(nc.vector.tensor_tensor(offs, tmp, offs, ALU.is_gt))
                        ch.link(nc.vector.tensor_tensor(tmp, tmp, offs, ALU.subtract))
                        ch.link(nc.vector.tensor_scalar(tmp, tmp, m, None, ALU.mult))
                        ch.link(nc.vector.tensor_tensor(o3, o3, tmp, ALU.subtract))
                        ch.link(nc.vector.tensor_scalar(offs, o3, rm, 0.0, ALU.mult, ALU.is_lt))
                        ch.link(nc.vector.tensor_scalar(offs, offs, m, None, ALU.mult))
                        ch.link(nc.vector.tensor_tensor(o3, o3, offs, ALU.add))
                        ch.link(nc.vector.tensor_scalar(tmp, o3, m, rm, ALU.subtract, ALU.mult))
                        ch.link(nc.vector.tensor_scalar(tmp, tmp, 0.0, m, ALU.is_ge, ALU.mult))
                        ch.link(nc.vector.tensor_tensor(o3, o3, tmp, ALU.subtract))
                        ch.link(nc.vector.tensor_scalar(o3, o3, 1.0 / (S2 - 1), 2.0, ALU.mult, ALU.mult))
                        ch.link(nc.vector.tensor_scalar(o3, o3, -1.0, 1.0, ALU.add, ALU.add))
                        ch.link(nc.vector.tensor_scalar(o3, o3, float(S2), -1.0, ALU.mult, ALU.add))
                        ch.link(nc.vector.tensor_scalar(o3, o3, 0.5, None, ALU.mult))

                    def sampled(t):
                        for hg in range(H // HG):
                            u = t * (H // HG) + hg
                            hs = slice(hg * HG, hg * HG + HG)
                            ixv = ofq[:, t, hg * HG * NK:(hg + 1) * HG * NK]
                            h2 = hat.rearrange("p a b c -> p (a b) c")
                            nc.vector.tensor_tensor(h2, iota_j[:, :].unsqueeze(1).to_broadcast([P, HG * NK, S2]),
                                                    ixv.unsqueeze(2).to_broadcast([P, HG * NK, S2]), ALU.subtract)\
                                .then_inc(a["hat"], 1)
                            dve.wait_ge(a["hatok"], u + 1)
                            if u % (H // HG) == 0:
                                dve.wait_ge(a["sub"], t + 1)
                            ch.link(nc.vector.tensor_tensor(hpr, hat, sx[:, hs, :].unsqueeze(2).to_broadcast([P, HG, NK, S2]),
                                                            ALU.mult))
                            ch.link(nc.vector.tensor_reduce(psc[:, hs, :], hpr, AX_X, ALU.add))
                            ch.link(nc.vector.tensor_reduce(pmx[:, hs], psc[:, hs, :], AX_X, ALU.max))
                            nc.vector.tensor_tensor(psc[:, hs, :], psc[:, hs, :], pmx[:, hs].unsqueeze(2).to_broadcast([P, HG, NK]),
                                                    ALU.subtract).then_inc(a["softk"], 1)
                            dve.wait_ge(a["softe"], u + 1)
                            ch.link(nc.vector.tensor_reduce(pmx[:, hs], psc[:, hs, :], AX_X, ALU.add))
                            ch.link(nc.vector.reciprocal(pmx[:, hs], pmx[:, hs]))
                            ch.link(nc.vector.tensor_scalar(pmx[:, hs], pmx[:, hs], 0.5, None, ALU.mult))
                            ch.link(nc.vector.tensor_tensor(psc[:, hs, :], psc[:, hs, :],
                                                            pmx[:, hs].unsqueeze(2).to_broadcast([P, HG, NK]), ALU.mult))
                            ch.link(nc.vector.tensor_tensor(hpr, hat, psc[:, hs, :].unsqueeze(3).to_broadcast([P, HG, NK, S2]),
                                                            ALU.mult))
                            ins = nc.vector.tensor_reduce(ax[:, hs, :], hpr.rearrange("p h k j -> p h j k"), AX_X, ALU.add)
                            if hg == H // HG - 1:
                                ins.then_inc(a["exp"], 1)
                            else:
                                ch.link(ins)

                    def soft(i, t):
                        n = NT * i + t
                        dve.wait_ge(a["s"], n + 1)
                        for j, (h0, h1) in enumerate(HS):
                            s3 = ps[:, 2 + j, 0:(h1 - h0) * S2].rearrange("p (h s) -> p h s", s=S2)
                            ch.link(nc.vector.tensor_reduce(smx[:, h0:h1], s3, AX_X, ALU.max))
                            if j == 0 and t >= 1:
                                dve.wait_ge(a["turn"], 4 * n)
                            ins = nc.vector.tensor_tensor(sx[:, h0:h1, :], s3, smx[:, h0:h1].unsqueeze(2)
                                                          .to_broadcast([P, h1 - h0, S2]), ALU.subtract)
                            if j == 2:
                                ins.then_inc(a["sub"], 1)
                        dve.wait_ge(a["exp"], n + 1)
                        ch.link(nc.vector.tensor_reduce(ssm, sx, AX_X, ALU.add))
                        ch.link(nc.vector.reciprocal(srs, ssm))

                    def attend(i, t):
                        n = NT * i + t
                        for q in (1, 3):
                            dve.wait_ge(a["turn"], 4 * n + q + 1)
                            nc.vector.tensor_copy(aT[:, 4 * q:4 * q + 4, :], ps[0:S2, 5 + q % 2, :]
                                                  .rearrange("p (h c) -> p h c", h=4)).then_inc(a["aT"], 1)
                        dve.wait_ge(a["o"], n + 1)
                        o3 = ps[:, 0, 0:P].rearrange("p (h d) -> p h d", h=H)
                        x3 = ox.rearrange("p (h d) -> p h d", h=H)
                        if i == 0:
                            nc.vector.tensor_copy(x3, o3).then_inc(a["osb"], 1)
                        else:
                            nc.vector.tensor_tensor(x3, o3, srs.unsqueeze(2).to_broadcast([P, H, HD]), ALU.mult)\
                                .then_inc(a["osb"], 1)

                    def attention(i):
                        keys_values(i)
                        if i == 0:
                            offsets()
                        for t in range(NT):
                            if i == 0:
                                sampled(t)
                            else:
                                soft(i, t)
                            attend(i, t)
                        project_rows(NT * i, bo1 if i == 0 else bo3 if i == 2 else None)

                    def product_keys():
                        for t in range(NT):
                            dve.wait_ge(k["sim"], t + 1)
                            s3 = ps[:, t % 2, :].rearrange("p (c n) -> p c n", c=16)
                            bc = lambda v: v.unsqueeze(2).to_broadcast([P, 16, PKN])
                            ch.link(nc.vector.tensor_reduce(kmax, s3, AX_X, ALU.max))
                            ch.link(nc.vector.tensor_tensor(eqk, s3, bc(kmax), ALU.is_ge))
                            ch.link(nc.vector.tensor_tensor(eqk, eqk, iota_k[:, :].unsqueeze(1).to_broadcast([P, 16, PKN]),
                                                            ALU.mult))
                            ch.link(nc.vector.tensor_reduce(kidx, eqk, AX_X, ALU.min))
                            ch.link(nc.vector.tensor_scalar(eid, kidx[:, 0:8], float(PKN), float(PKN * PKN + PKN), ALU.mult,
                                                            ALU.add))
                            ch.link(nc.vector.tensor_tensor(eid, eid, kidx[:, 8:16], ALU.add))
                            nc.vector.tensor_copy(eidi, eid).then_inc(k["idx"], 1)
                            ch.link(nc.vector.tensor_tensor(esc, kmax[:, 0:8], kmax[:, 8:16], ALU.add))
                            ch.link(nc.vector.tensor_scalar(esc, esc, 0.0, None, ALU.max))
                            dve.wait_ge(rows_in, b * (16 * PKH * NT) + 16 * PKH * (t + 1))
                            for h in range(PKH):
                                ins = nc.vector.tensor_tensor_reduce(junk, rows_g[:, h, 0:D], xn[:, t, :], 1.0, 0.0, ALU.mult,
                                                                     ALU.add, dots[:, h:h + 1])
                                if h < PKH - 1:
                                    ch.link(ins)
                                else:
                                    ins.then_inc(k["dot"], 1)
                            dve.wait_ge(k["act"], t + 1)
                            ch.link(nc.vector.tensor_tensor(hv, hv, esc, ALU.mult))
                            for h in range(PKH):
                                ins = nc.vector.scalar_tensor_tensor(x[:, t, :], rows_g[:, h, D:2 * D], hv[:, h:h + 1],
                                                                     x[:, t, :], ALU.mult, ALU.add)
                                if h < PKH - 1:
                                    ch.link(ins)
                                else:
                                    add_x(ins)
                                    dve.wait_ge(x_new, nx[0])

                    dve.wait_ge(i0["oT"], 1)
                    dve.wait_ge(i0["y"], 1)
                    y = bnk(1).rearrange("p (t d) -> p t d", t=NT)
                    ch.link(nc.vector.tensor_tensor(x[:, :, :], x[:, :, :], y, ALU.add))
                    add_x(nc.vector.tensor_tensor(x[:, :, :], x[:, :, :], pb0[:, :].unsqueeze(1).to_broadcast([P, NT, D]), ALU.add))

                    if stop_after >= 1:
                        norm(0)
                        gates(0)
                        for u in range(4 * (E + 1)):
                            if u >= 4:
                                dve.wait_ge(f["act"], u + 1)
                                dve.wait_ge(f["gb"], u // 4)
                                nc.vector.tensor_tensor(hb[:, u % 4, :], hb[:, u % 4, :], ps[:, 5 + u // 4 % 2, :], ALU.mult)\
                                    .then_inc(f["hg"], 1)
                        add_ffn(0)
                    if stop_after >= 2:
                        norm(1)
                        attention(0)
                    if stop_after >= 3:
                        norm(2)
                        gates(1)
                        for e in range(E):
                            dve.wait_ge(f["gb"], E + e + 1)
                            if e >= 2:
                                dve.wait_ge(f["up"], U0 + 2 * 3 * (e - 1))
                            nc.vector.tensor_tensor(xs[:, e % 2, :], xnT[:, :], ps[:, 5 + e % 2, :], ALU.mult).then_inc(f["xs"], 1)
                            for c in range(3):
                                u = 3 * e + c
                                n = CH1[c][1]
                                dve.wait_ge(f["act"], U0 + u + 1)
                                dve.wait_ge(f["up"], U0 + 2 * u + 2)
                                nc.vector.tensor_tensor(hb[0:n, u % 4, :], hb[0:n, u % 4, :], ps[0:n, 2 + u % 2, :], ALU.mult)\
                                    .then_inc(f["hg"], 1)
                        add_ffn(1)
                    if stop_after >= 4:
                        norm(3)
                        attention(1)
                    if stop_after >= 5:
                        norm(4)
                        gates(2)
                        for u in range(4 * E):
                            dve.wait_ge(f["act"], U0 + 3 * E + u + 1)
                            dve.wait_ge(f["gb"], 2 * E + u // 4 + 1)
                            nc.vector.tensor_tensor(hb[:, u % 4, :], hb[:, u % 4, :], ps[:, 5 + u // 4 % 2, :], ALU.mult)\
                                .then_inc(f["hg"], 1)
                        add_ffn(2)
                    if stop_after >= 6:
                        norm(5)
                        attention(2)
                    if stop_after >= 7:
                        norm(6)
                        product_keys()
                    assert nx[0] == NX, nx[0]

                @block.tensor
                def _(pe):
                    def norm(n):
                        norm_tensor(nc, pe, n, xn, ident, bnk(0), ln_xn, ln_turned)
                        pe.wait_ge(ln_xnT, n + 1)

                    def gates(n):
                        for t in range(NT):
                            mm = nc.tensor.matmul(ps[:, 7, t * E:t * E + E], xnT[:, t * P:t * P + P], gw[:, n, :],
                                                  start=True, stop=True)
                        mm.then_inc(g["log"], 1)

                    def gates_turned(n):
                        pe.wait_ge(g["done"], n + 1)
                        for t in range(NT):
                            mm = nc.tensor.transpose(ps[0:E, 6, t * P:t * P + P], gate[:, t, :], ident[:, :])
                        mm.then_inc(g["turn"], 1)

                    def gate_rows(n, e):
                        pe.wait_ge(g["gT"], n + 1)
                        if e >= 2:
                            if n == 1:
                                pe.wait_ge(f["xs"], e - 1)
                            else:
                                pe.wait_ge(f["hg"], (0, 0, 4 * E + 3 * E)[n] + 4 * (e - 1))
                        for t in range(NT):
                            mm = nc.tensor.transpose(ps[:, 5 + e % 2 if n else 5 + (e + 1) % 2, t * P:t * P + P],
                                                     gate[:, t, e:e + 1].to_broadcast([P, P]), ident[:, :])
                        mm.then_inc(f["gb"], 1)

                    def ffn(n, ups, w2, act0, hg0, down0, units, shared):
                        def down(v):
                            if shared and v < 4:
                                pe.wait_ge(f["act"], act0 + v + 1)
                            else:
                                pe.wait_ge(f["hg"], hg0 + v + 1 - (4 if shared else 0))
                            nc.tensor.matmul(bnk(7), w2(v), hb[0:w2(v).shape[0], v % 4, :], start=v == 0, stop=False)\
                                .then_inc(f["down"], 1)

                        for u in range(units):
                            ups(u)
                            if u >= 2:
                                down(u - 2)
                        down(units - 2)
                        down(units - 1)

                    def ffn_end(n, bias):
                        nc.tensor.matmul(bnk(7), bias, gT[:, :], start=False, stop=True).then_inc(f["y"], 1)

                    def ffn_turn(n):
                        pe.wait_ge(f["ysb"], n + 1)
                        for t in range(NT):
                            mm = nc.tensor.transpose(ps[:, 4, t * P:t * P + P], yT[:, t * P:t * P + P], ident[:, :])
                        mm.then_inc(f["yt"], 1)

                    def attention(i):
                        w = wa[i]
                        if i == 0:
                            pe.wait_ge(W["misc"], wcount["misc"])
                        nc.tensor.matmul(bnk(0), w["q"][:, :], xnT[:, :], start=True, stop=True).then_inc(a["proj"], 1)
                        nc.tensor.matmul(ps[:, 1, 0:S2], w["k"][:, :], ctxTb[:, :], start=True, stop=True)
                        nc.tensor.matmul(ps[0:S2, 1, P:2 * P], ctxTb[:, :], w["v"][:, :], start=True, stop=True)\
                            .then_inc(a["proj"], 1)
                        pe.wait_ge(a["q"], i + 1)
                        if i == 0:
                            for t in range(NT):
                                mm = nc.tensor.matmul(ps[:, 6, t * H * NK:(t + 1) * H * NK], qTx[:, t * P:t * P + P], woff[:, :],
                                                      start=True, stop=True)
                            mm.then_inc(a["off"], 1)
                        pe.wait_ge(a["kv"], 2 * i + 2)

                        def scores(t):
                            n = NT * i + t
                            if t >= 1:
                                pe.wait_ge(a["sub"], n)
                            for j, (h0, h1) in enumerate(HS):
                                mm = nc.tensor.matmul(ps[:, 2 + j, 0:(h1 - h0) * S2], qTx[:, t * P:t * P + P],
                                                      kbd[:, h0:h1, :].rearrange("p h s -> p (h s)"), start=True, stop=True)
                            mm.then_inc(a["s"], 1)

                        def weights(t):
                            n = NT * i + t
                            pe.wait_ge(a["exp"], n + 1)
                            src = ax if i == 0 else sx
                            for q in range(4):
                                if 4 * n + q >= 2:
                                    if q % 2 == 0:
                                        pe.wait_ge(a["aT_even"], (4 * n + q) // 2)
                                    else:
                                        pe.wait_ge(a["aT"], (4 * n + q - 1) // 2)
                                for hh in range(4):
                                    mm = nc.tensor.transpose(ps[0:S2, 5 + q % 2, hh * P:hh * P + P], src[:, 4 * q + hh, :],
                                                             ident[:, :])
                                mm.then_inc(a["turn"], 1)
                            pe.wait_ge(a["aT_even"], 2 * n + 2)
                            pe.wait_ge(a["aT"], 2 * n + 2)
                            for hh in range(H):
                                mm = nc.tensor.matmul(ps[:, 0, hh * HD:hh * HD + HD], aT[:, hh, :], vx[:, hh * HD:hh * HD + HD],
                                                      start=True, stop=True)
                            mm.then_inc(a["o"], 1)
                            pe.wait_ge(a["osb"], n + 1)
                            nc.tensor.transpose(ps[:, 1, 0:P], ox, ident[:, :]).then_inc(a["ot"], 1)
                            pe.wait_ge(a["otsb"], n + 1)
                            nc.tensor.matmul(ps[:, 7, t * P:t * P + P], oTx, w["o"][:, :], start=True, stop=True)\
                                .then_inc(a["y"], 1)

                        for t in range(NT):
                            scores(t)
                            weights(t)

                    for t in range(RT):
                        n = min(R, T - R * t)
                        mm = nc.tensor.transpose(ps[:, 0, R * t:R * t + n], at_out[0:n, t, :], ident[0:n, 0:n])
                    mm.then_inc(i0["turn"], 1)
                    pe.wait_ge(i0["oT"], 1)
                    for t in range(NT):
                        mm = nc.tensor.matmul(ps[:, 1, t * P:t * P + P], oT[:, t * P:t * P + P], wp0[:, :], start=True, stop=True)
                    mm.then_inc(i0["y"], 1)

                    def ups0(u):
                        e, c = u // 4, u % 4
                        if c == 2 and e < E:
                            if e == 0:
                                gates_turned(0)
                            gate_rows(0, e)
                        if u >= 3:
                            pe.wait_ge(f["act"], u - 2)
                        nc.tensor.matmul(bnk(1 + u % 3), w1_0[:, e, c * P:c * P + P], xnT[:, :], start=True, stop=True)\
                            .then_inc(f["up"], 1)

                    def ups1(u):
                        e, c = u // 3, u % 3
                        lo, n = CH1[c]
                        if u == 0:
                            gate_rows(1, 0)
                        if c == 1 and e < E - 1:
                            gate_rows(1, e + 1)
                        if c == 0:
                            pe.wait_ge(f["xs"], e + 1)
                        if u >= 2:
                            pe.wait_ge(f["act"], U0 + u - 1)
                            pe.wait_ge(f["hg"], 4 * E + u - 1)
                        nc.tensor.matmul(ps[0:n, u % 2, :], w1_1[:, e, lo:lo + n], xs[:, e % 2, :], start=True, stop=True)\
                            .then_inc(f["up"], 1)
                        nc.tensor.matmul(ps[0:n, 2 + u % 2, :], w3_1[:, e, lo:lo + n], xs[:, e % 2, :], start=True, stop=True)\
                            .then_inc(f["up"], 1)

                    def ups2(u):
                        e, c = u // 4, u % 4
                        if u == 0:
                            gate_rows(2, 0)
                        if c == 2 and e < E - 1:
                            gate_rows(2, e + 1)
                        if u >= 3:
                            pe.wait_ge(f["act"], U0 + 3 * E + u - 2)
                        nc.tensor.matmul(bnk(1 + u % 3), w1_2[:, e, c * P:c * P + P], xnT[:, :], start=True, stop=True)\
                            .then_inc(f["up"], 1)

                    if stop_after >= 1:
                        norm(0)
                        gates(0)
                        ffn(0, ups0, lambda v: w2_0[:, v // 4, v % 4, :], 0, 0, 0, 4 * (E + 1), True)
                        ffn_end(0, b2_0[:, :])
                        ffn_turn(0)
                    if stop_after >= 2:
                        norm(1)
                        attention(0)
                    if stop_after >= 3:
                        norm(2)
                        gates(1)
                        gates_turned(1)
                        ffn(1, ups1, lambda v: w2_1[0:CH1[v % 3][1], v // 3, v % 3, :], U0, 4 * E, 0, 3 * E, False)
                        nc.tensor.matmul(bnk(7), b2_2[:, :], zero8[:, :], start=False, stop=True).then_inc(f["y"], 1)
                        ffn_turn(1)
                    if stop_after >= 4:
                        norm(3)
                        attention(1)
                    if stop_after >= 5:
                        norm(4)
                        gates(2)
                        gates_turned(2)
                        ffn(2, ups2, lambda v: w2_2[:, v // 4, v % 4, :], U0 + 3 * E, 4 * E + 3 * E, 0, 4 * E, False)
                        ffn_end(2, b2_2[:, :])
                        ffn_turn(2)
                    if stop_after >= 6:
                        norm(5)
                        attention(2)
                    if stop_after >= 7:
                        norm(6)
                        for t in range(NT):
                            if t >= 2:
                                pe.wait_ge(k["idx"], t - 1)
                            nc.tensor.matmul(bnk(t % 2), xnT[:, t * P:t * P + P], wcomb[:, :], start=True, stop=True)\
                                .then_inc(k["sim"], 1)

                @block.scalar
                def _(act):
                    norm = lambda n: norm_scalar(nc, act, n, xnT, bnk(0), ln_turned, ln_xnT)

                    def gates(n):
                        act.wait_ge(g["max"], n + 1)
                        nc.scalar.activation(glog[:, :, :], glog[:, :, :], ACT.Exp).then_inc(g["exp"], 1)

                    def ffn_out(n, bias):
                        act.wait_ge(f["y"], n + 1)
                        if bias is None:
                            nc.scalar.copy(yT, bnk(7)).then_inc(f["ysb"], 1)
                        else:
                            nc.scalar.activation(yT, bnk(7), ACT.Identity, bias=bias).then_inc(f["ysb"], 1)

                    def attention(i):
                        act.wait_ge(a["proj"], 2 * i + 1)
                        if i == 0:
                            nc.scalar.activation(qTx, bnk(0), ACT.Identity, bias=bq1[:, :]).then_inc(a["q"], 1)
                        else:
                            nc.scalar.copy(qTx, bnk(0)).then_inc(a["q"], 1)
                        for t in range(NT):
                            n = NT * i + t
                            if i == 0:
                                act.wait_ge(a["s"], n + 1)
                                if t >= 1:
                                    act.wait_ge(a["exp"], t)
                                for j, (h0, h1) in enumerate(HS):
                                    ins = nc.scalar.mul(sx[:, h0:h1, :], ps[:, 2 + j, 0:(h1 - h0) * S2]
                                                        .rearrange("p (h s) -> p h s", s=S2), 0.5 * SCALE)
                                ins.then_inc(a["sub"], 1)
                                for hg in range(H // HG):
                                    u = t * (H // HG) + hg
                                    act.wait_ge(a["hat"], u + 1)
                                    nc.scalar.activation(hat, hat, ACT.Abs).then_inc(a["abs"], 1)
                                    act.wait_ge(a["abs"], u + 1)
                                    nc.scalar.activation(hat, hat, ACT.Relu, bias=1.0, scale=-1.0).then_inc(a["hatok"], 1)
                                    act.wait_ge(a["softk"], u + 1)
                                    nc.scalar.activation(psc[:, hg * HG:hg * HG + HG, :], psc[:, hg * HG:hg * HG + HG, :], ACT.Exp)\
                                        .then_inc(a["softe"], 1)
                            else:
                                act.wait_ge(a["sub"], n + 1)
                                nc.scalar.activation(sx, sx, ACT.Exp, scale=SCALE).then_inc(a["exp"], 1)
                            for q in (0, 2):
                                act.wait_ge(a["turn"], 4 * n + q + 1)
                                nc.scalar.copy(aT[:, 4 * q:4 * q + 4, :], ps[0:S2, 5 + q % 2, :]
                                               .rearrange("p (h c) -> p h c", h=4)).then_inc(a["aT_even"], 1)
                            act.wait_ge(a["ot"], n + 1)
                            nc.scalar.copy(oTx, ps[:, 1, 0:P]).then_inc(a["otsb"], 1)

                    act.wait_ge(i0["turn"], 1)
                    nc.scalar.copy(oT, bnk(0)).then_inc(i0["oT"], 1)
                    if stop_after >= 1:
                        norm(0)
                        gates(0)
                        act.wait_ge(W["ffn0"], wcount["ffn0"])
                        for u in range(4 * (E + 1)):
                            act.wait_ge(f["up"], u + 1)
                            if u >= 4:
                                act.wait_ge(f["down"], u - 3)
                            nc.scalar.activation(hb[:, u % 4, :], bnk(1 + u % 3), ACT.Gelu_apprx_tanh,
                                                 bias=b1_0[:, u // 4, u % 4:u % 4 + 1]).then_inc(f["act"], 1)
                        ffn_out(0, bs0[:, :])
                    if stop_after >= 2:
                        norm(1)
                        attention(0)
                    if stop_after >= 3:
                        norm(2)
                        gates(1)
                        for u in range(3 * E):
                            n = CH1[u % 3][1]
                            act.wait_ge(f["up"], U0 + 2 * u + 1)
                            if u >= 4:
                                act.wait_ge(f["down"], U0 + u - 3)
                            nc.scalar.activation(hb[0:n, u % 4, :], ps[0:n, u % 2, :], ACT.Silu).then_inc(f["act"], 1)
                        ffn_out(1, None)
                    if stop_after >= 4:
                        norm(3)
                        attention(1)
                    if stop_after >= 5:
                        norm(4)
                        gates(2)
                        for u in range(4 * E):
                            act.wait_ge(f["up"], U0 + 6 * E + u + 1)
                            if u >= 4:
                                act.wait_ge(f["down"], U0 + 3 * E + u - 3)
                            nc.scalar.activation(hb[:, u % 4, :], bnk(1 + u % 3), ACT.Relu,
                                                 bias=b1_2[:, u // 4, u % 4:u % 4 + 1]).then_inc(f["act"], 1)
                        ffn_out(2, None)
                    if stop_after >= 6:
                        norm(5)
                        attention(2)
                    if stop_after >= 7:
                        norm(6)
                        for t in range(NT):
                            act.wait_ge(k["dot"], t + 1)
                            nc.scalar.activation(hv, dots, ACT.Gelu).then_inc(k["act"], 1)
            clear_sems(loop_sems)


def norm_vector(nc, dve, n, x, xn, stats, mv, rstd, ln_stats, ln_mean, ln_rstd, ln_xn):
    for t in range(NT):
        nc.vector.bn_stats(stats[:, t, :], x[:, t, :]).then_inc(ln_stats, 1)
    dve.wait_ge(ln_stats, NT * (n + 1))
    for t in range(NT):
        nc.vector.bn_aggr(mv[:, t, :], stats[:, t, :]).then_inc(ln_mean, 1)
    dve.wait_ge(ln_mean, NT * (n + 1))
    dve.wait_ge(ln_rstd, n + 1)
    for t in range(NT):
        nc.vector.tensor_scalar(xn[:, t, :], x[:, t, :], mv[:, t, 0:1], rstd[:, t:t + 1],
                                ALU.subtract, ALU.mult).then_inc(ln_xn, 1)


def norm_pool(nc, pool, ch, n, ln_mean, ln_rstd, mv, rstd, neghalf):
    pool.wait_ge(ln_mean, NT * (n + 1))
    ch.link(nc.gpsimd.tensor_scalar(rstd[:, :], mv[:, :, 1], EPS, None, ALU.add))
    nc.gpsimd.tensor_tensor(rstd[:, :], rstd[:, :], neghalf[:, 0:NT], ALU.pow).then_inc(ln_rstd, 1)


def norm_tensor(nc, pe, n, xn, ident, bank, ln_xn, ln_turned):
    for t in range(NT):
        pe.wait_ge(ln_xn, NT * n + t + 1)
        mm = nc.tensor.transpose(bank[:, t * P:t * P + P], xn[:, t, :], ident[:, :])
    mm.then_inc(ln_turned, 1)


def norm_scalar(nc, act, n, xnT, bank, ln_turned, ln_xnT):
    act.wait_ge(ln_turned, n + 1)
    nc.scalar.copy(xnT[:, :], bank).then_inc(ln_xnT, 1)


def kernel(**inputs):
    import numpy as _np
    import concourse.bacc as _bacc
    from concourse import mybir as _mybir
    from concourse.bass_utils import run_bass_kernel_spmd as _run

    a = {k: _np.asarray(v) for k, v in inputs.items()}
    c = _np.ascontiguousarray

    def cols(v):
        return v.reshape(v.shape[0], -1, P).transpose(2, 0, 1)

    L0, F0, L1, F1, L2, F2, L3, F3 = ("L0_xattn_", "L0_ffn_", "L1_xattn_", "L1_ffn_", "L2_xattn_", "L2_ffn_",
                                      "L3_xattn_", "L3_ffn_")
    arrays = {
        "x": a["x"], "ctx_1024": a["ctx_1024"], "mask": a["mask_SxS_bc0"], "mask2": a["mask_BxS2_if0"],
        "Wq0": a[L0 + "Wq"], "Wk0": a[L0 + "Wk"], "Wv0": a[L0 + "Wv"], "Wp0": a[L0 + "proj_W"], "bp0": a[L0 + "proj_b"],
        "hist_W": a[L0 + "hist_W"], "hist_b": a[L0 + "hist_b"], "hist_ln_g": a[L0 + "hist_ln_g"],
        "hist_ln_b": a[L0 + "hist_ln_b"], "ctx_W1": a[L0 + "ctx_W1"], "ctx_b1": a[L0 + "ctx_b1"],
        "ctx_W2": a[L0 + "ctx_W2"].reshape(-1), "ctx_b2": a[L0 + "ctx_b2"], "kg_W1": a[L0 + "kg_W1"],
        "kg_b1": a[L0 + "kg_b1"], "kg_ln_g": a[L0 + "kg_ln_g"], "kg_ln_b": a[L0 + "kg_ln_b"],
        "kg_W2": a[L0 + "kg_W2"], "kg_b2": a[L0 + "kg_b2"],
        "Wfc_s": a[F0 + "Wfc_s"], "Wproj_s": a[F0 + "Wproj_s"], "bproj_s": a[F0 + "bproj_s"],
        "Wr0": a[F0 + "Wr"], "Wfc": a[F0 + "Wfc"], "bfc": cols(_np.concatenate([a[F0 + "bfc_s"][None], a[F0 + "bfc"]])), "Wproj": a[F0 + "Wproj"], "bproj": a[F0 + "bproj"],
        "wq1": a[L1 + "Wq"].T, "wk1": a[L1 + "Wk"].T, "wv1": a[L1 + "Wv"].T, "wo1": a[L1 + "Wo"].T,
        "bq1": a[L1 + "bq"], "bk1": a[L1 + "bk"], "bv1": a[L1 + "bv"], "bo1": a[L1 + "bo"],
        "Woff": a[L1 + "Woff"].T, "boff": a[L1 + "boff"],
        "Wr1": a[F1 + "gate_w"].T, "eb1": a[F1 + "expert_bias"], "w1": a[F1 + "w1"], "w2": a[F1 + "w2"], "w3": a[F1 + "w3"],
        "wq2": a[L2 + "wq"].T, "wk2": a[L2 + "wk"].T, "wv2": a[L2 + "wv"].T, "wo2": a[L2 + "wo"].T,
        "W1": a[F2 + "W1"], "b1": cols(a[F2 + "b1"]), "W2": a[F2 + "W2"], "b2": a[F2 + "b2"], "Wr2": a[F2 + "Wr"], "br2": a[F2 + "br"],
        "wq3": a[L3 + "W_qkv"][:, 0:D], "wk3": a[L3 + "W_qkv"][:, D:2 * D], "wv3": a[L3 + "W_qkv"][:, 2 * D:],
        "wo3": a[L3 + "W_proj"], "bo3": a[L3 + "b_proj"],
        "w_qT": a[F3 + "w_q"].T,
        "keysT": a[F3 + "keys"].transpose(0, 2, 3, 1),
        "w_ud": _np.concatenate([a[F3 + "w_down"], a[F3 + "w_up"]], axis=1),
    }
    nc = _bacc.Bacc("TRN2", target_bir_lowering=False, num_devices=1)
    feed, A = {}, {}
    for name, v in arrays.items():
        v = c(v)
        feed[f"in_{name}"] = v
        A[name] = nc.dram_tensor(f"in_{name}", v.shape, _mybir.dt.from_np(v.dtype), kind="ExternalInput").ap()
    out = nc.dram_tensor("out", (B, T, D), _mybir.dt.float32, kind="ExternalOutput").ap()
    build(nc, A, out, STOP)
    return _run(nc, [feed], core_ids=[0]).results[0]["out"]
```

```python
from contextlib import ExitStack

import numpy as np

import concourse.bass as bass
from concourse import mybir

ALU = mybir.AluOpType
ACT = mybir.ActivationFunctionType
F32 = mybir.dt.float32
F32R = mybir.dt.float32r
BF16 = mybir.dt.bfloat16
U32 = mybir.dt.uint32
I32 = mybir.dt.int32
U8 = mybir.dt.uint8
AX_X = mybir.AxisListType.X

P = 128
B, T, D = 4, 512, 128
NT = T // P
S2 = 77
H, HD = 16, 8
EPS = 1e-5
SCALE = HD ** -0.5
NK = 5
E = 8
HID = 512
HID1 = 352
CH1 = [(0, 128), (128, 128), (256, 96)]
R = 103
RT = -(-T // R)
RI = R + 2
NEG = -1e30
ARENA = 12540
STOP = 99
PKH, PKN, PKD = 8, 32, 64


class Chain:

    def __init__(self, eng, sem):
        self.eng, self.sem, self.n = eng, sem, 0

    def link(self, ins):
        self.n += 1
        ins.then_inc(self.sem, 1)
        self.eng.wait_ge(self.sem, self.n)


def build(nc, A, out, stop_after=99):
    with ExitStack() as ctx:
        used = [0]

        def sb(name, shape, dt=F32):
            used[0] += int(np.prod(shape[1:])) * (1 if dt == U8 else 4)
            return ctx.enter_context(nc.sbuf_tensor(name, shape, dt))

        def sem(name):
            return ctx.enter_context(nc.semaphore(name))

        ps = ctx.enter_context(nc.psum_tensor("ps", [P, 8, 512], F32))

        ident = sb("ident", [P, P])
        shift = sb("shift", [P, 3, P])
        headmask = sb("headmask", [P, H])
        iota_j = sb("iota_j", [P, S2])
        iota_e = sb("iota_e", [P, E])
        iota_k = sb("iota_k", [P, PKN])
        neghalf = sb("neghalf", [P, 8])
        ref_k = sb("ref_k", [P, H, NK])
        loc = sb("loc", [P, NT])
        ident_bf = sb("ident_bf", [P, P], BF16)
        quadmask = sb("quadmask", [P, 4])
        row24 = sb("row24", [P, 1])
        first_row = sb("first_row", [P, 1])
        far_q = sb("far_q", [P, P + 2], BF16)
        far_k = sb("far_k", [P, P + 2], BF16)
        wcol = sb("wcol", [P, 12, B])
        wq_rows = sb("wq_rows", [P, 4, 3, P]); wk_rows = sb("wk_rows", [P, 4, P])
        q3r = sb("q3r", [P, 2, T], F32R)
        kmr = sb("kmr", [P, 4, T], F32R)

        wqkv0 = sb("wqkv0", [P, 3 * D]); wp0 = sb("wp0", [P, D])
        wq0, wk0, wv0 = (wqkv0[:, i * D:i * D + D] for i in range(3))
        pb0 = sb("pb0", [P, D])
        wa = [{n: sb(f"w{n}{i}", [P, D]) for n in "qkvo"} for i in (1, 2, 3)]
        woff = sb("woff", [P, H * NK]); boff = sb("boff", [P, H * NK])
        bq1 = sb("bq1", [P, 1]); bk1 = sb("bk1", [P, 1]); bv1 = sb("bv1", [P, D])
        bo1 = sb("bo1", [P, D]); bo3 = sb("bo3", [P, D])
        len1 = sb("len1", [P, B]); rlen1 = sb("rlen1", [P, B])
        gw = sb("gw", [P, 3, E])
        gb = sb("gb", [P, 2, E])
        w1_0 = sb("w1_0", [P, E + 1, HID]); w2_0 = sb("w2_0", [P, E + 1, 4, D])
        b1_0 = sb("b1_0", [P, E + 1, 4]); bs0 = sb("bs0", [P, 1]); b2_0 = sb("b2_0", [E, D])
        w1_1 = sb("w1_1", [P, E, HID1]); w3_1 = sb("w3_1", [P, E, HID1]); w2_1 = sb("w2_1", [P, E, 3, D])
        w1_2 = sb("w1_2", [P, E, HID]); w2_2 = sb("w2_2", [P, E, 4, D])
        b1_2 = sb("b1_2", [P, E, 4]); b2_2 = sb("b2_2", [E, D])
        wcomb = sb("wcomb", [P, 2 * PKH * PKN])
        ctxT = sb("ctxT", [P, B, S2])
        kern = sb("kern", [P, B, H * 9])
        keep = sb("keep", [RI, RT, T], U8)
        maskq = sb("maskq", [R, RT, T], U8)

        is_causal = sb("is_causal", [1, 1], I32)

        x = sb("x", [P, NT, D]); xn = sb("xn", [P, NT, D])
        xnTp = sb("xnTp", [P, T + 3]); xnT = xnTp[:, 2:T + 2]
        stats = sb("stats", [P, NT, 6]); mv = sb("mv", [P, NT, 2]); rstd = sb("rstd", [P, NT])
        ctxTb = sb("ctxTb", [P, S2]); kernb = sb("kernb", [P, H * 9])
        lenb = sb("lenb", [P, 2])
        gate = sb("gate", [P, NT, E]); glog = sb("glog", [P, NT, E]); gsel = sb("gsel", [P, NT, E])
        gtop = sb("gtop", [P, NT, 8]); gidx = sb("gidx", [P, NT, 8], U32); gidf = sb("gidf", [P, NT, 2])
        gm = sb("gm", [P, 2, NT, E]); gs = sb("gs", [P, NT]); gr = sb("gr", [P, NT])
        gT = sb("gT", [E, T])
        arena = sb("arena", [P, ARENA])


        at = [0]

        def carve(*shape, rows=P, dt=F32):
            n = int(np.prod(shape))
            v = arena[0:rows, at[0]:at[0] + n]
            at[0] += n
            assert at[0] <= ARENA, at[0]
            if dt is not F32:
                v = v.bitcast(dt)
            names = "abcd"[:len(shape)]
            if len(shape) > 1:
                v = v.rearrange(f"p ({' '.join(names)}) -> p {' '.join(names)}",
                                **{n_: s for n_, s in zip(names, shape)})
            return v

        done = sem("done")
        ln_stats = sem("ln_stats"); ln_mean = sem("ln_mean"); ln_rstd = sem("ln_rstd")
        ln_xn = sem("ln_xn"); ln_turned = sem("ln_turned"); ln_xnT = sem("ln_xnT")
        x_new = sem("x_new")
        dve_chain = sem("dve_chain"); act_chain = sem("act_chain"); pool_chain = sem("pool_chain")
        x_in = sem("x_in"); x_out = sem("x_out"); batch_in = sem("batch_in")
        loop_sems = [ln_stats, ln_mean, ln_rstd, ln_xn, ln_turned, ln_xnT, x_new, dve_chain,
                     act_chain, pool_chain, x_in, x_out, batch_in]

        def lsem(name):
            s = sem(name)
            loop_sems.append(s)
            return s

        W = {k: sem("w_" + k) for k in ("attn0", "misc", "ffn0", "ffn1", "ffn2", "last", "kgen", "keep", "p3")}
        wcount = {k: 0 for k in W}

        def clear_sems(sems):
            for s in sems:
                nc.gpsimd.sem_clear(s)
            nc.all_engine_barrier()

        at[0] = 0
        ctx_sb = carve(B, D, rows=S2)
        histw = carve(2 * D)
        histb = carve(2 * D, rows=S2); histg = carve(2 * D, rows=S2); histlb = carve(2 * D, rows=S2)
        cw1 = carve(2, 64); cb1 = carve(64, rows=S2); cw2 = carve(64, rows=S2); cb2 = carve(1, rows=S2)
        kw1 = carve(2, D); kb1 = carve(D, rows=B); kg = carve(D, rows=B); kb = carve(D, rows=B)
        kw2 = carve(H * 9); kb2 = carve(H * 9, rows=B)
        eh = carve(B, 2 * D, rows=S2); ehT = carve(B, 2, S2)
        hst = carve(B, 6, rows=S2); hmv = carve(B, 2, rows=S2); hrs = carve(B, rows=S2)
        aw1 = carve(B, 64, rows=S2); aws = carve(B, rows=S2); awt = carve(S2, rows=B); awn = carve(S2, rows=B)
        sm = carve(4, rows=B); awc = carve(B, rows=S2); ccT = carve(2, B)
        kh = carve(D, rows=B); khT = carve(B); kst = carve(6, rows=B); kmv = carve(2, rows=B)
        krs = carve(1, rows=B); kp = carve(H, 9, rows=B); kmx = carve(H, rows=B)
        wqt = carve(8, D); keyd = carve(8, 2 * PKN)
        m77 = carve(B, S2, dt=I32)
        mf = carve(B, S2)
        sel4 = carve(B, P, rows=B)
        kk = carve(12, P, rows=B)
        tri = carve(NT, T)
        mask_in = arena[:, at[0]:at[0] + NT * T // 4].bitcast(U8)\
            .rearrange("p (t n) -> p t n", t=NT)
        diff = arena[:, at[0] + NT * T // 4:at[0] + NT * T // 4 + 2]
        sel24 = arena[:, at[0] + NT * T // 4 + 2:at[0] + NT * T // 4 + 6]
        assert at[0] + NT * T // 4 + 6 <= ARENA, at[0]

        p_const = sem("p_const"); p_pe = sem("p_pe"); p_dve = sem("p_dve"); p_act = sem("p_act")
        p_dvec = sem("p_dvec"); p_pool = sem("p_pool"); p_poolc = sem("p_poolc")
        p_far = sem("p_far"); p_kk = sem("p_kk"); p_flag = sem("p_flag"); p_end = sem("p_end")
        with nc.Block() as block:
            @block.sync
            def _(sp):
                def ld(group, dst, src):
                    wcount[group] += 16
                    sp.dma_start(dst, src).then_inc(W[group], 16)

                row = lambda v, n: v.rearrange("(a n) -> a n", a=1).to_broadcast([n, v.shape[0]])
                ld("kgen", ctx_sb, A["ctx_1024"].rearrange("b s d -> s b d"))
                ld("kgen", histw, A["hist_W"])
                ld("kgen", histb, row(A["hist_b"], S2))
                ld("kgen", histg, row(A["hist_ln_g"], S2))
                ld("kgen", histlb, row(A["hist_ln_b"], S2))
                ld("kgen", cw1, A["ctx_W1"].rearrange("(c p) n -> p c n", p=P))
                ld("kgen", cb1, row(A["ctx_b1"], S2))
                ld("kgen", cw2, row(A["ctx_W2"], S2))
                ld("kgen", cb2, row(A["ctx_b2"], S2))
                ld("kgen", kw1, A["kg_W1"].rearrange("(c p) n -> p c n", p=P))
                ld("kgen", kb1, row(A["kg_b1"], B))
                ld("kgen", kg, row(A["kg_ln_g"], B))
                ld("kgen", kb, row(A["kg_ln_b"], B))
                ld("kgen", kw2, A["kg_W2"])
                ld("kgen", kb2, row(A["kg_b2"], B))
                ld("p3", wqt, A["w_qT"].rearrange("(c p) d -> p c d", p=P))
                ld("attn0", wq0, A["Wq0"]); ld("attn0", wk0, A["Wk0"])
                ld("attn0", wv0, A["Wv0"]); ld("attn0", wp0[:, :], A["Wp0"])
                ld("attn0", pb0[:, :], row(A["bp0"], P))
                sp.wait_ge(p_const, 1)
                for t in range(RT):
                    lo, hi = max(0, R * t - 1), min(T, R * t + R + 1)
                    o = lo - (R * t - 1)
                    ld("keep", keep[o:o + hi - lo, t, :], A["mask"][lo:hi, :])
                ld("keep", mask_in, A["mask"].rearrange("(t p) n -> p t n", p=P))
                for t in range(RT):
                    n = min(R, T - R * t)
                    ld("keep", maskq[0:n, t, :], A["mask"][R * t:R * t + n, :])
                ld("misc", m77, A["mask2"].rearrange("(a b) s -> a b s", a=1).to_broadcast([P, B, S2]))
                for i, d in enumerate(wa):
                    for n in "qkvo":
                        ld("misc", d[n][:, :], A[f"w{n}{i + 1}"])
                ld("misc", woff[:, :], A["Woff"]); ld("misc", boff[:, :], row(A["boff"], P))
                ld("misc", bq1[:, :], A["bq1"].rearrange("(n a) -> n a", a=1))
                ld("misc", bk1[:, :], A["bk1"].rearrange("(n a) -> n a", a=1))
                ld("misc", bv1[:, :], row(A["bv1"], P)); ld("misc", bo1[:, :], row(A["bo1"], P))
                ld("misc", bo3[:, :], row(A["bo3"], P))
                for i, n in enumerate(("Wr0", "Wr1", "Wr2")):
                    ld("misc", gw[:, i, :], A[n])
                ld("misc", gb[:, 0, :], row(A["eb1"], P)); ld("misc", gb[:, 1, :], row(A["br2"], P))
                ld("ffn0", w1_0[:, 0, :], A["Wfc_s"])
                ld("ffn0", w1_0[:, 1:, :], A["Wfc"].rearrange("e d h -> d e h"))
                ld("ffn0", w2_0[:, 0, :, :], A["Wproj_s"].rearrange("(c p) d -> p c d", p=P))
                ld("ffn0", b1_0[:, :, :], A["bfc"])
                for e in range(E):
                    ld("ffn0", w2_0[:, 1 + e, :, :], A["Wproj"][e].rearrange("(c p) d -> p c d", p=P))
                ld("ffn0", bs0[:, :], A["bproj_s"].rearrange("(n a) -> n a", a=1))
                ld("ffn0", b2_0[:, :], A["bproj"])
                ld("ffn1", w1_1[:, :, :], A["w1"].rearrange("e d h -> d e h"))
                ld("ffn1", w3_1[:, :, :], A["w3"].rearrange("e d h -> d e h"))
                for e in range(E):
                    ld("ffn1", w2_1[:, e, 0:2, :], A["w2"][e, 0:256].rearrange("(c p) d -> p c d", p=P))
                    ld("ffn1", w2_1[0:96, e, 2, :], A["w2"][e, 256:HID1])
                ld("ffn2", w1_2[:, :, :], A["W1"].rearrange("e d h -> d e h"))
                for e in range(E):
                    ld("ffn2", w2_2[:, e, :, :], A["W2"][e].rearrange("(c p) d -> p c d", p=P))
                ld("ffn2", b2_2[:, :], A["b2"])
                ld("ffn2", b1_2[:, :, :], A["b1"])
                for s, n in wcount.items():
                    if n:
                        sp.wait_ge(W[s], n)

            def p_consts(ch):
                def select(out_, op, fill, base, pattern, mult):
                    ch.link(nc.gpsimd.affine_select(out=out_, in_=out_, compare_op=op, fill=fill, base=base,
                                                    pattern=pattern, channel_multiplier=mult))

                ch.link(nc.gpsimd.tensor_copy(ident_bf[:, :], ident[:, :]))
                ch.link(nc.gpsimd.memset(quadmask[:, :], 1.0))
                select(quadmask[:, :], ALU.is_ge, 0.0, 0, [[-32, 4]], 1)
                select(quadmask[:, :], ALU.is_ge, 0.0, 31, [[32, 4]], -1)
                ch.link(nc.gpsimd.memset(sel24, 0.0))
                select(sel24, ALU.not_equal, 1.0, -24, [[-32, 4]], 1)
                ch.link(nc.gpsimd.memset(first_row[:, :], 0.0))
                select(first_row[:, :], ALU.not_equal, NEG, 0, [[0, 1]], 1)
                ch.link(nc.gpsimd.memset(far_q[:, :], 0.0))
                select(far_q[:, :], ALU.is_ge, NEG, 0, [[-1, P + 2]], 1)
                ch.link(nc.gpsimd.memset(far_k[:, :], 0.0))
                select(far_k[:, :], ALU.is_ge, NEG, -2, [[1, P + 2]], -1)
                ch.link(nc.gpsimd.memset(tri, 1.0))
                nc.gpsimd.affine_select(out=tri, in_=tri, compare_op=ALU.is_gt, fill=0.0, base=0,
                                        pattern=[[-P, NT], [1, T]], channel_multiplier=-1).then_inc(p_far, 1)

            @block.gpsimd
            def _(pool):
                ch = Chain(pool, p_poolc)
                nc.gpsimd.memset(xnTp[:, 0:2], 0.0)
                nc.gpsimd.memset(xnTp[:, T + 2:T + 3], 0.0)
                nc.gpsimd.memset(wq_rows[:, :, :, :], 0.0)
                nc.gpsimd.memset(wk_rows[:, :, :], 0.0)
                nc.gpsimd.memset(kk, 0.0).then_inc(p_kk, 1)
                nc.gpsimd.memset(maskq[:, :, :], 0)
                ch.link(nc.gpsimd.memset(keep[:, :, :], 1))
                nc.gpsimd.memset(neghalf[:, :], -0.5).then_inc(p_const, 1)
                ch.link(nc.gpsimd.memset(keyd, 0.0))
                for c in range(8):
                    p_, hp = c // 4, c % 4
                    for u in range(2):
                        pool.dma_start(keyd[64 * u:64 * u + 64, c, PKN * u:PKN * u + PKN],
                                       A["keysT"][2 * hp + u, p_]).then_inc(W["last"], 16)
                ch.link(nc.gpsimd.memset(ident[:, :], 0.0))
                ch.link(nc.gpsimd.affine_select(out=ident[:, :], in_=ident[:, :], compare_op=ALU.not_equal,
                                                fill=1.0, base=0, pattern=[[-1, P]], channel_multiplier=1))
                ch.link(nc.gpsimd.memset(shift[:, :, :], 0.0))
                ch.link(nc.gpsimd.affine_select(out=shift[:, :, :], in_=shift[:, :, :], compare_op=ALU.not_equal,
                                                fill=1.0, base=0, pattern=[[-1, 3], [-1, P]], channel_multiplier=1))
                ch.link(nc.gpsimd.memset(headmask[:, :], 1.0))
                ch.link(nc.gpsimd.affine_select(out=headmask[:, :], in_=headmask[:, :], compare_op=ALU.is_ge,
                                                fill=0.0, base=0, pattern=[[-HD, H]], channel_multiplier=1))
                ch.link(nc.gpsimd.affine_select(out=headmask[:, :], in_=headmask[:, :], compare_op=ALU.is_ge,
                                                fill=0.0, base=HD - 1, pattern=[[HD, H]], channel_multiplier=-1))
                ch.link(nc.gpsimd.memset(sel4, 0.0))
                ch.link(nc.gpsimd.affine_select(out=sel4, in_=sel4, compare_op=ALU.not_equal,
                                                fill=1.0, base=0, pattern=[[-1, B], [0, P]], channel_multiplier=1))
                fl = dict(allow_small_or_imprecise_dtypes=True)
                ch.link(nc.gpsimd.iota(iota_j[:, :], [[1, S2]], base=0, channel_multiplier=0, **fl))
                ch.link(nc.gpsimd.iota(iota_e[:, :], [[1, E]], base=0, channel_multiplier=0, **fl))
                ch.link(nc.gpsimd.iota(iota_k[:, :], [[1, PKN]], base=-PKN, channel_multiplier=0, **fl))
                ch.link(nc.gpsimd.iota(ref_k[:, :, :], [[0, H], [1, NK]], base=-3, channel_multiplier=0, **fl))
                nc.gpsimd.iota(loc[:, :], [[P, NT]], base=0, channel_multiplier=1, **fl).then_inc(p_const, 1)
                p_consts(ch)
                pool.wait_ge(p_dve, 2)
                ch.link(nc.gpsimd.tensor_scalar(hrs, hmv[:, :, 1], EPS, None, ALU.add))
                nc.gpsimd.tensor_tensor(hrs, hrs, neghalf[0:S2, 0:B], ALU.pow).then_inc(p_pool, 1)
                pool.wait_ge(p_dve, 9)
                ch.link(nc.gpsimd.tensor_scalar(krs, kmv[:, 1:2], EPS, None, ALU.add))
                nc.gpsimd.tensor_tensor(krs, krs, neghalf[0:B, 0:1], ALU.pow).then_inc(p_pool, 1)

            @block.tensor
            def _(pe):
                pe.wait_ge(p_const, 2)
                pe.wait_ge(W["kgen"], wcount["kgen"])
                for b in range(B):
                    mm = nc.tensor.transpose(ps[:, 0, b * P:b * P + S2], ctx_sb[:, b, :], ident[0:S2, 0:S2])
                mm.then_inc(p_pe, 1)
                pe.wait_ge(p_dve, 1)
                for b in range(B):
                    mm = nc.tensor.matmul(ps[0:S2, 1 + b // 2, (b % 2) * 256:(b % 2) * 256 + 256], ctxT[:, b, :], histw,
                                          start=True, stop=True)
                mm.then_inc(p_pe, 1)
                pe.wait_ge(p_act, 1)
                for b in range(B):
                    for c in range(2):
                        o = (b * 2 + c) % 4 * P
                        mm = nc.tensor.transpose(ps[:, 3 + b // 2, o:o + S2], eh[:, b, c * P:c * P + P],
                                                 ident[0:S2, 0:S2])
                mm.then_inc(p_pe, 1)
                pe.wait_ge(p_dve, 3)
                for b in range(B):
                    for c in range(2):
                        mm = nc.tensor.matmul(ps[0:S2, 5, b * 64:b * 64 + 64], ehT[:, b, c, :], cw1[:, c, :],
                                              start=c == 0, stop=c == 1)
                mm.then_inc(p_pe, 1)
                pe.wait_ge(p_dve, 5)
                nc.tensor.transpose(ps[0:B, 6, 0:S2], aws, ident[0:S2, 0:S2]).then_inc(p_pe, 1)
                pe.wait_ge(p_dve, 7)
                nc.tensor.transpose(ps[0:S2, 6, 128:128 + B], awn, ident[0:B, 0:B]).then_inc(p_pe, 1)
                pe.wait_ge(p_act, 4)
                for b in range(B):
                    for c in range(2):
                        mm = nc.tensor.matmul(ps[:, 7, c * B + b:c * B + b + 1], eh[:, b, c * P:c * P + P],
                                              awc[:, b:b + 1], start=True, stop=True)
                mm.then_inc(p_pe, 1)
                pe.wait_ge(p_act, 5)
                for c in range(2):
                    mm = nc.tensor.matmul(ps[0:B, 0, 0:D], ccT[:, c, :], kw1[:, c, :], start=c == 0, stop=c == 1)
                mm.then_inc(p_pe, 1)
                pe.wait_ge(p_act, 6)
                nc.tensor.transpose(ps[:, 1, 0:B], kh, ident[0:B, 0:B]).then_inc(p_pe, 1)
                pe.wait_ge(p_act, 7)
                nc.tensor.matmul(ps[0:B, 2, 0:H * 9], khT, kw2, start=True, stop=True).then_inc(p_pe, 1)
                pe.wait_ge(p_dve, 12)
                for b in range(B):
                    mm = nc.tensor.matmul(ps[:, 3 + b // 2, (b % 2) * 256:(b % 2) * 256 + H * 9], sel4[:, b, :],
                                          kp.rearrange("p h n -> p (h n)"), start=True, stop=True)
                mm.then_inc(p_pe, 1)
                pe.wait_ge(W["p3"], wcount["p3"])
                pe.wait_ge(W["last"], 16 * 16)
                for c in range(8):
                    mm = nc.tensor.matmul(ps[:, 5, c * 64:c * 64 + 64], wqt[:, c, :], keyd[:, c, :],
                                          start=True, stop=True)
                mm.then_inc(p_pe, 1)
                pe.wait_ge(p_kk, 2)
                for n in range(12):
                    mm = nc.tensor.transpose(ps[:, 6, n * B:n * B + B], kk[:, n, :], ident[0:B, 0:B])
                mm.then_inc(p_pe, 1)
                pe.wait_ge(p_flag, 1)
                nc.tensor.matmul(ps[0:1, 7, 0:1], diff[:, 0:1], diff[:, 1:2], start=True, stop=True)\
                    .then_inc(p_pe, 1)

            @block.vector
            def _(dve):
                ch = Chain(dve, p_dvec)
                dve.wait_ge(p_pe, 1)
                nc.vector.tensor_copy(ctxT[:, :, :], ps[:, 0, :].rearrange("p (b s) -> p b s", b=B)[:, :, 0:S2])\
                    .then_inc(p_dve, 1)
                dve.wait_ge(p_pe, 2)
                for b in range(B):
                    src = ps[0:S2, 1 + b // 2, (b % 2) * 256:(b % 2) * 256 + 256]
                    ch.link(nc.vector.tensor_tensor(eh[:, b, :], src, histb, ALU.add))
                    ch.link(nc.vector.bn_stats(hst[:, b, :], eh[:, b, :]))
                    ch.link(nc.vector.bn_aggr(hmv[:, b, :], hst[:, b, :]))
                nc.vector.memset(sm[:, :], 0.0).then_inc(p_dve, 1)
                dve.wait_ge(p_pool, 1)
                for b in range(B):
                    ch.link(nc.vector.tensor_scalar(eh[:, b, :], eh[:, b, :], hmv[:, b, 0:1], hrs[:, b:b + 1],
                                                    ALU.subtract, ALU.mult))
                    ch.link(nc.vector.tensor_tensor(eh[:, b, :], eh[:, b, :], histg, ALU.mult))
                    ch.link(nc.vector.tensor_tensor(eh[:, b, :], eh[:, b, :], histlb, ALU.add))
                dve.wait_ge(p_pe, 3)
                for b in range(B):
                    src = ps[:, 3 + b // 2, (b % 2) * 256:(b % 2) * 256 + 256]
                    last = nc.vector.tensor_copy(ehT[:, b, :, :], src.rearrange("p (c s) -> p c s", c=2)[:, :, 0:S2])
                last.then_inc(p_dve, 1)
                dve.wait_ge(p_pe, 4)
                nc.vector.tensor_tensor(aw1, ps[0:S2, 5, 0:B * 64].rearrange("p (b n) -> p b n", b=B),
                                        cb1.unsqueeze(1).to_broadcast([S2, B, 64]), ALU.add).then_inc(p_dve, 1)
                dve.wait_ge(p_act, 2)
                ch.link(nc.vector.tensor_tensor(aw1, aw1, cw2.unsqueeze(1).to_broadcast([S2, B, 64]), ALU.mult))
                ch.link(nc.vector.tensor_reduce(aws, aw1, AX_X, ALU.add))
                nc.vector.tensor_scalar(aws, aws, cb2, None, ALU.add).then_inc(p_dve, 1)
                dve.wait_ge(p_pe, 5)
                ch.link(nc.vector.tensor_reduce(sm[:, 0:1], ps[0:B, 6, 0:S2], AX_X, ALU.max))
                nc.vector.tensor_scalar(awt, ps[0:B, 6, 0:S2], sm[:, 0:1], None, ALU.subtract).then_inc(p_dve, 1)
                dve.wait_ge(p_act, 3)
                ch.link(nc.vector.tensor_reduce(sm[:, 1:2], awt, AX_X, ALU.add))
                ch.link(nc.vector.reciprocal(sm[:, 2:3], sm[:, 1:2]))
                nc.vector.tensor_scalar(awn, awt, sm[:, 2:3], None, ALU.mult).then_inc(p_dve, 1)
                dve.wait_ge(p_pe, 8)
                ch.link(nc.vector.tensor_tensor(kh, ps[0:B, 0, 0:D], kb1, ALU.add))
                ch.link(nc.vector.bn_stats(kst, kh))
                nc.vector.bn_aggr(kmv, kst).then_inc(p_dve, 2)
                dve.wait_ge(p_pool, 2)
                ch.link(nc.vector.tensor_scalar(kh, kh, kmv[:, 0:1], krs, ALU.subtract, ALU.mult))
                ch.link(nc.vector.tensor_tensor(kh, kh, kg, ALU.mult))
                nc.vector.tensor_tensor(kh, kh, kb, ALU.add).then_inc(p_dve, 1)
                dve.wait_ge(p_pe, 10)
                kp2 = kp.rearrange("p h n -> p (h n)")
                ch.link(nc.vector.tensor_tensor(kp2, ps[0:B, 2, 0:H * 9], kb2, ALU.add))
                ch.link(nc.vector.tensor_reduce(kmx, kp, AX_X, ALU.max))
                nc.vector.tensor_tensor(kp, kp, kmx.unsqueeze(2).to_broadcast([B, H, 9]), ALU.subtract)\
                    .then_inc(p_dve, 1)
                dve.wait_ge(p_act, 8)
                ch.link(nc.vector.tensor_reduce(kmx, kp, AX_X, ALU.add))
                ch.link(nc.vector.reciprocal(kmx, kmx))
                nc.vector.tensor_tensor(kp, kp, kmx.unsqueeze(2).to_broadcast([B, H, 9]), ALU.mult)\
                    .then_inc(p_dve, 1)
                dve.wait_ge(p_pe, 11)
                for b in range(B):
                    nc.vector.tensor_copy(kern[:, b, :], ps[:, 3 + b // 2, (b % 2) * 256:(b % 2) * 256 + H * 9])
                dve.wait_ge(p_pe, 12)
                nc.vector.tensor_copy(wcomb[:, :], ps[:, 5, :])
                dve.wait_ge(W["misc"], wcount["misc"])
                ch.link(nc.vector.tensor_scalar(mf, m77, -1.0, 1.0, ALU.mult, ALU.add))
                ch.link(nc.vector.tensor_reduce(len1[:, :], mf, AX_X, ALU.add))
                ch.link(nc.vector.tensor_scalar(len1[:, :], len1[:, :], -1.0, None, ALU.add))
                ch.link(nc.vector.reciprocal(rlen1[:, :], len1[:, :]))
                dve.wait_ge(p_kk, 1)
                kp4 = kp.rearrange("b (g r) (y x) -> b g r y x", g=4, y=3)
                for gg in range(4):
                    for dx in range(3):
                        dst = kk[:, gg * 3 + dx, :].rearrange("b (r q) -> b r q", r=4)[:, :, 0:24]
                        last = nc.vector.tensor_copy(dst.rearrange("b r (y d) -> b r y d", y=3),
                                                     kp4[:, gg, :, :, dx].unsqueeze(3).to_broadcast([B, 4, 3, HD]))
                last.then_inc(p_kk, 1)
                dve.wait_ge(p_pe, 13)
                nc.vector.tensor_copy(wcol[:, :, :], ps[:, 6, 0:12 * B].rearrange("p (n b) -> p n b", n=12))
                dve.wait_ge(W["attn0"], wcount["attn0"])
                for dy in range(3):
                    src = lambda w: w.rearrange("p (g r d) -> p g r d", g=4, r=4)
                    nc.vector.tensor_copy(wq_rows[:, :, dy, :].rearrange("p g (r q) -> p g r q", r=4)[:, :, :, 8 * dy:8 * dy + 8],
                                          src(wq0))
                    nc.vector.tensor_copy(wk_rows[:, :, :].rearrange("p g (r q) -> p g r q", r=4)[:, :, :, 8 * dy:8 * dy + 8],
                                          src(wk0))
                dve.wait_ge(p_far, 1)
                ch.link(nc.vector.tensor_reduce(row24[:, :], sel24, AX_X, ALU.add))
                dve.wait_ge(W["keep"], wcount["keep"])
                ch.link(nc.vector.tensor_tensor(tri, tri, mask_in, ALU.not_equal))
                ch.link(nc.vector.memset(diff[:, 1:2], 1.0))
                nc.vector.tensor_reduce(diff[:, 0:1], tri.rearrange("p t n -> p (t n)"), AX_X, ALU.add).then_inc(p_flag, 1)
                dve.wait_ge(p_pe, 14)
                nc.vector.tensor_scalar(is_causal[:, :], ps[0:1, 7, 0:1], 0.0, None, ALU.is_equal)
                dve.wait_ge(W["keep"], wcount["keep"])
                nc.vector.tensor_scalar(keep[:, :, :], keep[:, :, :], -1.0, 1.0, ALU.mult, ALU.add)

            @block.scalar
            def _(act):
                act.wait_ge(p_dvec, 6 * B)
                nc.scalar.activation(eh, eh, ACT.Gelu).then_inc(p_act, 1)
                act.wait_ge(p_dve, 4)
                nc.scalar.activation(aw1, aw1, ACT.Gelu).then_inc(p_act, 1)
                act.wait_ge(p_dve, 6)
                nc.scalar.activation(awt, awt, ACT.Exp).then_inc(p_act, 1)
                act.wait_ge(p_pe, 6)
                nc.scalar.copy(awc, ps[0:S2, 6, 128:128 + B]).then_inc(p_act, 1)
                act.wait_ge(p_pe, 7)
                nc.scalar.copy(ccT, ps[:, 7, 0:2 * B].rearrange("p (c b) -> p c b", c=2)).then_inc(p_act, 1)
                act.wait_ge(p_dve, 10)
                nc.scalar.activation(kh, kh, ACT.Gelu).then_inc(p_act, 1)
                act.wait_ge(p_pe, 9)
                nc.scalar.copy(khT, ps[:, 1, 0:B]).then_inc(p_act, 1)
                act.wait_ge(p_dve, 11)
                nc.scalar.activation(kp, kp, ACT.Exp).then_inc(p_act, 1)

        at[0] = 0
        oT = carve(T)
        qT = carve(RT * R + 2)
        kT0 = carve(T); v0 = carve(NT, D)
        qm = carve(RT * R + 2); band = carve(3, R)
        sc = carve(2, T + 2); pr = carve(2, T); pT = carve(2, 4, R)
        at_out = carve(RT, D); mx = carve(8); rs = carve(RT); rr = carve(RT)
        at[0] = T
        q3 = carve(4, T)
        kpad = carve(T + 2); kc = carve(T); km = carve(4, T)
        near = at[0]
        pt = carve(2, 1280)
        end = at[0]
        at[0] = near
        ks = carve(4, D); prod = carve(9, D); near_dots = carve(9, H); nearw = carve(2, 9, H)
        at[0] = end
        v9 = carve(NT, H, HD + 1); vm = carve(NT, D)
        e01 = carve(NT, 2, H); mA = carve(NT, H); mz = carve(NT, P)
        osb = carve(NT, H, HD + 1); den = carve(NT, H); num = carve(NT, D); tmp = carve(NT, D)
        at[0] = 0
        qTx = carve(T); kTx = carve(S2); vx = carve(D, rows=S2); kbd = carve(H, S2)
        ox = carve(D); oTx = carve(P)
        ssm = carve(2, H); srs = carve(H)
        branch = at[0]
        sx = carve(2, H, S2); aT = carve(H, P, rows=S2); smx = carve(H)
        at[0] = branch
        HG = 4
        NG = H // HG
        ofq = carve(NT, H * NK)
        hat = carve(3, HG, NK, S2)
        hsc = carve(HG, NK, S2)
        hw = carve(HG, NK, S2)
        psc = carve(H, NK); pmx = carve(H)
        aTs = carve(2, HG, P, rows=S2)
        at[0] = branch + NT * H * NK
        offs = carve(NT, H * NK); off_i = carve(NT, H * NK, dt=I32); off_t = carve(NT, H * NK)
        at[0] = 0
        hb = carve(4, T); xs = carve(2, T); yT = carve(T)
        at[0] = 0
        sims = carve(16, PKN); eqk = carve(16, PKN); kmax = carve(16); kidx = carve(16)
        eid = carve(8); eidi = carve(8, dt=I32); esc = carve(8); dots = carve(8); hv = carve(8)
        rows_g = carve(PKH, 2 * D); junk = carve(D); accu = carve(D)

        rows_in = sem("rows_in")
        b_ready = lsem("b_ready")
        q0_mm = lsem("q0_mm"); q0_sb = lsem("q0_sb")
        g = {n: lsem("g_" + n) for n in ("log", "max", "exp", "done", "turn", "gT")}
        f = {n: lsem("f_" + n) for n in ("up", "act", "hg", "gb", "xs", "down", "y", "ysb", "yt")}
        a = {n: lsem("a_" + n) for n in ("proj", "q", "kv", "s", "sub", "exp", "p", "turn", "aT", "o", "osb",
                                         "ot", "otsb", "y", "off", "aT_even")}
        s1 = {n: lsem("s1_" + n) for n in ("ix", "pos", "abs", "hat", "sc", "used", "shift", "exp", "w", "turn", "aT", "pv",
                                           "osb", "ot", "otsb", "y")}
        k = {n: lsem("k_" + n) for n in ("sim", "idx", "dot", "act")}
        i0 = {n: lsem("i0_" + n) for n in ("qm", "s", "a", "c", "m", "p", "t", "pt", "o", "n", "mb", "turn", "oT", "y")}

        i1 = {n: lsem("i1_" + n) for n in ("nmm", "nsb", "ne", "q", "qsb", "k", "ksb", "kc", "kmr", "km", "amm", "amax",
                                           "mz", "mt", "q3m", "bmm", "exp", "pv", "osb", "e", "ee", "num", "turn")}
        bnk = lambda i: ps[:, i, :]
        HS = [(0, 6), (6, 12), (12, 16)]
        U0 = 4 * (E + 1)
        NX = (1, 2, 6, 7, 11, 12, 16, 20)[min(stop_after, 7)]

        causal = nc.values_load(is_causal[0:1, 0:1], min_val=0, max_val=1)

        with nc.Fori(0, B) as b:
            with nc.Block() as block:
                @block.sync
                def _(sp):
                    sp.dma_start(x[:, :, :], A["x"][bass.ds(b, 1)].rearrange("a (t p) d -> p (a t) d", p=P))\
                        .then_inc(x_in, 16)

                @block.gpsimd
                def _(pool):
                    ch = Chain(pool, pool_chain)
                    norm_pool(nc, pool, ch, 0, ln_mean, ln_rstd, mv, rstd, neghalf)

                @block.vector
                def _(dve):
                    nc.vector.tensor_copy(kernb[:, :], kern[:, bass.ds(b, 1), :].rearrange("p a n -> p (a n)"))
                    nc.vector.tensor_copy(ctxTb[:, :], ctxT[:, bass.ds(b, 1), :].rearrange("p a n -> p (a n)"))
                    nc.vector.tensor_copy(lenb[:, 0:1], len1[:, bass.ds(b, 1)])
                    nc.vector.tensor_copy(lenb[:, 1:2], rlen1[:, bass.ds(b, 1)])
                    dve.wait_ge(x_in, 16)
                    norm_vector(nc, dve, 0, x, xn, stats, mv, rstd, ln_stats, ln_mean, ln_rstd, ln_xn)

                @block.tensor
                def _(pe):
                    norm_tensor(nc, pe, 0, xn, ident, bnk(0), ln_xn, ln_turned)

                @block.scalar
                def _(act):
                    norm_scalar(nc, act, 0, xnT, bnk(0), ln_turned, ln_xnT)
            clear_sems(loop_sems)

            with nc.If(causal >= 1):
                with nc.Block() as block:
                    G = 4
                    PAIRS = [(0, 0, 2), (1, 0, 3), (2, 0, 4)]
                    NEARW = [(0, 1, 0, 0, 1), (0, 3, 1, 0, 2), (0, 6, 2, 0, 3),
                             (1, 0, 0, 0, 2), (1, 2, 1, 0, 3), (1, 5, 2, 0, 3)]

                    @block.sync
                    def _(sp):
                        sp.wait_ge(i1["turn"], 1)

                    @block.gpsimd
                    def _(pool):
                        for gg in range(G):
                            pool.wait_ge(i1["kc"], gg + 1)
                            for r in range(4):
                                if gg:
                                    pool.wait_ge(i1["bmm"], 4 * (gg - 1) + r + 1)
                                nc.gpsimd.tensor_scalar(km[:, r, :], kc, quadmask[:, r:r + 1], None, ALU.mult)\
                                    .then_inc(i1["km"], 1)

                    @block.tensor
                    def _(pe):
                        def queries_keys(gg):
                            if gg:
                                pe.wait_ge(i1["ksb"], gg)
                                pe.wait_ge(i1["q3m"], gg)
                            for dy in range(3):
                                mm = nc.tensor.matmul(bnk(6), wq_rows[:, gg, dy, :], xnTp[:, 1 + dy:1 + dy + T],
                                                      start=dy == 0, stop=dy == 2)
                            mm.then_inc(i1["q"], 1)
                            pe.wait_ge(i1["qsb"], gg + 1)
                            nc.tensor.matmul(bnk(6), wk_rows[:, gg, :], xnT, start=True, stop=True).then_inc(i1["k"], 1)

                        def shifted(t):
                            s = 3 * (t % 2)
                            if t >= 2:
                                pe.wait_ge(i1["ne"], t - 1)
                            c = 2 + P * t
                            for off, bank, o, w0_, w1_ in ((-1, 0, 0, 0, 384), (0, 1, 0, 0, 384), (1, 2, 0, 0, 256),
                                                           (-2, 2, 256, 128, 256)):
                                mm = nc.tensor.matmul(ps[:, s + bank, o:o + w1_ - w0_], xnTp[:, c + off:c + off + P],
                                                      wqkv0[:, w0_:w1_], start=True, stop=True)
                            mm.then_inc(i1["nmm"], 1)

                        def spans(base):
                            f_ = ps[:, base:base + 3, :].rearrange("p b n -> p (b n)")
                            return lambda a_, n_: f_[:, a_:a_ + n_]

                        def max_scores(gg, r):
                            h_ = 4 * gg + r
                            pe.wait_ge(i1["kmr"], h_ + 1)
                            if h_:
                                pe.wait_ge(i1["amax"], h_)
                            else:
                                pe.wait_ge(i1["ne"], 4)
                            at_ = spans(0)
                            for t, o in ((3, 0), (2, 512), (0, 896), (1, 1024)):
                                nc.tensor.matmul(at_(o, P * t + P), q3r[:, gg % 2, P * t:P * t + P],
                                                 kmr[:, r, 0:P * t + P], start=True, stop=False)
                                if t:
                                    mm = nc.tensor.matmul(at_(o + P * t - 2, P + 2), ident_bf[:, :], far_q[:, :],
                                                          start=False, stop=True)
                                else:
                                    mm = nc.tensor.matmul(at_(o, P), ident_bf[:, :], far_q[:, 2:P + 2],
                                                          start=False, stop=True)
                            mm.then_inc(i1["amm"], 1)

                        def scores(gg, r):
                            h_ = 4 * gg + r
                            pe.wait_ge(i1["km"], h_ + 1)
                            if r == 0:
                                pe.wait_ge(i1["q3m"], gg + 1)
                            if h_:
                                pe.wait_ge(i1["exp"], h_)
                            at_ = spans(3)
                            for t, o in ((0, 0), (1, 512), (3, 896), (2, 1024)):
                                n_ = T - P * t
                                nc.tensor.matmul(at_(o, n_), km[:, r, P * t:P * t + P], q3[:, gg, P * t:T],
                                                 start=True, stop=False)
                                w_ = min(n_, P + 2)
                                mm = nc.tensor.matmul(at_(o, w_), ident_bf[:, :], far_k[:, 0:w_], start=False, stop=True)
                            mm.then_inc(i1["bmm"], 1)

                        def weighted(gg, r):
                            h_ = 4 * gg + r
                            pe.wait_ge(i1["exp"], h_ + 1)
                            if r == 0 and gg:
                                pe.wait_ge(i1["osb"], gg)
                            col = {0: 0, 1: 512, 3: 896, 2: 1024}
                            for t in range(NT):
                                o = (t * 4 + r) * (HD + 1)
                                for kt in range(t + 1):
                                    c = col[kt] + P * (t - kt)
                                    mm = nc.tensor.matmul(ps[:, 7, o:o + HD + 1], pt[:, h_ % 2, c:c + P], v9[:, kt, h_, :],
                                                          start=kt == 0, stop=kt == t)
                            mm.then_inc(i1["pv"], 1)

                        def maximum_in(gg):
                            pe.wait_ge(i1["mz"], gg + 1)
                            pe.wait_ge(i1["ksb"], min(gg + 1, G))
                            for t in range(NT):
                                mm = nc.tensor.transpose(ps[:, 6, t * P:t * P + P], mz[:, t, :], ident[:, :])
                            mm.then_inc(i1["mt"], 1)

                        queries_keys(0)
                        for t in range(NT):
                            shifted(t)
                        for r in range(4):
                            max_scores(0, r)
                        maximum_in(0)
                        for gg in range(G):
                            if gg + 1 < G:
                                queries_keys(gg + 1)
                            for r in range(4):
                                scores(gg, r)
                                if gg + 1 < G:
                                    max_scores(gg + 1, r)
                                if r:
                                    weighted(gg, r - 1)
                            weighted(gg, 3)
                            if gg + 1 < G:
                                maximum_in(gg + 1)
                        pe.wait_ge(i1["num"], 1)
                        for t in range(NT):
                            mm = nc.tensor.transpose(ps[:, 0, t * P:t * P + P], num[:, t, :], ident[:, :])
                        mm.then_inc(i1["turn"], 1)

                    @block.scalar
                    def _(act):
                        def queries_keys(gg):
                            act.wait_ge(i1["q"], gg + 1)
                            nc.scalar.copy(q3[:, gg, :], bnk(6))
                            if gg >= 2:
                                act.wait_ge(i1["amm"], 4 * (gg - 1))
                            nc.scalar.copy(q3r[:, gg % 2, :], bnk(6)).then_inc(i1["qsb"], 1)
                            act.wait_ge(i1["k"], gg + 1)
                            if gg:
                                act.wait_ge(i1["kc"], gg)
                            nc.scalar.copy(kpad[:, 1:T + 1], bnk(6)).then_inc(i1["ksb"], 1)

                        queries_keys(0)
                        for t in range(NT):
                            s = 3 * (t % 2)
                            act.wait_ge(i1["nmm"], t + 1)
                            if t:
                                act.wait_ge(i1["ne"], t)
                            for dst, bank, o in ((0, 2, 256), (1, 0, 128), (2, 1, 128), (3, 2, 128)):
                                nc.scalar.copy(ks[:, dst, :], ps[:, s + bank, o:o + P])
                            nc.scalar.copy(vm[:, t, :], ps[:, s, 256:384])
                            nc.scalar.copy(v9[:, t, :, 0:HD], ps[:, s + 1, 256:384].rearrange("p (h d) -> p h d", h=H))\
                                .then_inc(i1["nsb"], 1)
                        for gg in range(G):
                            if gg + 1 < G:
                                queries_keys(gg + 1)
                            for r in range(4):
                                h_ = 4 * gg + r
                                act.wait_ge(i1["bmm"], h_ + 1)
                                if h_ >= 2:
                                    act.wait_ge(i1["pv"], h_ - 1)
                                nc.scalar.activation(pt[:, h_ % 2, :], ps[:, 3:6, :].rearrange("p b n -> p (b n)")[:, 0:1280],
                                                     ACT.Exp, scale=SCALE).then_inc(i1["exp"], 1)
                        act.wait_ge(i1["e"], 1)
                        nc.scalar.activation(e01, e01, ACT.Exp, scale=SCALE).then_inc(i1["ee"], 1)
                        act.wait_ge(i1["turn"], 1)
                        nc.scalar.copy(oT, bnk(0))

                    @block.vector
                    def _(dve):
                        ch = Chain(dve, dve_chain)

                        def keys(gg):
                            dve.wait_ge(i1["ksb"], gg + 1)
                            if gg:
                                dve.wait_ge(i1["km"], 4 * gg)
                            w = lambda dx: wcol[:, gg * 3 + dx, bass.ds(b, 1)]
                            ch.link(nc.vector.tensor_scalar(kc, kpad[:, 0:T], w(0), row24[:, :], ALU.mult, ALU.add))
                            ch.link(nc.vector.scalar_tensor_tensor(kc, kpad[:, 1:T + 1], w(1), kc, ALU.mult, ALU.add))
                            nc.vector.scalar_tensor_tensor(kc, kpad[:, 2:T + 2], w(2), kc, ALU.mult, ALU.add)\
                                .then_inc(i1["kc"], 1)
                            dve.wait_ge(i1["kc"], gg + 1)
                            for r in range(4):
                                if gg:
                                    dve.wait_ge(i1["amm"], 4 * (gg - 1) + r + 1)
                                nc.vector.tensor_scalar(kmr[:, r, :], kc, quadmask[:, r:r + 1], None, ALU.mult)\
                                    .then_inc(i1["kmr"], 1)

                        def near_scores(t):
                            s = 3 * (t % 2)
                            dve.wait_ge(i1["nsb"], t + 1)
                            n = 0
                            for q_, k_, c in PAIRS:
                                ins = nc.vector.tensor_tensor(prod[:, n:n + c, :], ks[:, k_:k_ + c, :],
                                                              ps[:, s + q_, 0:P].unsqueeze(1).to_broadcast([P, c, D]), ALU.mult)
                                n += c
                            ch.link(ins)
                            ch.link(nc.vector.tensor_reduce(near_dots.rearrange("p n h -> p (n h)"),
                                                            prod.rearrange("p n (h d) -> p (n h) d", h=H), AX_X, ALU.add))
                            p2 = prod.rearrange("p n d -> p (n d)")[:, 0:2 * 9 * H].rearrange("p (e n h) -> p e n h", e=2, n=9)
                            ch.link(nc.vector.tensor_tensor(p2, nearw, near_dots.unsqueeze(1).to_broadcast([P, 2, 9, H]), ALU.mult))
                            nc.vector.tensor_reduce(e01[:, t, :, :], p2.rearrange("p e n h -> p e h n"), AX_X, ALU.add)\
                                .then_inc(i1["ne"], 1)
                            if t == 0:
                                dve.wait_ge(i1["ne"], 1)
                                ch.link(nc.vector.tensor_scalar(e01[:, 0, 1, :], e01[:, 0, 1, :], first_row[:, :], None, ALU.add))

                        def maxima(gg):
                            flat = ps[:, 0:3, :].rearrange("p b n -> p (b n)")
                            for r in range(4):
                                h_ = 4 * gg + r
                                dve.wait_ge(i1["amm"], h_ + 1)
                                for t, o in ((3, 0), (2, 512), (0, 896), (1, 1024)):
                                    ins = nc.vector.tensor_reduce(mA[:, t, h_:h_ + 1], flat[:, o:o + P * t + P], AX_X, ALU.max)
                                ins.then_inc(i1["amax"], 1)

                        def maximum_out(gg):
                            hs = slice(4 * gg, 4 * gg + 4)
                            dve.wait_ge(i1["amax"], 4 * gg + 4)
                            for j in range(2):
                                ch.link(nc.vector.tensor_tensor(mA[:, :, hs], mA[:, :, hs], e01[:, :, j, hs], ALU.max))
                            if gg:
                                dve.wait_ge(i1["mt"], gg)
                            nc.vector.tensor_scalar(mz.rearrange("p t (r c) -> p t r c", r=4)[:, :, :, 24], mA[:, :, hs], -1.0, None,
                                                    ALU.mult).then_inc(i1["mz"], 1)

                        def maximum_in(gg):
                            dve.wait_ge(i1["mt"], gg + 1)
                            dve.wait_ge(i1["qsb"], gg + 1)
                            nc.vector.tensor_tensor(q3[:, gg, :], q3[:, gg, :], bnk(6), ALU.add).then_inc(i1["q3m"], 1)

                        def outputs(gg):
                            dve.wait_ge(i1["pv"], 4 * gg + 4)
                            nc.vector.tensor_copy(osb[:, :, 4 * gg:4 * gg + 4, :], ps[:, 7, 0:NT * 4 * (HD + 1)]
                                                  .rearrange("p (t r d) -> p t r d", t=NT, r=4)).then_inc(i1["osb"], 1)

                        nc.vector.memset(kpad[:, 0:1], 0.0)
                        nc.vector.memset(kpad[:, T + 1:T + 2], 0.0)
                        nc.vector.memset(mz, 0.0)
                        nc.vector.memset(v9[:, :, :, HD:HD + 1], 1.0)
                        ch.link(nc.vector.memset(nearw, 0.0))
                        kw = kernb[:, :].rearrange("p (h y x) -> p y x h", y=3, x=3)
                        for j, n, dy, dx, c in NEARW:
                            ins = nc.vector.tensor_copy(nearw[:, j, n:n + c, :], kw[:, dy, dx:dx + c, :])
                        ch.link(ins)
                        keys(0)
                        for t in range(NT):
                            near_scores(t)
                        maxima(0)
                        maximum_out(0)
                        maximum_in(0)
                        for gg in range(G):
                            if gg + 1 < G:
                                keys(gg + 1)
                                maxima(gg + 1)
                                maximum_out(gg + 1)
                            outputs(gg)
                            if gg + 1 < G:
                                maximum_in(gg + 1)
                        nc.vector.tensor_tensor(e01, e01, mA.unsqueeze(2).to_broadcast([P, NT, 2, H]), ALU.subtract)\
                            .then_inc(i1["e"], 1)
                        dve.wait_ge(i1["ee"], 1)
                        dve.wait_ge(i1["osb"], G)
                        ch.link(nc.vector.tensor_tensor(den, osb[:, :, :, HD], e01[:, :, 0, :], ALU.add))
                        ch.link(nc.vector.tensor_tensor(den, den, e01[:, :, 1, :], ALU.add))
                        ch.link(nc.vector.reciprocal(den, den))
                        four = lambda v: v.rearrange("p t (h d) -> p t h d", h=H)
                        wide = lambda v: v.unsqueeze(3).to_broadcast([P, NT, H, HD])
                        ch.link(nc.vector.tensor_tensor(four(tmp), v9[:, :, :, 0:HD], wide(e01[:, :, 0, :]), ALU.mult))
                        ch.link(nc.vector.tensor_tensor(four(num), osb[:, :, :, 0:HD], four(tmp), ALU.add))
                        ch.link(nc.vector.tensor_tensor(four(tmp), four(vm), wide(e01[:, :, 1, :]), ALU.mult))
                        ch.link(nc.vector.tensor_tensor(num, num, tmp, ALU.add))
                        nc.vector.tensor_tensor(four(num), four(num), wide(den), ALU.mult).then_inc(i1["num"], 1)
                clear_sems(loop_sems)
            with nc.Else():
                with nc.Block() as block:
                    @block.vector
                    def _(dve):
                        nc.vector.memset(qT[:, 0:1], 0.0)
                        nc.vector.memset(qT[:, 1 + T:RT * R + 2], 0.0)
                        nc.vector.memset(sc[:, :, 0:1], 0.0)
                        nc.vector.memset(sc[:, :, T + 1:T + 2], 0.0)
                        dve.wait_ge(q0_mm, 2)
                        nc.vector.tensor_copy(kT0, bnk(2))
                        dve.wait_ge(q0_mm, 3)
                        nc.vector.tensor_copy(v0, bnk(3).rearrange("p (t d) -> p t d", t=NT))

                    @block.tensor
                    def _(pe):
                        nc.tensor.matmul(bnk(1), wq0, xnT, start=True, stop=True).then_inc(q0_mm, 1)
                        nc.tensor.matmul(bnk(2), wk0, xnT, start=True, stop=True).then_inc(q0_mm, 1)
                        for t in range(NT):
                            mm = nc.tensor.matmul(ps[:, 3, t * P:t * P + P], xnT[:, t * P:t * P + P], wv0,
                                                  start=True, stop=True)
                        mm.then_inc(q0_mm, 1)

                    @block.scalar
                    def _(act):
                        act.wait_ge(q0_mm, 1)
                        nc.scalar.copy(qT[:, 1:1 + T], bnk(1))
                clear_sems(loop_sems)
                with nc.Fori(0, H) as h:
                    with nc.Block() as block:
                        @block.vector
                        def _(dve):
                            ch = Chain(dve, dve_chain)
                            nc.vector.tensor_scalar(qm, qT, headmask[:, bass.ds(h, 1)], None, ALU.mult)\
                                .then_inc(i0["qm"], 1)
                            for dx in range(3):
                                for dy in range(3):
                                    w = kernb[0:RI, bass.ds(h * 9 + (dy * 3 + dx), 1)]
                                    if dy == 0:
                                        ch.link(nc.vector.tensor_scalar(band[0:RI, dx, :], shift[0:RI, 0, 0:R], w, None,
                                                                        ALU.mult))
                                    else:
                                        ins = nc.vector.scalar_tensor_tensor(band[0:RI, dx, :], shift[0:RI, dy, 0:R], w,
                                                                             band[0:RI, dx, :], ALU.mult, ALU.add)
                                        if dy == 2:
                                            ins.then_inc(i0["qm"], 1)
                                        else:
                                            ch.link(ins)

                            def finish(t):
                                dve.wait_ge(i0["t"], t + 1)
                                nc.vector.tensor_copy(pT[:, t % 2, :, :], ps[:, 4 + t % 2, 0:4 * R]
                                                      .rearrange("p (c r) -> p c r", c=4)).then_inc(i0["pt"], 1)
                                dve.wait_ge(i0["p"], t + 1)
                                ch.link(nc.vector.reciprocal(rr[0:R, t:t + 1], rs[0:R, t:t + 1]))
                                dve.wait_ge(i0["o"], t + 1)
                                nc.vector.tensor_scalar(at_out[0:R, t, bass.ds(h * HD, HD)],
                                                        ps[0:R, 6, t * HD:t * HD + HD], rr[0:R, t:t + 1], None, ALU.mult)

                            for t in range(RT):
                                dve.wait_ge(i0["s"], t + 1)
                                if t >= 2:
                                    dve.wait_ge(i0["c"], t - 1)
                                nc.vector.tensor_tensor(sc[0:RI, t % 2, 1:T + 1], ps[0:RI, t % 2, :], keep[:, t, :], ALU.mult)\
                                    .then_inc(i0["a"], 1)
                                dve.wait_ge(i0["c"], t + 1)
                                if t >= 2:
                                    dve.wait_ge(i0["t"], t - 1)
                                ch.link(nc.vector.scalar_tensor_tensor(pr[0:R, t % 2, :], maskq[0:R, t, :], NEG,
                                                                       ps[0:R, 2 + t % 2, :], ALU.mult, ALU.add))
                                ch.link(nc.vector.tensor_reduce(mx[0:R, t:t + 1], pr[0:R, t % 2, :], AX_X, ALU.max))
                                nc.vector.tensor_scalar(mx[0:R, t:t + 1], mx[0:R, t:t + 1], -SCALE, None, ALU.mult)\
                                    .then_inc(i0["m"], 1)
                                if t >= 1:
                                    finish(t - 1)
                            finish(RT - 1)

                        @block.tensor
                        def _(pe):
                            pe.wait_ge(i0["qm"], 1)

                            def scores(t):
                                if t >= 2:
                                    pe.wait_ge(i0["a"], t - 1)
                                nc.tensor.matmul(ps[0:RI, t % 2, :], qm[:, R * t:R * t + RI], kT0, start=True, stop=True)\
                                    .then_inc(i0["s"], 1)

                            def pv(t):
                                pe.wait_ge(i0["p"], t + 1)
                                if t >= 2:
                                    pe.wait_ge(i0["pt"], t - 1)
                                for c in range(4):
                                    mm = nc.tensor.transpose(ps[:, 4 + t % 2, c * R:c * R + R],
                                                             pr[0:R, t % 2, c * P:c * P + P], ident[0:R, 0:R])
                                mm.then_inc(i0["t"], 1)
                                pe.wait_ge(i0["pt"], t + 1)
                                for c in range(4):
                                    mm = nc.tensor.matmul(ps[0:R, 6, t * HD:t * HD + HD], pT[:, t % 2, c, :],
                                                          v0[:, c, bass.ds(h * HD, HD)], start=c == 0, stop=c == 3)
                                mm.then_inc(i0["o"], 1)

                            scores(0)
                            for t in range(RT):
                                if t + 1 < RT:
                                    scores(t + 1)
                                pe.wait_ge(i0["a"], t + 1)
                                pe.wait_ge(i0["qm"], 4)
                                if t >= 2:
                                    pe.wait_ge(i0["m"], t - 1)
                                for dx in range(3):
                                    mm = nc.tensor.matmul(ps[0:R, 2 + t % 2, :], band[0:RI, dx, :],
                                                          sc[0:RI, t % 2, dx:dx + T], start=dx == 0, stop=dx == 2)
                                mm.then_inc(i0["c"], 1)
                                if t >= 1:
                                    pv(t - 1)
                            pv(RT - 1)

                        @block.scalar
                        def _(act):
                            for t in range(RT):
                                act.wait_ge(i0["m"], t + 1)
                                nc.scalar.activation(pr[0:R, t % 2, :], pr[0:R, t % 2, :], ACT.Exp, bias=mx[0:R, t:t + 1],
                                                     scale=SCALE, accum_out=rs[0:R, t:t + 1]).then_inc(i0["p"], 1)
                    clear_sems(loop_sems)
                with nc.Block() as block:
                    @block.tensor
                    def _(pe):
                        for t in range(RT):
                            n = min(R, T - R * t)
                            mm = nc.tensor.transpose(ps[:, 0, R * t:R * t + n], at_out[0:n, t, :], ident[0:n, 0:n])
                        mm.then_inc(i0["turn"], 1)

                    @block.scalar
                    def _(act):
                        act.wait_ge(i0["turn"], 1)
                        nc.scalar.copy(oT, bnk(0))
                clear_sems(loop_sems)

            with nc.Block() as block:
                LN = dict(x=x, xn=xn, stats=stats, mv=mv, rstd=rstd, ln_stats=ln_stats, ln_mean=ln_mean,
                          ln_rstd=ln_rstd, ln_xn=ln_xn)

                @block.sync
                def _(sp):
                    sp.wait_ge(x_new, NX)
                    sp.dma_start(out[bass.ds(b, 1)].rearrange("a (t p) d -> p (a t) d", p=P), x[:, :, :])\
                        .then_inc(x_out, 16)
                    sp.wait_ge(x_out, 16)

                @block.gpsimd
                def _(pool):
                    ch = Chain(pool, pool_chain)
                    norm = lambda n: norm_pool(nc, pool, ch, n, ln_mean, ln_rstd, mv, rstd, neghalf)
                    for n in range(min(7, stop_after)):
                        norm(n)
                        if n == 1:
                            pool.wait_ge(s1["ix"], 1)
                            for u in range(NT * NG):
                                t, hg = u // NG, u % NG
                                if u >= 3:
                                    pool.wait_ge(s1["w"], u - 2)
                                nc.gpsimd.tensor_tensor(
                                    hat[:, u % 3, :, :, :].rearrange("p h k j -> p (h k) j"),
                                    iota_j[:, :].unsqueeze(1).to_broadcast([P, HG * NK, S2]),
                                    ofq[:, t, hg * HG * NK:(hg + 1) * HG * NK].unsqueeze(2).to_broadcast([P, HG * NK, S2]),
                                    ALU.subtract).then_inc(s1["pos"], 1)
                    for t in range(NT if stop_after >= 7 else 0):
                        pool.wait_ge(k["idx"], t + 1)
                        for h in range(PKH):
                            pool.indirect_dma_start(out=rows_g[:, h, :], out_offset=None, in_=A["w_ud"],
                                                    in_offset=bass.IndirectOffsetOnAxis(ap=eidi[:, h:h + 1], axis=0))\
                                .then_inc(rows_in, 16)

                @block.vector
                def _(dve):
                    ch = Chain(dve, dve_chain)
                    nx = [0]

                    def norm(n):
                        if nx[0]:
                            dve.wait_ge(x_new, nx[0])
                        norm_vector(nc, dve, n, **LN)

                    def add_x(ins):
                        nx[0] += 1
                        ins.then_inc(x_new, 1)

                    def gates(n):
                        dve.wait_ge(g["log"], n + 1)
                        lg = ps[:, 7, 0:NT * E].rearrange("p (t e) -> p t e", t=NT)
                        if n == 2:
                            ch.link(nc.vector.tensor_tensor(glog[:, :, :], lg, gb[:, 1:2, :].to_broadcast([P, NT, E]), ALU.add))
                        else:
                            ch.link(nc.vector.tensor_copy(glog[:, :, :], lg))
                        ch.link(nc.vector.tensor_reduce(gs[:, :], glog[:, :, :], AX_X, ALU.max))
                        nc.vector.tensor_tensor(glog[:, :, :], glog[:, :, :], gs[:, :].unsqueeze(2).to_broadcast([P, NT, E]),
                                                ALU.subtract).then_inc(g["max"], 1)
                        dve.wait_ge(g["exp"], n + 1)
                        ch.link(nc.vector.tensor_reduce(gs[:, :], glog[:, :, :], AX_X, ALU.add))
                        ch.link(nc.vector.reciprocal(gr[:, :], gs[:, :]))
                        ch.link(nc.vector.tensor_tensor(glog[:, :, :], glog[:, :, :], gr[:, :].unsqueeze(2).to_broadcast([P, NT, E]),
                                                        ALU.mult))
                        pick = glog
                        if n == 1:
                            pick = gsel
                            ch.link(nc.vector.tensor_tensor(gsel[:, :, :], glog[:, :, :], gb[:, 0:1, :].to_broadcast([P, NT, E]),
                                                            ALU.add))
                        for t in range(NT):
                            ins = nc.vector.max(gtop[:, t, :], pick[:, t, :])
                            ins.then_inc(dve_chain, 1)
                            ch.n += 1
                        dve.wait_ge(dve_chain, ch.n)
                        for t in range(NT):
                            ins = nc.vector.max_index(gidx[:, t, :], gtop[:, t, :], pick[:, t, :])
                            ins.then_inc(dve_chain, 1)
                            ch.n += 1
                        dve.wait_ge(dve_chain, ch.n)
                        ch.link(nc.vector.tensor_copy(gidf[:, :, :], gidx[:, :, 0:2]))
                        for j in range(2):
                            ins = nc.vector.tensor_tensor(gm[:, j, :, :], iota_e[:, :].unsqueeze(1).to_broadcast([P, NT, E]),
                                                          gidf[:, :, j:j + 1].to_broadcast([P, NT, E]), ALU.is_equal)
                            ins.then_inc(dve_chain, 1)
                            ch.n += 1
                        dve.wait_ge(dve_chain, ch.n)
                        ch.link(nc.vector.tensor_tensor(gm[:, 0, :, :], gm[:, 0, :, :], gm[:, 1, :, :], ALU.add))
                        mul = nc.vector.tensor_tensor(gate[:, :, :], glog[:, :, :], gm[:, 0, :, :], ALU.mult)
                        if n != 1:
                            ch.link(mul)
                            ch.link(nc.vector.tensor_reduce(gs[:, :], gate[:, :, :], AX_X, ALU.add))
                            ch.link(nc.vector.reciprocal(gr[:, :], gs[:, :]))
                            mul = nc.vector.tensor_tensor(gate[:, :, :], gate[:, :, :],
                                                          gr[:, :].unsqueeze(2).to_broadcast([P, NT, E]), ALU.mult)
                        mul.then_inc(g["done"], 1)
                        dve.wait_ge(g["turn"], n + 1)
                        nc.vector.tensor_copy(gT[:, :], ps[0:E, 6, :]).then_inc(g["gT"], 1)

                    def add_ffn(n):
                        dve.wait_ge(f["yt"], n + 1)
                        add_x(nc.vector.tensor_tensor(x[:, :, :], x[:, :, :], bnk(4).rearrange("p (t d) -> p t d", t=NT), ALU.add))

                    def project_rows(projected, count, bias):
                        dve.wait_ge(projected, count)
                        for t in range(NT):
                            y = ps[:, 7, t * P:t * P + P]
                            if bias is not None:
                                ch.link(nc.vector.tensor_tensor(x[:, t, :], x[:, t, :], bias[:, :], ALU.add))
                            add_x(nc.vector.tensor_tensor(x[:, t, :], x[:, t, :], y, ALU.add))

                    def keys_values(i):
                        w = wa[i]
                        dve.wait_ge(a["proj"], 2 * i + 2)
                        if i == 0:
                            dve.wait_ge(W["misc"], wcount["misc"])
                            ch.link(nc.vector.tensor_scalar(kTx, ps[:, 1, 0:S2], bk1[:, :], None, ALU.add))
                            ch.link(nc.vector.tensor_scalar(kTx, kTx, 0.5 * SCALE, None, ALU.mult))
                            ch.link(nc.vector.tensor_tensor(vx, ps[0:S2, 1, P:2 * P], bv1[0:S2, :], ALU.add))
                            nc.vector.tensor_scalar(vx, vx, 0.5, None, ALU.mult).then_inc(a["kv"], 1)
                        else:
                            ch.link(nc.vector.tensor_copy(kTx, ps[:, 1, 0:S2]))
                            nc.vector.tensor_copy(vx, ps[0:S2, 1, P:2 * P]).then_inc(a["kv"], 1)
                        nc.vector.tensor_tensor(kbd, kTx.unsqueeze(1).to_broadcast([P, H, S2]),
                                                headmask[:, :].unsqueeze(2).to_broadcast([P, H, S2]), ALU.mult)\
                            .then_inc(a["kv"], 1)

                    def offsets():
                        o3 = ofq
                        dve.wait_ge(a["off"], 1)
                        pso = ps[:, 6, 0:NT * H * NK].rearrange("p (t n) -> p t n", t=NT)
                        bc = lambda v: v.unsqueeze(1).to_broadcast([P, NT, H * NK])
                        ch.link(nc.vector.tensor_tensor(o3, pso, bc(boff[:, :]), ALU.add))
                        ch.link(nc.vector.tensor_tensor(o3, o3, bc(ref_k[:, :, :].rearrange("p h k -> p (h k)")), ALU.add))
                        ch.link(nc.vector.tensor_tensor(o3, o3, loc[:, :].unsqueeze(2).to_broadcast([P, NT, H * NK]), ALU.add))
                        m, rm = lenb[:, 0:1], lenb[:, 1:2]
                        ch.link(nc.vector.tensor_scalar(offs, o3, rm, None, ALU.mult))
                        ch.link(nc.vector.tensor_copy(off_i, offs))
                        tmp = off_t
                        ch.link(nc.vector.tensor_copy(tmp, off_i))
                        ch.link(nc.vector.tensor_tensor(offs, tmp, offs, ALU.is_gt))
                        ch.link(nc.vector.tensor_tensor(tmp, tmp, offs, ALU.subtract))
                        ch.link(nc.vector.tensor_scalar(tmp, tmp, m, None, ALU.mult))
                        ch.link(nc.vector.tensor_tensor(o3, o3, tmp, ALU.subtract))
                        ch.link(nc.vector.tensor_scalar(offs, o3, rm, 0.0, ALU.mult, ALU.is_lt))
                        ch.link(nc.vector.tensor_scalar(offs, offs, m, None, ALU.mult))
                        ch.link(nc.vector.tensor_tensor(o3, o3, offs, ALU.add))
                        ch.link(nc.vector.tensor_scalar(tmp, o3, m, rm, ALU.subtract, ALU.mult))
                        ch.link(nc.vector.tensor_scalar(tmp, tmp, 0.0, m, ALU.is_ge, ALU.mult))
                        ch.link(nc.vector.tensor_tensor(o3, o3, tmp, ALU.subtract))
                        ch.link(nc.vector.tensor_scalar(o3, o3, 1.0 / (S2 - 1), 2.0, ALU.mult, ALU.mult))
                        ch.link(nc.vector.tensor_scalar(o3, o3, -1.0, 1.0, ALU.add, ALU.add))
                        ch.link(nc.vector.tensor_scalar(o3, o3, float(S2), -1.0, ALU.mult, ALU.add))
                        nc.vector.tensor_scalar(o3, o3, 0.5, None, ALU.mult).then_inc(s1["ix"], 1)

                    def point_scores(u):
                        hs = slice(u % NG * HG, u % NG * HG + HG)
                        dve.wait_ge(s1["sc"], u + 1)
                        dve.wait_ge(s1["hat"], u + 1)
                        s3 = ps[:, 1 + u % NG, 0:HG * S2].rearrange("p (h s) -> p h s", h=HG)
                        nc.vector.tensor_tensor(hsc, hat[:, u % 3, :, :, :], s3.unsqueeze(2).to_broadcast([P, HG, NK, S2]),
                                                ALU.mult).then_inc(s1["used"], 1)
                        dve.wait_ge(s1["used"], u + 1)
                        if u >= NG:
                            dve.wait_ge(s1["w"], u - NG + 1)
                        ch.link(nc.vector.tensor_reduce(psc[:, hs, :], hsc, AX_X, ALU.add))
                        ch.link(nc.vector.tensor_reduce(pmx[:, hs], psc[:, hs, :], AX_X, ALU.max))
                        nc.vector.tensor_tensor(psc[:, hs, :], psc[:, hs, :], pmx[:, hs].unsqueeze(2).to_broadcast([P, HG, NK]),
                                                ALU.subtract).then_inc(s1["shift"], 1)

                    def point_weights(u):
                        hs = slice(u % NG * HG, u % NG * HG + HG)
                        dve.wait_ge(s1["exp"], u + 1)
                        ch.link(nc.vector.tensor_reduce(ssm[:, u // NG % 2, hs], psc[:, hs, :], AX_X, ALU.add))
                        if u:
                            dve.wait_ge(s1["turn"], u)
                        nc.vector.tensor_tensor(hw, hat[:, u % 3, :, :, :],
                                                psc[:, hs, :].unsqueeze(3).to_broadcast([P, HG, NK, S2]), ALU.mult)\
                            .then_inc(s1["w"], 1)

                    def sampled_out(t):
                        ch.link(nc.vector.reciprocal(srs, ssm[:, t % 2, :]))
                        dve.wait_ge(s1["pv"], (t + 1) * NG)
                        if t:
                            dve.wait_ge(s1["ot"], t)
                        nc.vector.tensor_tensor(ox.rearrange("p (h d) -> p h d", h=H),
                                                ps[:, 0, 0:P].rearrange("p (h d) -> p h d", h=H),
                                                srs.unsqueeze(2).to_broadcast([P, H, HD]), ALU.mult).then_inc(s1["osb"], 1)

                    def sampled_attention():
                        keys_values(0)
                        offsets()
                        point_scores(0)
                        for u in range(NT * NG):
                            if u + 1 < NT * NG:
                                point_scores(u + 1)
                            point_weights(u)
                            if u >= NG and u % NG == 0:
                                sampled_out(u // NG - 1)
                        sampled_out(NT - 1)
                        project_rows(s1["y"], NT, bo1)

                    def soft(i, t):
                        n = NT * (i - 1) + t
                        dve.wait_ge(a["s"], n + 1)
                        for j, (h0, h1) in enumerate(HS):
                            s3 = ps[:, 2 + j, 0:(h1 - h0) * S2].rearrange("p (h s) -> p h s", s=S2)
                            ch.link(nc.vector.tensor_reduce(smx[:, h0:h1], s3, AX_X, ALU.max))
                            if j == 0 and n >= 2:
                                dve.wait_ge(a["turn"], 4 * (n - 1))
                            ins = nc.vector.tensor_tensor(sx[:, n % 2, h0:h1, :], s3, smx[:, h0:h1].unsqueeze(2)
                                                          .to_broadcast([P, h1 - h0, S2]), ALU.subtract)
                            if j == 2:
                                ins.then_inc(a["sub"], 1)

                    def attend(i, t):
                        n = NT * (i - 1) + t
                        dve.wait_ge(a["exp"], n + 1)
                        ch.link(nc.vector.tensor_reduce(ssm[:, 0, :], sx[:, n % 2, :, :], AX_X, ALU.add))
                        ch.link(nc.vector.reciprocal(srs, ssm[:, 0, :]))
                        for q in (1, 3):
                            dve.wait_ge(a["turn"], 4 * n + q + 1)
                            nc.vector.tensor_copy(aT[:, 4 * q:4 * q + 4, :], ps[0:S2, 5 + q % 2, :]
                                                  .rearrange("p (h c) -> p h c", h=4)).then_inc(a["aT"], 1)
                        dve.wait_ge(a["o"], n + 1)
                        nc.vector.tensor_tensor(ox.rearrange("p (h d) -> p h d", h=H),
                                                ps[:, 0, 0:P].rearrange("p (h d) -> p h d", h=H),
                                                srs.unsqueeze(2).to_broadcast([P, H, HD]), ALU.mult).then_inc(a["osb"], 1)

                    def attention(i):
                        keys_values(i)
                        soft(i, 0)
                        for t in range(NT):
                            if t + 1 < NT:
                                soft(i, t + 1)
                            attend(i, t)
                        project_rows(a["y"], NT * i, bo3 if i == 2 else None)

                    def product_keys():
                        for t in range(NT):
                            dve.wait_ge(k["sim"], t + 1)
                            s3 = ps[:, t % 2, :].rearrange("p (c n) -> p c n", c=16)
                            bc = lambda v: v.unsqueeze(2).to_broadcast([P, 16, PKN])
                            ch.link(nc.vector.tensor_reduce(kmax, s3, AX_X, ALU.max))
                            ch.link(nc.vector.tensor_tensor(eqk, s3, bc(kmax), ALU.is_ge))
                            ch.link(nc.vector.tensor_tensor(eqk, eqk, iota_k[:, :].unsqueeze(1).to_broadcast([P, 16, PKN]),
                                                            ALU.mult))
                            ch.link(nc.vector.tensor_reduce(kidx, eqk, AX_X, ALU.min))
                            ch.link(nc.vector.tensor_scalar(eid, kidx[:, 0:8], float(PKN), float(PKN * PKN + PKN), ALU.mult,
                                                            ALU.add))
                            ch.link(nc.vector.tensor_tensor(eid, eid, kidx[:, 8:16], ALU.add))
                            nc.vector.tensor_copy(eidi, eid).then_inc(k["idx"], 1)
                            ch.link(nc.vector.tensor_tensor(esc, kmax[:, 0:8], kmax[:, 8:16], ALU.add))
                            ch.link(nc.vector.tensor_scalar(esc, esc, 0.0, None, ALU.max))
                            dve.wait_ge(rows_in, b * (16 * PKH * NT) + 16 * PKH * (t + 1))
                            for h in range(PKH):
                                ins = nc.vector.tensor_tensor_reduce(junk, rows_g[:, h, 0:D], xn[:, t, :], 1.0, 0.0, ALU.mult,
                                                                     ALU.add, dots[:, h:h + 1])
                                if h < PKH - 1:
                                    ch.link(ins)
                                else:
                                    ins.then_inc(k["dot"], 1)
                            dve.wait_ge(k["act"], t + 1)
                            ch.link(nc.vector.tensor_tensor(hv, hv, esc, ALU.mult))
                            for h in range(PKH):
                                ins = nc.vector.scalar_tensor_tensor(x[:, t, :], rows_g[:, h, D:2 * D], hv[:, h:h + 1],
                                                                     x[:, t, :], ALU.mult, ALU.add)
                                if h < PKH - 1:
                                    ch.link(ins)
                                else:
                                    add_x(ins)
                                    dve.wait_ge(x_new, nx[0])

                    dve.wait_ge(i0["y"], 1)
                    y = bnk(1).rearrange("p (t d) -> p t d", t=NT)
                    ch.link(nc.vector.tensor_tensor(x[:, :, :], x[:, :, :], y, ALU.add))
                    add_x(nc.vector.tensor_tensor(x[:, :, :], x[:, :, :], pb0[:, :].unsqueeze(1).to_broadcast([P, NT, D]), ALU.add))

                    if stop_after >= 1:
                        norm(0)
                        gates(0)
                        for u in range(4 * (E + 1)):
                            if u >= 4:
                                dve.wait_ge(f["act"], u + 1)
                                dve.wait_ge(f["gb"], u // 4)
                                nc.vector.tensor_tensor(hb[:, u % 4, :], hb[:, u % 4, :], ps[:, 5 + u // 4 % 2, :], ALU.mult)\
                                    .then_inc(f["hg"], 1)
                        add_ffn(0)
                    if stop_after >= 2:
                        norm(1)
                        sampled_attention()
                    if stop_after >= 3:
                        norm(2)
                        gates(1)
                        for e in range(E):
                            dve.wait_ge(f["gb"], E + e + 1)
                            if e >= 2:
                                dve.wait_ge(f["up"], U0 + 2 * 3 * (e - 1))
                            nc.vector.tensor_tensor(xs[:, e % 2, :], xnT, ps[:, 5 + e % 2, :], ALU.mult).then_inc(f["xs"], 1)
                            for c in range(3):
                                u = 3 * e + c
                                n = CH1[c][1]
                                dve.wait_ge(f["act"], U0 + u + 1)
                                dve.wait_ge(f["up"], U0 + 2 * u + 2)
                                nc.vector.tensor_tensor(hb[0:n, u % 4, :], hb[0:n, u % 4, :], ps[0:n, 2 + u % 2, :], ALU.mult)\
                                    .then_inc(f["hg"], 1)
                        add_ffn(1)
                    if stop_after >= 4:
                        norm(3)
                        attention(1)
                    if stop_after >= 5:
                        norm(4)
                        gates(2)
                        for u in range(4 * E):
                            dve.wait_ge(f["act"], U0 + 3 * E + u + 1)
                            dve.wait_ge(f["gb"], 2 * E + u // 4 + 1)
                            nc.vector.tensor_tensor(hb[:, u % 4, :], hb[:, u % 4, :], ps[:, 5 + u // 4 % 2, :], ALU.mult)\
                                .then_inc(f["hg"], 1)
                        add_ffn(2)
                    if stop_after >= 6:
                        norm(5)
                        attention(2)
                    if stop_after >= 7:
                        norm(6)
                        product_keys()
                    assert nx[0] == NX, nx[0]

                @block.tensor
                def _(pe):
                    def norm(n):
                        norm_tensor(nc, pe, n, xn, ident, bnk(0), ln_xn, ln_turned)
                        pe.wait_ge(ln_xnT, n + 1)

                    def gates(n):
                        for t in range(NT):
                            mm = nc.tensor.matmul(ps[:, 7, t * E:t * E + E], xnT[:, t * P:t * P + P], gw[:, n, :],
                                                  start=True, stop=True)
                        mm.then_inc(g["log"], 1)

                    def gates_turned(n):
                        pe.wait_ge(g["done"], n + 1)
                        for t in range(NT):
                            mm = nc.tensor.transpose(ps[0:E, 6, t * P:t * P + P], gate[:, t, :], ident[:, :])
                        mm.then_inc(g["turn"], 1)

                    def gate_rows(n, e):
                        pe.wait_ge(g["gT"], n + 1)
                        if e >= 2:
                            if n == 1:
                                pe.wait_ge(f["xs"], e - 1)
                            else:
                                pe.wait_ge(f["hg"], (0, 0, 4 * E + 3 * E)[n] + 4 * (e - 1))
                        for t in range(NT):
                            mm = nc.tensor.transpose(ps[:, 5 + e % 2 if n else 5 + (e + 1) % 2, t * P:t * P + P],
                                                     gate[:, t, e:e + 1].to_broadcast([P, P]), ident[:, :])
                        mm.then_inc(f["gb"], 1)

                    def ffn(n, ups, w2, act0, hg0, down0, units, shared):
                        def down(v, last=False):
                            if shared and v < 4:
                                pe.wait_ge(f["act"], act0 + v + 1)
                            else:
                                pe.wait_ge(f["hg"], hg0 + v + 1 - (4 if shared else 0))
                            nc.tensor.matmul(bnk(7), w2(v), hb[0:w2(v).shape[0], v % 4, :], start=v == 0, stop=last)\
                                .then_inc(f["down"], 1)

                        for u in range(units):
                            ups(u)
                            if u >= 2:
                                down(u - 2)
                        down(units - 2)
                        down(units - 1, n == 1)

                    def ffn_end(n, bias):
                        nc.tensor.matmul(bnk(7), bias, gT[:, :], start=False, stop=True).then_inc(f["y"], 1)

                    def ffn_turn(n):
                        pe.wait_ge(f["ysb"], n + 1)
                        for t in range(NT):
                            mm = nc.tensor.transpose(ps[:, 4, t * P:t * P + P], yT[:, t * P:t * P + P], ident[:, :])
                        mm.then_inc(f["yt"], 1)

                    def projections(i):
                        w = wa[i]
                        nc.tensor.matmul(bnk(0), w["q"][:, :], xnT, start=True, stop=True).then_inc(a["proj"], 1)
                        nc.tensor.matmul(ps[:, 1, 0:S2], w["k"][:, :], ctxTb[:, :], start=True, stop=True)
                        nc.tensor.matmul(ps[0:S2, 1, P:2 * P], ctxTb[:, :], w["v"][:, :], start=True, stop=True)\
                            .then_inc(a["proj"], 1)
                        pe.wait_ge(a["q"], i + 1)

                    def sampled_attention():
                        pe.wait_ge(W["misc"], wcount["misc"])
                        projections(0)
                        for t in range(NT):
                            mm = nc.tensor.matmul(ps[:, 6, t * H * NK:(t + 1) * H * NK], qTx[:, t * P:t * P + P], woff[:, :],
                                                  start=True, stop=True)
                        mm.then_inc(a["off"], 1)
                        pe.wait_ge(a["kv"], 2)

                        def scores(u):
                            t, hg = u // NG, u % NG
                            if t:
                                pe.wait_ge(s1["used"], u - NG + 1)
                            nc.tensor.matmul(ps[:, 1 + hg, 0:HG * S2], qTx[:, t * P:t * P + P],
                                             kbd[:, hg * HG:hg * HG + HG, :].rearrange("p h s -> p (h s)"),
                                             start=True, stop=True).then_inc(s1["sc"], 1)

                        def turned(u):
                            pe.wait_ge(s1["w"], u + 1)
                            if u == 0:
                                pe.wait_ge(s1["ix"], 1)
                            if u >= 2:
                                pe.wait_ge(s1["aT"], u - 1)
                            for h_ in range(HG):
                                for p_ in range(NK):
                                    mm = nc.tensor.matmul(ps[0:S2, 5 + u % 2, h_ * P:h_ * P + P], hw[:, h_, p_, :], ident[:, :],
                                                          start=p_ == 0, stop=p_ == NK - 1)
                            mm.then_inc(s1["turn"], 1)

                        def values(u):
                            t, hg = u // NG, u % NG
                            pe.wait_ge(s1["aT"], u + 1)
                            if t and hg == 0:
                                pe.wait_ge(s1["osb"], t)
                            for h_ in range(HG):
                                c = (hg * HG + h_) * HD
                                mm = nc.tensor.matmul(ps[:, 0, c:c + HD], aTs[:, u % 2, h_, :], vx[:, c:c + HD],
                                                      start=True, stop=True)
                            mm.then_inc(s1["pv"], 1)

                        def out_turned(t):
                            pe.wait_ge(s1["osb"], t + 1)
                            nc.tensor.transpose(ps[:, 7, t * P:t * P + P], ox, ident[:, :]).then_inc(s1["ot"], 1)

                        def out_projected(t):
                            pe.wait_ge(s1["otsb"], t + 1)
                            nc.tensor.matmul(ps[:, 7, t * P:t * P + P], oTx, wa[0]["o"][:, :], start=True, stop=True)\
                                .then_inc(s1["y"], 1)

                        for u in range(NG):
                            scores(u)
                        for u in range(NT * NG):
                            t, hg = u // NG, u % NG
                            turned(u)
                            if t + 1 < NT:
                                scores(u + NG)
                            if t and hg == 1:
                                out_turned(t - 1)
                            if t and hg == 2:
                                out_projected(t - 1)
                            if u:
                                values(u - 1)
                        values(NT * NG - 1)
                        out_turned(NT - 1)
                        out_projected(NT - 1)

                    def attention(i):
                        w = wa[i]
                        projections(i)
                        pe.wait_ge(a["kv"], 2 * i + 2)

                        def scores(t):
                            n = NT * (i - 1) + t
                            if t >= 1:
                                pe.wait_ge(a["sub"], n)
                            for j, (h0, h1) in enumerate(HS):
                                mm = nc.tensor.matmul(ps[:, 2 + j, 0:(h1 - h0) * S2], qTx[:, t * P:t * P + P],
                                                      kbd[:, h0:h1, :].rearrange("p h s -> p (h s)"), start=True, stop=True)
                            mm.then_inc(a["s"], 1)

                        def weights_turned(t):
                            n = NT * (i - 1) + t
                            pe.wait_ge(a["exp"], n + 1)
                            for q in range(4):
                                if 4 * n + q >= 2:
                                    if q % 2 == 0:
                                        pe.wait_ge(a["aT_even"], (4 * n + q) // 2)
                                    else:
                                        pe.wait_ge(a["aT"], (4 * n + q - 1) // 2)
                                for hh in range(4):
                                    mm = nc.tensor.transpose(ps[0:S2, 5 + q % 2, hh * P:hh * P + P], sx[:, n % 2, 4 * q + hh, :],
                                                             ident[:, :])
                                mm.then_inc(a["turn"], 1)

                        def values(t):
                            n = NT * (i - 1) + t
                            pe.wait_ge(a["aT_even"], 2 * n + 2)
                            pe.wait_ge(a["aT"], 2 * n + 2)
                            for hh in range(H):
                                mm = nc.tensor.matmul(ps[:, 0, hh * HD:hh * HD + HD], aT[:, hh, :], vx[:, hh * HD:hh * HD + HD],
                                                      start=True, stop=True)
                            mm.then_inc(a["o"], 1)

                        def projected(t):
                            n = NT * (i - 1) + t
                            pe.wait_ge(a["osb"], n + 1)
                            nc.tensor.transpose(ps[:, 1, 0:P], ox, ident[:, :]).then_inc(a["ot"], 1)
                            pe.wait_ge(a["otsb"], n + 1)
                            nc.tensor.matmul(ps[:, 7, t * P:t * P + P], oTx, w["o"][:, :], start=True, stop=True)\
                                .then_inc(a["y"], 1)

                        scores(0)
                        for t in range(NT):
                            if t + 1 < NT:
                                scores(t + 1)
                            weights_turned(t)
                            if t:
                                projected(t - 1)
                            values(t)
                        projected(NT - 1)

                    for t in range(NT):
                        mm = nc.tensor.matmul(ps[:, 1, t * P:t * P + P], oT[:, t * P:t * P + P], wp0[:, :], start=True, stop=True)
                    mm.then_inc(i0["y"], 1)

                    def ups0(u):
                        e, c = u // 4, u % 4
                        if c == 2 and e < E:
                            if e == 0:
                                gates_turned(0)
                            gate_rows(0, e)
                        if u >= 3:
                            pe.wait_ge(f["act"], u - 2)
                        nc.tensor.matmul(bnk(1 + u % 3), w1_0[:, e, c * P:c * P + P], xnT, start=True, stop=True)\
                            .then_inc(f["up"], 1)

                    def ups1(u):
                        e, c = u // 3, u % 3
                        lo, n = CH1[c]
                        if u == 0:
                            gate_rows(1, 0)
                        if c == 1 and e < E - 1:
                            gate_rows(1, e + 1)
                        if c == 0:
                            pe.wait_ge(f["xs"], e + 1)
                        if u >= 2:
                            pe.wait_ge(f["act"], U0 + u - 1)
                            pe.wait_ge(f["hg"], 4 * E + u - 1)
                        nc.tensor.matmul(ps[0:n, u % 2, :], w1_1[:, e, lo:lo + n], xs[:, e % 2, :], start=True, stop=True)\
                            .then_inc(f["up"], 1)
                        nc.tensor.matmul(ps[0:n, 2 + u % 2, :], w3_1[:, e, lo:lo + n], xs[:, e % 2, :], start=True, stop=True)\
                            .then_inc(f["up"], 1)

                    def ups2(u):
                        e, c = u // 4, u % 4
                        if u == 0:
                            gate_rows(2, 0)
                        if c == 2 and e < E - 1:
                            gate_rows(2, e + 1)
                        if u >= 3:
                            pe.wait_ge(f["act"], U0 + 3 * E + u - 2)
                        nc.tensor.matmul(bnk(1 + u % 3), w1_2[:, e, c * P:c * P + P], xnT, start=True, stop=True)\
                            .then_inc(f["up"], 1)

                    if stop_after >= 1:
                        norm(0)
                        gates(0)
                        ffn(0, ups0, lambda v: w2_0[:, v // 4, v % 4, :], 0, 0, 0, 4 * (E + 1), True)
                        ffn_end(0, b2_0[:, :])
                        ffn_turn(0)
                    if stop_after >= 2:
                        norm(1)
                        sampled_attention()
                    if stop_after >= 3:
                        norm(2)
                        gates(1)
                        gates_turned(1)
                        ffn(1, ups1, lambda v: w2_1[0:CH1[v % 3][1], v // 3, v % 3, :], U0, 4 * E, 0, 3 * E, False)
                        ffn_turn(1)
                    if stop_after >= 4:
                        norm(3)
                        attention(1)
                    if stop_after >= 5:
                        norm(4)
                        gates(2)
                        gates_turned(2)
                        ffn(2, ups2, lambda v: w2_2[:, v // 4, v % 4, :], U0 + 3 * E, 4 * E + 3 * E, 0, 4 * E, False)
                        ffn_end(2, b2_2[:, :])
                        ffn_turn(2)
                    if stop_after >= 6:
                        norm(5)
                        attention(2)
                    if stop_after >= 7:
                        norm(6)
                        for t in range(NT):
                            if t >= 2:
                                pe.wait_ge(k["idx"], t - 1)
                            nc.tensor.matmul(bnk(t % 2), xnT[:, t * P:t * P + P], wcomb[:, :], start=True, stop=True)\
                                .then_inc(k["sim"], 1)

                @block.scalar
                def _(act):
                    norm = lambda n: norm_scalar(nc, act, n, xnT, bnk(0), ln_turned, ln_xnT)

                    def gates(n):
                        act.wait_ge(g["max"], n + 1)
                        nc.scalar.activation(glog[:, :, :], glog[:, :, :], ACT.Exp).then_inc(g["exp"], 1)

                    def ffn_out(n, bias):
                        if n == 1:
                            act.wait_ge(f["down"], U0 + 3 * E)
                        else:
                            act.wait_ge(f["y"], 1 + n // 2)
                        if bias is None:
                            nc.scalar.copy(yT, bnk(7)).then_inc(f["ysb"], 1)
                        else:
                            nc.scalar.activation(yT, bnk(7), ACT.Identity, bias=bias).then_inc(f["ysb"], 1)

                    def sampled_attention():
                        act.wait_ge(a["proj"], 1)
                        nc.scalar.activation(qTx, bnk(0), ACT.Identity, bias=bq1[:, :]).then_inc(a["q"], 1)

                        def interpolation(u):
                            act.wait_ge(s1["pos"], u + 1)
                            v = hat[:, u % 3, :, :, :]
                            nc.scalar.activation(v, v, ACT.Abs).then_inc(s1["abs"], 1)
                            act.wait_ge(s1["abs"], u + 1)
                            nc.scalar.activation(v, v, ACT.Relu, bias=1.0, scale=-1.0).then_inc(s1["hat"], 1)

                        def weights_in(u):
                            act.wait_ge(s1["turn"], u + 1)
                            if u >= 2:
                                act.wait_ge(s1["pv"], u - 1)
                            nc.scalar.copy(aTs[:, u % 2, :, :], ps[0:S2, 5 + u % 2, :].rearrange("p (h c) -> p h c", h=HG))\
                                .then_inc(s1["aT"], 1)

                        def out_in(t):
                            act.wait_ge(s1["ot"], t + 1)
                            if t:
                                act.wait_ge(s1["y"], t)
                            nc.scalar.copy(oTx, ps[:, 7, t * P:t * P + P]).then_inc(s1["otsb"], 1)

                        interpolation(0)
                        interpolation(1)
                        for u in range(NT * NG):
                            hs = slice(u % NG * HG, u % NG * HG + HG)
                            act.wait_ge(s1["shift"], u + 1)
                            nc.scalar.activation(psc[:, hs, :], psc[:, hs, :], ACT.Exp).then_inc(s1["exp"], 1)
                            if u + 2 < NT * NG:
                                interpolation(u + 2)
                            if u:
                                weights_in(u - 1)
                            if u >= NG and u % NG == 2:
                                out_in(u // NG - 1)
                        weights_in(NT * NG - 1)
                        out_in(NT - 1)

                    def attention(i):
                        act.wait_ge(a["proj"], 2 * i + 1)
                        nc.scalar.copy(qTx, bnk(0)).then_inc(a["q"], 1)

                        def exps(t):
                            n = NT * (i - 1) + t
                            act.wait_ge(a["sub"], n + 1)
                            nc.scalar.activation(sx[:, n % 2, :, :], sx[:, n % 2, :, :], ACT.Exp, scale=SCALE)\
                                .then_inc(a["exp"], 1)

                        def out_in(t):
                            act.wait_ge(a["ot"], NT * (i - 1) + t + 1)
                            nc.scalar.copy(oTx, ps[:, 1, 0:P]).then_inc(a["otsb"], 1)

                        exps(0)
                        for t in range(NT):
                            n = NT * (i - 1) + t
                            if t + 1 < NT:
                                exps(t + 1)
                            if n:
                                act.wait_ge(a["o"], n)
                            for q in (0, 2):
                                act.wait_ge(a["turn"], 4 * n + q + 1)
                                nc.scalar.copy(aT[:, 4 * q:4 * q + 4, :], ps[0:S2, 5 + q % 2, :]
                                               .rearrange("p (h c) -> p h c", h=4)).then_inc(a["aT_even"], 1)
                            if t:
                                out_in(t - 1)
                        out_in(NT - 1)

                    if stop_after >= 1:
                        norm(0)
                        gates(0)
                        act.wait_ge(W["ffn0"], wcount["ffn0"])
                        for u in range(4 * (E + 1)):
                            act.wait_ge(f["up"], u + 1)
                            if u >= 4:
                                act.wait_ge(f["down"], u - 3)
                            nc.scalar.activation(hb[:, u % 4, :], bnk(1 + u % 3), ACT.Gelu_apprx_tanh,
                                                 bias=b1_0[:, u // 4, u % 4:u % 4 + 1]).then_inc(f["act"], 1)
                        ffn_out(0, bs0[:, :])
                    if stop_after >= 2:
                        norm(1)
                        sampled_attention()
                    if stop_after >= 3:
                        norm(2)
                        gates(1)
                        for u in range(3 * E):
                            n = CH1[u % 3][1]
                            act.wait_ge(f["up"], U0 + 2 * u + 1)
                            if u >= 4:
                                act.wait_ge(f["down"], U0 + u - 3)
                            nc.scalar.activation(hb[0:n, u % 4, :], ps[0:n, u % 2, :], ACT.Silu).then_inc(f["act"], 1)
                        ffn_out(1, None)
                    if stop_after >= 4:
                        norm(3)
                        attention(1)
                    if stop_after >= 5:
                        norm(4)
                        gates(2)
                        for u in range(4 * E):
                            act.wait_ge(f["up"], U0 + 6 * E + u + 1)
                            if u >= 4:
                                act.wait_ge(f["down"], U0 + 3 * E + u - 3)
                            nc.scalar.activation(hb[:, u % 4, :], bnk(1 + u % 3), ACT.Relu,
                                                 bias=b1_2[:, u // 4, u % 4:u % 4 + 1]).then_inc(f["act"], 1)
                        ffn_out(2, None)
                    if stop_after >= 6:
                        norm(5)
                        attention(2)
                    if stop_after >= 7:
                        norm(6)
                        for t in range(NT):
                            act.wait_ge(k["dot"], t + 1)
                            nc.scalar.activation(hv, dots, ACT.Gelu).then_inc(k["act"], 1)
            clear_sems(loop_sems)


def norm_vector(nc, dve, n, x, xn, stats, mv, rstd, ln_stats, ln_mean, ln_rstd, ln_xn):
    for t in range(NT):
        nc.vector.bn_stats(stats[:, t, :], x[:, t, :]).then_inc(ln_stats, 1)
    dve.wait_ge(ln_stats, NT * (n + 1))
    for t in range(NT):
        nc.vector.bn_aggr(mv[:, t, :], stats[:, t, :]).then_inc(ln_mean, 1)
    dve.wait_ge(ln_mean, NT * (n + 1))
    dve.wait_ge(ln_rstd, n + 1)
    for t in range(NT):
        nc.vector.tensor_scalar(xn[:, t, :], x[:, t, :], mv[:, t, 0:1], rstd[:, t:t + 1],
                                ALU.subtract, ALU.mult).then_inc(ln_xn, 1)


def norm_pool(nc, pool, ch, n, ln_mean, ln_rstd, mv, rstd, neghalf):
    pool.wait_ge(ln_mean, NT * (n + 1))
    ch.link(nc.gpsimd.tensor_scalar(rstd[:, :], mv[:, :, 1], EPS, None, ALU.add))
    nc.gpsimd.tensor_tensor(rstd[:, :], rstd[:, :], neghalf[:, 0:NT], ALU.pow).then_inc(ln_rstd, 1)


def norm_tensor(nc, pe, n, xn, ident, bank, ln_xn, ln_turned):
    for t in range(NT):
        pe.wait_ge(ln_xn, NT * n + t + 1)
        mm = nc.tensor.transpose(bank[:, t * P:t * P + P], xn[:, t, :], ident[:, :])
    mm.then_inc(ln_turned, 1)


def norm_scalar(nc, act, n, xnT, bank, ln_turned, ln_xnT):
    act.wait_ge(ln_turned, n + 1)
    nc.scalar.copy(xnT, bank).then_inc(ln_xnT, 1)


def kernel(**inputs):
    import numpy as _np
    import concourse.bacc as _bacc
    from concourse import mybir as _mybir
    from concourse.bass_utils import run_bass_kernel_spmd as _run

    a = {k: _np.asarray(v) for k, v in inputs.items()}
    c = _np.ascontiguousarray

    def cols(v):
        return v.reshape(v.shape[0], -1, P).transpose(2, 0, 1)

    L0, F0, L1, F1, L2, F2, L3, F3 = ("L0_xattn_", "L0_ffn_", "L1_xattn_", "L1_ffn_", "L2_xattn_", "L2_ffn_",
                                      "L3_xattn_", "L3_ffn_")
    arrays = {
        "x": a["x"], "ctx_1024": a["ctx_1024"], "mask": a["mask_SxS_bc0"], "mask2": a["mask_BxS2_if0"],
        "Wq0": a[L0 + "Wq"], "Wk0": a[L0 + "Wk"], "Wv0": a[L0 + "Wv"], "Wp0": a[L0 + "proj_W"], "bp0": a[L0 + "proj_b"],
        "hist_W": a[L0 + "hist_W"], "hist_b": a[L0 + "hist_b"], "hist_ln_g": a[L0 + "hist_ln_g"],
        "hist_ln_b": a[L0 + "hist_ln_b"], "ctx_W1": a[L0 + "ctx_W1"], "ctx_b1": a[L0 + "ctx_b1"],
        "ctx_W2": a[L0 + "ctx_W2"].reshape(-1), "ctx_b2": a[L0 + "ctx_b2"], "kg_W1": a[L0 + "kg_W1"],
        "kg_b1": a[L0 + "kg_b1"], "kg_ln_g": a[L0 + "kg_ln_g"], "kg_ln_b": a[L0 + "kg_ln_b"],
        "kg_W2": a[L0 + "kg_W2"], "kg_b2": a[L0 + "kg_b2"],
        "Wfc_s": a[F0 + "Wfc_s"], "Wproj_s": a[F0 + "Wproj_s"], "bproj_s": a[F0 + "bproj_s"],
        "Wr0": a[F0 + "Wr"], "Wfc": a[F0 + "Wfc"], "bfc": cols(_np.concatenate([a[F0 + "bfc_s"][None], a[F0 + "bfc"]])), "Wproj": a[F0 + "Wproj"], "bproj": a[F0 + "bproj"],
        "wq1": a[L1 + "Wq"].T, "wk1": a[L1 + "Wk"].T, "wv1": a[L1 + "Wv"].T, "wo1": a[L1 + "Wo"].T,
        "bq1": a[L1 + "bq"], "bk1": a[L1 + "bk"], "bv1": a[L1 + "bv"], "bo1": a[L1 + "bo"],
        "Woff": a[L1 + "Woff"].T, "boff": a[L1 + "boff"],
        "Wr1": a[F1 + "gate_w"].T, "eb1": a[F1 + "expert_bias"], "w1": a[F1 + "w1"], "w2": a[F1 + "w2"], "w3": a[F1 + "w3"],
        "wq2": a[L2 + "wq"].T, "wk2": a[L2 + "wk"].T, "wv2": a[L2 + "wv"].T, "wo2": a[L2 + "wo"].T,
        "W1": a[F2 + "W1"], "b1": cols(a[F2 + "b1"]), "W2": a[F2 + "W2"], "b2": a[F2 + "b2"], "Wr2": a[F2 + "Wr"], "br2": a[F2 + "br"],
        "wq3": a[L3 + "W_qkv"][:, 0:D], "wk3": a[L3 + "W_qkv"][:, D:2 * D], "wv3": a[L3 + "W_qkv"][:, 2 * D:],
        "wo3": a[L3 + "W_proj"], "bo3": a[L3 + "b_proj"],
        "w_qT": a[F3 + "w_q"].T,
        "keysT": a[F3 + "keys"].transpose(0, 2, 3, 1),
        "w_ud": _np.concatenate([a[F3 + "w_down"], a[F3 + "w_up"]], axis=1),
    }
    nc = _bacc.Bacc("TRN2", target_bir_lowering=False, num_devices=1)
    feed, A = {}, {}
    for name, v in arrays.items():
        v = c(v)
        feed[f"in_{name}"] = v
        A[name] = nc.dram_tensor(f"in_{name}", v.shape, _mybir.dt.from_np(v.dtype), kind="ExternalInput").ap()
    out = nc.dram_tensor("out", (B, T, D), _mybir.dt.float32, kind="ExternalOutput").ap()
    build(nc, A, out, STOP)
    return _run(nc, [feed], core_ids=[0]).results[0]["out"]
```
